# Optimizing a Trainium2 kernel written in Bass

```python
import numpy as np
import jax
import jax.numpy as jnp

def _softmax(x, axis=-1):
    return jax.nn.softmax(x, axis=axis)

def _gelu(x):
    return jax.nn.gelu(x, approximate=True)

def _silu(x):
    return jax.nn.silu(x)

def _sigmoid(x):
    return jax.nn.sigmoid(x)

def _layernorm(x, axis=-1, eps=1e-05):
    m = jnp.mean(x, axis=axis, keepdims=True)
    v = jnp.var(x, axis=axis, keepdims=True)
    return (x - m) / jnp.sqrt(v + eps)

def _scatter_add(tgt, idx, src, axis=0):
    return tgt.at[idx].add(src)

def _segment_sum(src, seg, n):
    return jax.ops.segment_sum(src, seg, n)
kernel_name = 'mk_decoder_preln_d2_seqx_r8_e20e03'

def setup_inputs(seed: int=0):
    np.random.seed(seed)
    _w = jnp.asarray

    def _rec_inputs():
        import jax
        import jax.numpy as jnp
        _rk = jax.random.key(seed)
        x = -0.0002928 + 1 * jax.random.normal(jax.random.fold_in(_rk, 1), (64, 128, 128), jnp.float32)
        _lenS = 128 - jax.random.randint(jax.random.fold_in(_rk, 7), (64,), 0, max(1, 128 // 4) + 1, jnp.int32)
        _lenS2 = 120 - jax.random.randint(jax.random.fold_in(_rk, 8), (64,), 0, max(1, 120 // 4) + 1, jnp.int32)
        _ctx_1024P = jax.random.normal(jax.random.fold_in(_rk, 11), (64, 16, 128), jnp.float32)
        _ctx_1024c = jax.random.dirichlet(jax.random.fold_in(_rk, 511), 0.3 * jnp.ones((16,), jnp.float32), (64, 120))
        _ctx_1024t = jnp.einsum('bsk,bkd->bsd', _ctx_1024c, _ctx_1024P)
        _ctx_1024t = _ctx_1024t * jax.lax.rsqrt(jnp.mean(jnp.square(_ctx_1024t)) + 1e-12) * 0.953939
        ctx_1024 = -1.39393e-06 + 0.999914 * (_ctx_1024t + 0.3 * jax.random.normal(jax.random.fold_in(_rk, 611), (64, 120, 128), jnp.float32))
        fside_BxS2_0 = jax.random.uniform(jax.random.fold_in(_rk, 12), (64, 120), jnp.float32, 0.0, 9)
        return (x, ctx_1024, fside_BxS2_0)
    x, ctx_1024, fside_BxS2_0 = _rec_inputs()

    def _L0_attn_setup():
        import jax, jax.numpy as jnp
        import numpy as np
        NUM_HEADS = 16
        EPS = 1e-06
        CHUNK = 128
        key = jax.random.key(seed)
        ks = jax.random.split(key, 6)
        B, T, E = (4, 256, 128)
        s = 0.02
        x = jax.random.normal(ks[0], (B, T, E), jnp.float32)
        Wq = jax.random.normal(ks[1], (E, E), jnp.float32) * s
        Wk = jax.random.normal(ks[2], (E, E), jnp.float32) * s
        Wv = jax.random.normal(ks[3], (E, E), jnp.float32) * s
        Wp = jax.random.normal(ks[4], (E, E), jnp.float32) * s
        bp = jnp.zeros((E,), jnp.float32)
        return {'x': x, 'Wq': Wq, 'Wk': Wk, 'Wv': Wv, 'Wp': Wp, 'bp': bp}
    _L0_attn_all = _L0_attn_setup()
    _L0_attn_in = {k: v for k, v in _L0_attn_all.items() if k in ('Wq', 'Wk', 'Wv', 'Wp', 'bp')}
    del _L0_attn_all

    def _L0_xattn_setup():
        import jax, jax.numpy as jnp
        import numpy as np
        EMBED = 128
        HEADS = 16
        HEAD_SIZE = EMBED // HEADS
        key = jax.random.key(seed)
        ks = jax.random.split(key, 11)
        B, S, E = (2, 256, EMBED)
        scale = 1.0 / np.sqrt(E)
        return {'q': jax.random.normal(ks[0], (B, S, E), jnp.float32), 'k': jax.random.normal(ks[1], (B, S, E), jnp.float32), 'v': jax.random.normal(ks[2], (B, S, E), jnp.float32), 'Wq': jax.random.normal(ks[3], (E, E), jnp.float32) * scale, 'bq': jnp.zeros((E,), jnp.float32), 'Wk': jax.random.normal(ks[4], (E, E), jnp.float32) * scale, 'bk': jnp.zeros((E,), jnp.float32), 'Wv': jax.random.normal(ks[5], (E, E), jnp.float32) * scale, 'bv': jnp.zeros((E,), jnp.float32), 'Wo': jax.random.normal(ks[6], (E, E), jnp.float32) * scale, 'bo': jnp.zeros((E,), jnp.float32)}
    _L0_xattn_all = _L0_xattn_setup()
    _L0_xattn_in = {k: v for k, v in _L0_xattn_all.items() if k in ('Wq', 'bq', 'Wk', 'bk', 'Wv', 'bv', 'Wo', 'bo')}
    del _L0_xattn_all

    def _L0_ffn_setup():
        import jax, jax.numpy as jnp
        import numpy as np
        BS, L, D = (4, 256, 128)
        H, E, K = (8, 16, 2)
        HD = D // H
        I = 512 // H
        key = jax.random.key(seed)
        ks = jax.random.split(key, 10)
        s = lambda k, shp, fan: jax.random.normal(k, shp, jnp.float32) / np.sqrt(fan)
        return {'x': jax.random.normal(ks[0], (BS, L, D), jnp.float32), 'Wm': s(ks[1], (D, D), D), 'bm': jnp.zeros((D,), jnp.float32), 'expert_emb': jax.random.normal(ks[2], (HD, E), jnp.float32), 'W1': s(ks[3], (E, HD, I), HD), 'b1': jnp.zeros((E, I), jnp.float32), 'W2': s(ks[4], (E, I, HD), I), 'b2': jnp.zeros((E, HD), jnp.float32), 'Wo': s(ks[5], (D, D), D), 'bo': jnp.zeros((D,), jnp.float32)}
    _L0_ffn_all = _L0_ffn_setup()
    _L0_ffn_in = {k: v for k, v in _L0_ffn_all.items() if k in ('Wm', 'bm', 'expert_emb', 'W1', 'b1', 'W2', 'b2', 'Wo', 'bo')}
    del _L0_ffn_all

    def _L1_attn_setup():
        import jax, jax.numpy as jnp
        import numpy as np
        MODEL_DIM = 128
        NUM_HEADS = 16
        D_K = MODEL_DIM // NUM_HEADS
        MAX_SEQ_LEN = 512

        def _xavier(key, shape):
            fan_in, fan_out = (shape[1], shape[0])
            limit = np.sqrt(6.0 / (fan_in + fan_out)).astype(np.float32)
            return jax.random.uniform(key, shape, jnp.float32, -limit, limit)
        key = jax.random.key(seed)
        ks = jax.random.split(key, 6)
        x = jax.random.normal(ks[0], (2, 256, MODEL_DIM), jnp.float32)
        wq = _xavier(ks[1], (MODEL_DIM, MODEL_DIM))
        wk = _xavier(ks[2], (MODEL_DIM, MODEL_DIM))
        wv = _xavier(ks[3], (MODEL_DIM, MODEL_DIM))
        wo = _xavier(ks[4], (MODEL_DIM, MODEL_DIM))
        bq = jnp.zeros((MODEL_DIM,), jnp.float32)
        bk = jnp.zeros((MODEL_DIM,), jnp.float32)
        bv = jnp.zeros((MODEL_DIM,), jnp.float32)
        bo = jnp.zeros((MODEL_DIM,), jnp.float32)
        half = D_K // 2
        theta = jnp.power(10000.0, jnp.arange(half, dtype=jnp.float32) * (-2.0 / D_K))
        angles = jnp.arange(MAX_SEQ_LEN, dtype=jnp.float32)[:, None] * theta[None, :]
        rot_cos = jnp.cos(angles)
        rot_sin = jnp.sin(angles)
        return {'x': x, 'wq': wq, 'bq': bq, 'wk': wk, 'bk': bk, 'wv': wv, 'bv': bv, 'wo': wo, 'bo': bo, 'rot_cos': rot_cos, 'rot_sin': rot_sin}
    _L1_attn_all = _L1_attn_setup()
    _L1_attn_in = {k: v for k, v in _L1_attn_all.items() if k in ('wq', 'bq', 'wk', 'bk', 'wv', 'bv', 'wo', 'bo', 'rot_cos', 'rot_sin')}
    del _L1_attn_all

    def _L1_xattn_setup():
        import jax, jax.numpy as jnp
        import numpy as np
        B, N, E, H = (2, 256, 128, 16)
        HD = E // H
        key = jax.random.key(seed)
        ks = jax.random.split(key, 8)
        query = jax.random.normal(ks[0], (B, N, E), dtype=jnp.float32)
        k_in = jax.random.normal(ks[1], (B, N, E), dtype=jnp.float32)
        v_in = jax.random.normal(ks[2], (B, N, E), dtype=jnp.float32)
        key_abundance = jax.random.randint(ks[3], (B, N), 1, 10).astype(jnp.float32)
        in_proj_weight = jax.random.normal(ks[4], (3 * E, HD * H), dtype=jnp.float32) * (1.0 / np.sqrt(E))
        in_proj_bias = jax.random.normal(ks[5], (3 * HD * H,), dtype=jnp.float32) * 0.02
        out_proj_weight = jax.random.normal(ks[6], (E, HD * H), dtype=jnp.float32) * (1.0 / np.sqrt(E))
        out_proj_bias = jax.random.normal(ks[7], (E,), dtype=jnp.float32) * 0.02
        return {'query': query, 'key': k_in, 'value': v_in, 'key_abundance': key_abundance, 'in_proj_weight': in_proj_weight, 'in_proj_bias': in_proj_bias, 'out_proj_weight': out_proj_weight, 'out_proj_bias': out_proj_bias, 'num_heads': H}
    _L1_xattn_all = _L1_xattn_setup()
    _L1_xattn_in = {k: v for k, v in _L1_xattn_all.items() if k in ('in_proj_weight', 'in_proj_bias', 'out_proj_weight', 'out_proj_bias')}
    del _L1_xattn_all

    def _L1_ffn_setup():
        import jax, jax.numpy as jnp
        import numpy as np
        DIM = 128
        HIDDEN = 256
        N_EXPERTS = 8
        TOP_K = 2
        EPS = 1e-06

        def rms_norm(x, scale, eps=EPS):
            ms = jnp.mean(jnp.square(x.astype(jnp.float32)), axis=-1, keepdims=True)
            s = scale.astype(jnp.float32) * jax.lax.rsqrt(ms + eps)
            return x * s.astype(x.dtype)

        def moe_linear(xf, ids, W):
            E = W.shape[0]
            out = jnp.zeros((xf.shape[0], W.shape[1]), dtype=xf.dtype)
            for e in range(E):
                out = out + jnp.where((ids == e)[:, None], xf @ W[e].T, 0.0)
            return out
        key = jax.random.key(seed)
        k1, k2, k3, k4 = jax.random.split(key, 4)
        x = jax.random.normal(k1, (4, 512, DIM), dtype=jnp.float32)
        norm_scale = jnp.ones((DIM,), dtype=jnp.float32)
        w_router = jax.random.normal(k2, (N_EXPERTS, DIM), dtype=jnp.float32) / np.sqrt(DIM)
        lim_up = np.sqrt(6.0 / (DIM + 2 * HIDDEN))
        w_up = jax.random.uniform(k3, (N_EXPERTS, 2 * HIDDEN, DIM), dtype=jnp.float32, minval=-lim_up, maxval=lim_up)
        lim_dn = np.sqrt(6.0 / (HIDDEN + DIM))
        w_down = jax.random.uniform(k4, (N_EXPERTS, DIM, HIDDEN), dtype=jnp.float32, minval=-lim_dn, maxval=lim_dn)
        return {'x': x, 'norm_scale': norm_scale, 'w_router': w_router, 'w_up': w_up, 'w_down': w_down}
    _L1_ffn_all = _L1_ffn_setup()
    _L1_ffn_in = {k: v for k, v in _L1_ffn_all.items() if k in ('norm_scale', 'w_router', 'w_up', 'w_down')}
    del _L1_ffn_all
    return {'x': x, 'ctx_1024': ctx_1024, 'fside_BxS2_0': fside_BxS2_0, 'L0_attn_Wq': _L0_attn_in['Wq'], 'L0_attn_Wk': _L0_attn_in['Wk'], 'L0_attn_Wv': _L0_attn_in['Wv'], 'L0_attn_Wp': _L0_attn_in['Wp'], 'L0_attn_bp': _L0_attn_in['bp'], 'L0_xattn_Wq': _L0_xattn_in['Wq'], 'L0_xattn_bq': _L0_xattn_in['bq'], 'L0_xattn_Wk': _L0_xattn_in['Wk'], 'L0_xattn_bk': _L0_xattn_in['bk'], 'L0_xattn_Wv': _L0_xattn_in['Wv'], 'L0_xattn_bv': _L0_xattn_in['bv'], 'L0_xattn_Wo': _L0_xattn_in['Wo'], 'L0_xattn_bo': _L0_xattn_in['bo'], 'L0_ffn_Wm': _L0_ffn_in['Wm'], 'L0_ffn_bm': _L0_ffn_in['bm'], 'L0_ffn_expert_emb': _L0_ffn_in['expert_emb'], 'L0_ffn_W1': _L0_ffn_in['W1'], 'L0_ffn_b1': _L0_ffn_in['b1'], 'L0_ffn_W2': _L0_ffn_in['W2'], 'L0_ffn_b2': _L0_ffn_in['b2'], 'L0_ffn_Wo': _L0_ffn_in['Wo'], 'L0_ffn_bo': _L0_ffn_in['bo'], 'L1_attn_wq': _L1_attn_in['wq'], 'L1_attn_bq': _L1_attn_in['bq'], 'L1_attn_wk': _L1_attn_in['wk'], 'L1_attn_bk': _L1_attn_in['bk'], 'L1_attn_wv': _L1_attn_in['wv'], 'L1_attn_bv': _L1_attn_in['bv'], 'L1_attn_wo': _L1_attn_in['wo'], 'L1_attn_bo': _L1_attn_in['bo'], 'L1_attn_rot_cos': _L1_attn_in['rot_cos'], 'L1_attn_rot_sin': _L1_attn_in['rot_sin'], 'L1_xattn_in_proj_weight': _L1_xattn_in['in_proj_weight'], 'L1_xattn_in_proj_bias': _L1_xattn_in['in_proj_bias'], 'L1_xattn_out_proj_weight': _L1_xattn_in['out_proj_weight'], 'L1_xattn_out_proj_bias': _L1_xattn_in['out_proj_bias'], 'L1_ffn_norm_scale': _L1_ffn_in['norm_scale'], 'L1_ffn_w_router': _L1_ffn_in['w_router'], 'L1_ffn_w_up': _L1_ffn_in['w_up'], 'L1_ffn_w_down': _L1_ffn_in['w_down']}

def reference(x, ctx_1024, fside_BxS2_0, L0_attn_Wq, L0_attn_Wk, L0_attn_Wv, L0_attn_Wp, L0_attn_bp, L0_xattn_Wq, L0_xattn_bq, L0_xattn_Wk, L0_xattn_bk, L0_xattn_Wv, L0_xattn_bv, L0_xattn_Wo, L0_xattn_bo, L0_ffn_Wm, L0_ffn_bm, L0_ffn_expert_emb, L0_ffn_W1, L0_ffn_b1, L0_ffn_W2, L0_ffn_b2, L0_ffn_Wo, L0_ffn_bo, L1_attn_wq, L1_attn_bq, L1_attn_wk, L1_attn_bk, L1_attn_wv, L1_attn_bv, L1_attn_wo, L1_attn_bo, L1_attn_rot_cos, L1_attn_rot_sin, L1_xattn_in_proj_weight, L1_xattn_in_proj_bias, L1_xattn_out_proj_weight, L1_xattn_out_proj_bias, L1_ffn_norm_scale, L1_ffn_w_router, L1_ffn_w_up, L1_ffn_w_down):
    import jax
    import jax.numpy as jnp

    def _L0_attn_ref(x, Wq, Wk, Wv, Wp, bp):
        import jax, jax.numpy as jnp
        import numpy as np
        NUM_HEADS = 16
        EPS = 1e-06
        CHUNK = 128
        B, T, E = x.shape
        H = NUM_HEADS
        D = E // H
        N = T // CHUNK
        q = x @ Wq.T
        k = x @ Wk.T
        v = x @ Wv.T

        def split_heads(t):
            return t.reshape(B, T, H, D).transpose(0, 2, 1, 3).reshape(B, H, N, CHUNK, D)
        phi_q = jax.nn.elu(split_heads(q)) + 1.0
        phi_k = jax.nn.elu(split_heads(k)) + 1.0
        vh = split_heads(v)
        kv = jnp.einsum('bhncd,bhnce->bhnde', phi_k, vh)
        zk = phi_k.sum(axis=3)
        S_prev = jnp.concatenate([jnp.zeros_like(kv[:, :, :1]), jnp.cumsum(kv, axis=2)[:, :, :-1]], axis=2)
        Z_prev = jnp.concatenate([jnp.zeros_like(zk[:, :, :1]), jnp.cumsum(zk, axis=2)[:, :, :-1]], axis=2)
        A = jnp.einsum('bhncd,bhnsd->bhncs', phi_q, phi_k)
        mask = jnp.tril(jnp.ones((CHUNK, CHUNK), bool))
        A = jnp.where(mask, A, 0.0)
        num = jnp.einsum('bhncs,bhnse->bhnce', A, vh) + jnp.einsum('bhncd,bhnde->bhnce', phi_q, S_prev)
        den = A.sum(-1) + jnp.einsum('bhncd,bhnd->bhnc', phi_q, Z_prev) + EPS
        y = num / den[..., None]
        y = y.reshape(B, H, T, D).transpose(0, 2, 1, 3).reshape(B, T, E)
        return y @ Wp.T + bp

    def _L0_xattn_ref(q, k, v, Wq, bq, Wk, bk, Wv, bv, Wo, bo):
        import jax, jax.numpy as jnp
        import numpy as np
        EMBED = 128
        HEADS = 16
        HEAD_SIZE = EMBED // HEADS
        B, Sq, E = q.shape
        Sk = k.shape[1]
        qh = (q @ Wq.T + bq).reshape(B, Sq, HEADS, HEAD_SIZE)
        kh = (k @ Wk.T + bk).reshape(B, Sk, HEADS, HEAD_SIZE)
        vh = (v @ Wv.T + bv).reshape(B, Sk, HEADS, HEAD_SIZE)
        scores = jnp.einsum('bqhe,bkhe->bhqk', qh, kh) / jnp.sqrt(jnp.float32(E))
        probs = jax.nn.softmax(scores, axis=-1)
        attn = jnp.einsum('bhqk,bkhd->bqhd', probs, vh)
        out = attn.reshape(B, Sq, E) @ Wo.T + bo
        return out

    def _L0_ffn_ref(x, Wm, bm, expert_emb, W1, b1, W2, b2, Wo, bo):
        import jax, jax.numpy as jnp
        import numpy as np
        BS, L, D = (4, 256, 128)
        H, E, K = (8, 16, 2)
        HD = D // H
        I = 512 // H
        bs, L_, d = x.shape
        h = x @ Wm + bm
        t = h.reshape(bs * L_ * H, HD)
        logits = t @ expert_emb
        w = jax.nn.softmax(logits, axis=-1)
        topw, topi = jax.lax.top_k(w, K)
        hmid = jax.nn.gelu(jnp.einsum('td,edi->tei', t, W1) + b1, approximate=False)
        eo = jnp.einsum('tei,eio->teo', hmid, W2) + b2
        sel = jnp.take_along_axis(eo, topi[:, :, None], axis=1)
        comb = (sel * topw[:, :, None]).sum(axis=1)
        out = comb.reshape(bs, L_, d)
        return out @ Wo + bo

    def _L1_attn_ref(x, wq, bq, wk, bk, wv, bv, wo, bo, rot_cos, rot_sin):
        import jax, jax.numpy as jnp
        import numpy as np
        MODEL_DIM = 128
        NUM_HEADS = 16
        D_K = MODEL_DIM // NUM_HEADS
        MAX_SEQ_LEN = 512

        def _xavier(key, shape):
            fan_in, fan_out = (shape[1], shape[0])
            limit = np.sqrt(6.0 / (fan_in + fan_out)).astype(np.float32)
            return jax.random.uniform(key, shape, jnp.float32, -limit, limit)
        b, t, m = x.shape
        h, d = (NUM_HEADS, m // NUM_HEADS)
        q = (x @ wq.T + bq).reshape(b, h, t, d)
        k = (x @ wk.T + bk).reshape(b, h, t, d)
        v = (x @ wv.T + bv).reshape(b, h, t, d)
        c = rot_cos[t]
        s = rot_sin[t]

        def rope(u):
            ur = u.reshape(b, h, t, d // 2, 2)
            re, im = (ur[..., 0], ur[..., 1])
            return jnp.stack([re * c - im * s, re * s + im * c], axis=-1).reshape(b, h, t, d)
        q, k = (rope(q), rope(k))
        scores = jnp.einsum('bhqd,bhkd->bhqk', q, k) / np.float32(np.sqrt(d))
        p = jax.nn.softmax(scores, axis=-1)
        o = jnp.einsum('bhqk,bhkd->bhqd', p, v)
        o = o.transpose(0, 2, 1, 3).reshape(b, t, m)
        return o @ wo.T + bo

    def _L1_xattn_ref(query, key, value, key_abundance, in_proj_weight, in_proj_bias, out_proj_weight, out_proj_bias, num_heads):
        import jax, jax.numpy as jnp
        import numpy as np
        B, N, E, H = (2, 256, 128, 16)
        HD = E // H
        b, n_q, e = query.shape
        n_k = key.shape[1]
        hd = in_proj_weight.shape[1] // num_heads
        w_q, w_k, w_v = jnp.split(in_proj_weight, 3, axis=0)
        b_q, b_k, b_v = jnp.split(in_proj_bias, 3, axis=0)
        q = query @ w_q.T + b_q
        k = key @ w_k.T + b_k
        v = value @ w_v.T + b_v
        q = q.reshape(b, n_q, num_heads, hd).transpose(0, 2, 1, 3)
        k = k.reshape(b, n_k, num_heads, hd).transpose(0, 2, 1, 3)
        v = v.reshape(b, n_k, num_heads, hd).transpose(0, 2, 1, 3)
        scale = 1.0 / jnp.sqrt(jnp.asarray(hd, dtype=q.dtype))
        scores = jnp.einsum('bhqd,bhkd->bhqk', q, k) * scale
        scores = scores + jnp.log(key_abundance)[:, None, None, :]
        attn = jax.nn.softmax(scores, axis=-1)
        out = jnp.einsum('bhqk,bhkd->bhqd', attn, v)
        out = out.transpose(0, 2, 1, 3).reshape(b, n_q, num_heads * hd)
        return out @ out_proj_weight.T + out_proj_bias

    def _L1_ffn_ref(x, norm_scale, w_router, w_up, w_down):
        import jax, jax.numpy as jnp
        import numpy as np
        DIM = 128
        HIDDEN = 256
        N_EXPERTS = 8
        TOP_K = 2
        EPS = 1e-06

        def rms_norm(x, scale, eps=EPS):
            ms = jnp.mean(jnp.square(x.astype(jnp.float32)), axis=-1, keepdims=True)
            s = scale.astype(jnp.float32) * jax.lax.rsqrt(ms + eps)
            return x * s.astype(x.dtype)

        def moe_linear(xf, ids, W):
            E = W.shape[0]
            out = jnp.zeros((xf.shape[0], W.shape[1]), dtype=xf.dtype)
            for e in range(E):
                out = out + jnp.where((ids == e)[:, None], xf @ W[e].T, 0.0)
            return out
        B, S, D = x.shape
        skip = x
        xn = rms_norm(x, norm_scale)
        scores = (xn @ w_router.T).astype(jnp.float32)
        scores_topk, idx = jax.lax.top_k(scores, TOP_K)
        weights = jax.nn.softmax(scores_topk, axis=-1)
        xf = jnp.broadcast_to(xn[..., None, :], (B, S, TOP_K, D)).reshape(-1, D)
        ids = idx.reshape(-1)
        up = moe_linear(xf, ids, w_up)
        u, gate = jnp.split(up, 2, axis=-1)
        h = u * jax.nn.silu(gate)
        down = moe_linear(h, ids, w_down)
        down = down.reshape(B, S, TOP_K, D)
        out = jnp.sum(down * weights[..., None].astype(down.dtype), axis=-2)
        return out + skip
    x = x + _L0_attn_ref(_layernorm(x, axis=-1), L0_attn_Wq, L0_attn_Wk, L0_attn_Wv, L0_attn_Wp, L0_attn_bp)
    x = x + _L0_xattn_ref(_layernorm(x, axis=-1), ctx_1024, ctx_1024, L0_xattn_Wq, L0_xattn_bq, L0_xattn_Wk, L0_xattn_bk, L0_xattn_Wv, L0_xattn_bv, L0_xattn_Wo, L0_xattn_bo)
    x = x + _L0_ffn_ref(_layernorm(x, axis=-1), L0_ffn_Wm, L0_ffn_bm, L0_ffn_expert_emb, L0_ffn_W1, L0_ffn_b1, L0_ffn_W2, L0_ffn_b2, L0_ffn_Wo, L0_ffn_bo)
    x = x + _L1_attn_ref(_layernorm(x, axis=-1), L1_attn_wq, L1_attn_bq, L1_attn_wk, L1_attn_bk, L1_attn_wv, L1_attn_bv, L1_attn_wo, L1_attn_bo, L1_attn_rot_cos, L1_attn_rot_sin)
    x = x + _L1_xattn_ref(_layernorm(x, axis=-1), ctx_1024, ctx_1024, fside_BxS2_0, L1_xattn_in_proj_weight, L1_xattn_in_proj_bias, L1_xattn_out_proj_weight, L1_xattn_out_proj_bias, 16)
    x = x + _L1_ffn_ref(_layernorm(x, axis=-1), L1_ffn_norm_scale, L1_ffn_w_router, L1_ffn_w_up, L1_ffn_w_down)
    return x

_drawn_inputs = setup_inputs


def setup_inputs(seed=0):
    import zlib

    import numpy as np

    out = dict(_drawn_inputs(seed))
    spreads = {'L0_attn_bp': (0.0, 0.1),
     'L0_xattn_bq': (0.0, 0.659),
     'L0_xattn_bk': (0.0, 0.8),
     'L0_xattn_bv': (0.0, 0.1),
     'L0_xattn_bo': (0.0, 0.1),
     'L0_ffn_bm': (0.0, 0.1),
     'L0_ffn_b1': (0.0, 0.1),
     'L0_ffn_b2': (0.0, 0.1),
     'L0_ffn_bo': (0.0, 0.1),
     'L1_attn_bq': (0.0, 0.614),
     'L1_attn_bk': (0.0, 0.532),
     'L1_attn_bv': (0.0, 0.1),
     'L1_attn_bo': (0.0, 0.1),
     'L1_ffn_norm_scale': (1.0, 0.2)}
    factors = {'L0_attn_Wq': 8.0,
     'L0_attn_Wk': 8.0,
     'L0_attn_Wv': 3.543,
     'L0_attn_Wp': 3.551,
     'L1_xattn_in_proj_bias': 3.096,
     'L1_xattn_out_proj_bias': 3.427}
    for name, (base, spread) in spreads.items():
        noise = np.random.default_rng([zlib.crc32(name.encode()), seed]).standard_normal(out[name].shape)
        drawn = base * np.exp(spread * noise) if base else spread * noise
        out[name] = jnp.asarray(drawn.astype(out[name].dtype))
    for name, factor in factors.items():
        out[name] = (out[name] * factor).astype(out[name].dtype)
    return out
```

```python
import math
from contextlib import ExitStack

import concourse.bass as bass
from concourse import mybir

F32, F32R = mybir.dt.float32, mybir.dt.float32r
ACT = mybir.ActivationFunctionType
ALU = mybir.AluOpType
AX = mybir.AxisListType

BATCH, SEQ, EMB, CTX = 64, 128, 128, 120
HEADS, HD = 16, 8
G = 2


class Step:

    def __init__(self, i, off):
        self.i, self.off, self.static, self.ring = i, off, isinstance(i, int), off % 2

    def back(self, n):
        return Step(self.i, self.off - n)

    def count(self, per_step, plus):
        return self.i * (2 * per_step) + (self.off * per_step + plus)

    def half(self, per_use, uses=0):
        return self.i * per_use + (self.off // 2 + uses) * per_use

    def ds(self, n):
        return bass.ds(self.i * (2 * n) + self.off * n, n)

    def ds1(self, n, b):
        return bass.ds(self.i * (2 * n) + (self.off * n + b), 1)


def need(eng, sem, value):
    if not isinstance(value, int) or value > 0:
        eng.wait_ge(sem, value)


class Semaphores:

    def __init__(self, nc, ctx, tag):
        self.nc, self.tag, self.made = nc, tag, []
        ctx.callback(self.zero)

    def __call__(self, name):
        self.made.append(self.nc.alloc_semaphore(f"{self.tag}_{name}"))
        return self.made[-1]

    def zero(self):
        self.nc.all_engine_barrier()
        self.nc.clear_and_free_semaphores(self.made)
        self.nc.all_engine_barrier()


def raw_words(ap):
    return ap.bitcast(F32)


ALL_PHASES = ("a0", "c0", "f0", "a1", "c1", "f1")


def attention_phase(nc, kind, tag, x_sb, const, stacks, dram):
    cross = kind in ("cross", "weighted")
    linear, scrambled, weighted = kind == "linear", kind == "scrambled", kind == "weighted"
    keys = CTX if cross else SEQ
    kn, qn = G * keys, G * SEQ
    scale = 1.0 if linear else 1.0 / math.sqrt(EMB if kind == "cross" else HD)
    q_blocks, k_stack, q_hi, k_blocks = stacks["q_blocks"], stacks["k_stack"], stacks["q_hi"], stacks["k_blocks"]
    steps_n = BATCH // G
    uses = [("xnT", 0), ("q", 0), ("k", 0), ("v", 0)]
    if cross:
        uses = [("maxT", 2), ("ctxT", 0)] + uses
    if scrambled:
        uses = [("maxT", 2)] + uses + [("vback", 1)]
    uses += [("y1", 3), ("y0", 2)]
    pos = {name: n for n, (name, _) in enumerate(uses)}
    n_max, n_sp, n_pool, n_shift = (4, 8, 4, 4) if scrambled else (5, 8, 7, 1)

    ctx = ExitStack()
    with ctx:
        def sb(name, shape, dt=F32):
            return ctx.enter_context(nc.sbuf_tensor(f"{tag}_{name}", shape, dt))

        sem = Semaphores(nc, ctx, tag)

        def sem2(name):
            return [sem(f"{name}{r}") for r in range(2)]

        wq, wk, wv = sb("wq", [128, EMB]), sb("wk", [128, EMB]), sb("wv", [128, EMB])
        wo, bo = sb("wo", [128, 4, EMB]), sb("bo", [128, EMB])
        bq, bk, bv = sb("bq", [128, 1]), sb("bk", [128, 1]), sb("bv", [128, EMB])
        stats, mv = sb("stats", [128, 2, G, 6]), sb("mv", [128, 2, G, 2])
        logvar, rstd = sb("logvar", [128, 2, G]), sb("rstd", [128, 2, G])
        xn, lnT = sb("xn", [128, 2, G, EMB]), sb("lnT", [128, 2, qn])
        q_parts, k_parts = sb("q_parts", [128, 2, 2, qn], F32R), sb("k_parts", [128, 2, 2, kn], F32R)
        v_raw, v_sb = sb("v_raw", [128, 2, G, EMB]), sb("v", [128, 2, G, EMB])
        if cross:
            ctx_in, ctxT = sb("ctx_in", [128, 2, G, EMB]), sb("ctxT", [128, 2, kn])
        if linear:
            feat = sb("feat", [128, 2, 2, 3, qn])
        else:
            negmax, negmaxT = sb("negmax", [128, 2, 16 * G]), sb("negmaxT", [16 if scrambled else 16 * G, 2, 16 * G * HD if scrambled else SEQ], F32R)
        if scrambled:
            vT, v_stack = sb("vT", [128, 2, qn]), sb("v_stack", [32, 4 * qn])
            k_placed, q_placed, v_placed = sb("k_placed", [128, 2, 4 * qn], F32R), sb("q_placed", [32, 2, 4 * qn], F32R), sb("v_placed", [32, 2, 4 * qn])
            rot, raw, raw_b = sb("rot", [128, 2, 4]), sb("raw", [128, 2, EMB]), sb("raw_b", [1, 2, EMB])
            rope_tmp, rot_b = sb("rope_tmp", [128, 2, 4, 16]), sb("rot_b", [1, 2, EMB])
            query_f, query_r, max_spread = sb("query_f", [128, 16], F32R), sb("query_r", [128, 8]), sb("max_spread", [128, 16 * G, 8], F32R)
        if weighted:
            den_w = sb("den_w", [128, 2, G, 32])
        probs = sb("probs", [128, 4, 512])
        logden, recip, attended = sb("logden", [128, 2, 512]), sb("recip", [128, 2, 512]), sb("attended", [128, 2, 512])
        banks = [ctx.enter_context(nc.psum_tensor(f"{tag}_bank{n}", [128, 512], F32)) for n in range(8)]
        misc, score_ps, scoreT_ps, out_ps, den_ps = banks[0:2], banks[2:4], banks[4:6], banks[6], banks[7]
        passed = {eng.engine: sem(f"passed_{name}") for name, eng in (("dve", nc.vector), ("pool", nc.gpsimd), ("pe", nc.tensor), ("sp", nc.sync))}
        weights_in, stats_done, mv_done = sem("weights_in"), sem("stats_done"), sem("mv_done")
        logvar_done, rstd_done, xn_done, x_biased = sem("logvar_done"), sem("rstd_done"), sem("xn_done"), sem("x_biased")
        xnT_mm, q_mm, k_mm, v_mm = sem("xnT_mm"), sem("q_mm"), sem("k_mm"), sem("v_mm")
        lnT_ready, vraw_ready, v_ready = sem("lnT_ready"), sem("vraw_ready"), sem("v_ready")
        qhi_ready, qlo_ready, khi_ready, klo_ready = sem("qhi_ready"), sem("qlo_ready"), sem("khi_ready"), sem("klo_ready")
        stack_sp, stack_pool = sem2("stack_sp"), sem2("stack_pool")
        scoresT_mm, probs_ready, values_mm = sem("scoresT_mm"), sem("probs_ready"), sem("values_mm")
        logden_ready, recip_ready, attended_ready = sem("logden_ready"), sem("recip_ready"), sem("attended_ready")
        y_mm, y_added = sem("y_mm"), sem("y_added")
        if cross:
            ctx_loaded, ctxT_mm, ctxT_ready = sem2("ctx_loaded"), sem("ctxT_mm"), sem("ctxT_ready")
        if linear:
            feat_act, feat_done = sem("feat_act"), sem("feat_done")
        else:
            max_in, shift_in = sem2("max_in"), sem2("shift_in")
            scores_mm, max_done, maxT_mm, maxT_ready = sem("scores_mm"), sem("max_done"), sem("maxT_mm"), sem("maxT_ready")
        if scrambled:
            max_spread_done, queries_made = sem("max_spread_done"), sem("queries_made")
            vT_ready, vback_mm, v_in = sem("vT_ready"), sem("vback_mm"), sem2("v_in")
            k_in, k_in_pool, q_in = sem2("k_in"), sem2("k_in_pool"), sem2("q_in")
            q_grouped, k_grouped, v_grouped = sem("q_grouped"), sem("k_grouped"), sem("v_grouped")
            rope_in, rope_mul, rope_add, rope_done = sem("rope_in"), sem("rope_mul"), sem("rope_add"), sem("rope_done")

        def head(tile, g, b, n):
            return tile[:, (g * G + b) * n:(g * G + b + 1) * n]

        def heads4(tile, g, b, n):
            if scrambled:
                at = 16 * g + 8 * b
                return tile.rearrange("p j (f q) -> p j f q", f=16)[:, :, :, at:at + 8]
            return tile[:, :, (g * G + b) * n:(g * G + b + 1) * n]

        def rows_of(parts, r, part, j):
            return raw_words(parts[:, r, part, 64 * j:64 * j + 64] if scrambled else parts[32 * j:32 * j + 32, r, part, :])

        def grouped(tile):
            return tile.rearrange("p (q f r) -> p q f r", f=16, r=8)

        def placed(tile):
            return tile.rearrange("p (f q r) -> p q f r", f=16, r=8)

        def live(s):
            return not s.static or 0 <= s.off < steps_n

        def run_steps(eng, body, before_loop=None):
            lead = 5
            loops = (steps_n - lead) // 2
            for t in range(lead):
                body(Step(0, t))
            if before_loop:
                before_loop()
            with eng.Fori(0, loops) as i:
                for u in range(2):
                    body(Step(i, lead + u))
            for t in range(lead + 2 * loops, steps_n + 3):
                body(Step(0, t))

        n_weights = 8 if not linear else 5

        def pass_waits(eng):
            eng.sem_inc(passed[eng.engine], 1)

        with nc.Block() as block:
            @block.sync
            def _(sp):
                sp.dma_start(raw[:, 0, :] if scrambled else wq[:], dram["wq"]).then_inc(weights_in, 16)
                sp.dma_start(raw[:, 1, :] if scrambled else wk[:], dram["wk"]).then_inc(weights_in, 16)
                sp.dma_start(wv[:], dram["wv"]).then_inc(weights_in, 16)
                sp.dma_start(wo[:], dram["wo"]).then_inc(weights_in, 16)
                sp.dma_start(bo[:], dram["bo"].broadcast_to([128, EMB])).then_inc(weights_in, 16)
                if scrambled:
                    sp.dma_start(raw_b[:, 0, :], dram["bq"]).then_inc(weights_in, 16)
                    sp.dma_start(raw_b[:, 1, :], dram["bk"]).then_inc(weights_in, 16)
                    sp.dma_start(bv[:, 0:1], dram["bv"]).then_inc(weights_in, 16)
                    sp.dma_start(rot[:, 0, :], dram["cos"].broadcast_to([128, 4])).then_inc(rope_in, 16)
                    sp.dma_start(rot[:, 1, :], dram["sin"].broadcast_to([128, 4])).then_inc(rope_in, 16)
                    sp.wait_ge(rope_done, 1)
                    sp.dma_start(bq[:], rot_b[0:1, 0, :]).then_inc(rope_in, 16)
                    sp.dma_start(bk[:], rot_b[0:1, 1, :]).then_inc(rope_in, 16)
                elif not linear:
                    sp.dma_start(bq[:], dram["bq"]).then_inc(weights_in, 16)
                    sp.dma_start(bk[:], dram["bk"]).then_inc(weights_in, 16)
                    sp.dma_start(bv[:], dram["bv"].broadcast_to([128, EMB])).then_inc(weights_in, 16)

                def load_ctx(s):
                    need(sp, ctxT_mm, s.count(1, -1))
                    pass_waits(sp)
                    sp.dma_start(ctx_in[:CTX, s.ring, :, :], dram["ctx"][s.ds(G), :, :].rearrange("b s e -> s b e")) \
                        .then_inc(ctx_loaded[s.ring], 16)

                if cross:
                    load_ctx(Step(0, 0))

                def step(t):
                    r = t.ring
                    if cross and live(t.back(-1)):
                        load_ctx(t.back(-1))
                    if not live(t):
                        return
                    if not linear:
                        need(sp, scores_mm, t.back(1).count(8, 0))
                        pass_waits(sp)
                        sp.wait_ge(qhi_ready, t.count(1, 1))
                        if scrambled:
                            for j in range(4):
                                sp.dma_start(raw_words(q_placed[8 * j:8 * j + 8, r, :]), rows_of(q_parts, r, 0, j)).then_inc(q_in[r], 16)
                        else:
                            sp.dma_start(raw_words(q_hi[r][0:32, :]), raw_words(q_parts[:, r, 0, :])).then_inc(max_in[r], 16)
                        sp.wait_ge(khi_ready, t.count(1, 1))
                        for j in range(4):
                            sp.dma_start(raw_words(k_blocks[r][8 * j:8 * j + 8, j, :4 * kn]), rows_of(k_parts, r, 0, j)).then_inc(max_in[r], 16)
                    need(sp, scoresT_mm, t.back(1).count(8, 0))
                    pass_waits(sp)
                    sp.wait_ge(qhi_ready, t.count(1, 1))
                    for rep in range(2):
                        for j in range(4):
                            at = 32 * rep + 8 * j
                            sp.dma_start(raw_words(q_blocks[r][at:at + 8, j, :]), rows_of(q_parts, r, 0, j)).then_inc(stack_sp[r], 16)
                    if scrambled:
                        sp.wait_ge(khi_ready, t.count(1, 1))
                        for j in range(4):
                            sp.dma_start(raw_words(k_placed[8 * j:8 * j + 8, r, :]), rows_of(k_parts, r, 0, j)).then_inc(k_in[r], 16)

                run_steps(sp, step)

            @block.gpsimd
            def _(pool):
                pool.wait_ge(weights_in, 16 * n_weights)

                def step(t):
                    if not live(t):
                        return
                    r = t.ring
                    pool.wait_ge(xn_done, t.count(1, 1))
                    pool.tensor_tensor(x_sb[:, t.ds(G), :], x_sb[:, t.ds(G), :],
                                       bo[:].unsqueeze(1).broadcast_to([128, G, EMB]), ALU.add).then_inc(x_biased, 1)
                    need(pool, scoresT_mm, t.back(1).count(8, 0))
                    pool.wait_ge(khi_ready, t.count(1, 1))
                    pool.wait_ge(klo_ready, t.count(1, 1))
                    pass_waits(pool)
                    for rep, part in ((0, 0), (1, 1), (2, 0)):
                        if not scrambled:
                            pool.dma_start(raw_words(k_stack[r][32 * rep:32 * rep + 32, :4 * kn]), raw_words(k_parts[:, r, part, :])).then_inc(stack_pool[r], 16)
                        elif rep:
                            for j in range(4):
                                at = 32 * rep + 8 * j
                                pool.dma_start(raw_words(k_placed[at:at + 8, r, :]), rows_of(k_parts, r, part, j)).then_inc(k_in_pool[r], 16)
                    pool.wait_ge(qlo_ready, t.count(1, 1))
                    pass_waits(pool)
                    for j in range(4):
                        pool.dma_start(raw_words(q_blocks[r][64 + 8 * j:72 + 8 * j, j, :]), rows_of(q_parts, r, 1, j)).then_inc(stack_pool[r], 16)
                    if not scrambled:
                        pool.wait_ge(vraw_ready, t.count(1, 1))
                        need(pool, values_mm, t.back(1).count(8, 0))
                        pass_waits(pool)
                        if weighted:
                            a = const["abundance"][:keys, t.ds(G)].unsqueeze(2)
                            pool.tensor_tensor(v_sb[:keys, r], v_raw[:keys, r], a.broadcast_to([keys, G, EMB]), ALU.mult)
                            pool.tensor_tensor(den_w[:keys, r], const["ones"][:keys, 0:32].unsqueeze(1).broadcast_to([keys, G, 32]),
                                               a.broadcast_to([keys, G, 32]), ALU.mult).then_inc(v_ready, 1)
                        else:
                            pool.tensor_copy(v_sb[:keys, r], v_raw[:keys, r]).then_inc(v_ready, 1)

                run_steps(pool, step)

            @block.scalar
            def _(act):
                act.preload_act_table_set("natural_log_exp_and_others")
                act.wait_ge(weights_in, 16 * n_weights)
                if scrambled:
                    act.wait_ge(rope_in, 64)

                def rstd_of(s):
                    act.wait_ge(mv_done, s.count(1, 1))
                    act.activation(logvar[:, s.ring, :], mv[:, s.ring, :, 1], ACT.Ln, bias=const["eps_ln"][:]).then_inc(logvar_done, 1)
                    act.wait_ge(logvar_done, s.count(1, 1))
                    need(act, xn_done, s.count(1, -1))
                    act.activation(rstd[:, s.ring, :], logvar[:, s.ring, :], ACT.Exp, scale=-0.5).then_inc(rstd_done, 1)

                def recip_of(s, b):
                    act.wait_ge(values_mm, s.count(8, 4 * b + 4))
                    need(act, recip_ready, s.count(2, b - 1))
                    act.activation(logden[:, b, :], den_ps[:], ACT.Ln, bias=const["eps_den" if linear else "zero"][:]).then_inc(logden_ready, 1)
                    act.wait_ge(logden_ready, s.count(2, b + 1))
                    need(act, attended_ready, s.count(2, b - 1))
                    act.activation(recip[:, b, :], logden[:, b, :], ACT.Exp, scale=-1.0).then_inc(recip_ready, 1)

                rstd_of(Step(0, 0))

                def step(t):
                    C = t.back(2)
                    r = t.ring
                    if not linear and live(C):
                        act.wait_ge(maxT_mm, C.count(1, 1))
                        need(act, shift_in[C.ring], C.half(16 * n_shift))
                        act.activation(negmaxT[:, C.ring, :], misc[0][0:negmaxT.shape[0], 0:negmaxT.shape[2]], ACT.Copy).then_inc(maxT_ready, 1)
                        act.wait_ge(maxT_ready, C.count(1, 1))
                        need(act, scoresT_mm, C.back(1).count(8, 0))
                        if scrambled:
                            for j in range(4):
                                act.dma_start(raw_words(q_blocks[C.ring][96:97, j, :]), raw_words(negmaxT[:, C.ring, 32 * G * j:32 * G * (j + 1)])) \
                                    .then_inc(shift_in[C.ring], 16)
                        else:
                            act.dma_start(raw_words(q_blocks[C.ring][96:97, :, :]), raw_words(negmaxT[:, C.ring, :])).then_inc(shift_in[C.ring], 16)
                    if scrambled and live(t.back(1)):
                        B = t.back(1)
                        act.wait_ge(q_in[B.ring], B.half(16 * 4, 1))
                        need(act, scores_mm, B.back(1).count(8, 0))
                        act.activation(grouped(q_hi[B.ring][0:32, :]), placed(q_placed[:, B.ring, :]), ACT.Copy).then_inc(q_grouped, 1)
                    if live(t):
                        if cross:
                            act.wait_ge(ctxT_mm, t.count(1, 1))
                            need(act, v_mm, t.count(1, -1))
                            act.activation(ctxT[:, r, :], misc[pos["ctxT"] % 2][:, 0:kn], ACT.Copy).then_inc(ctxT_ready, 1)
                        bank = misc[pos["xnT"] % 2]
                        act.wait_ge(xnT_mm, t.count(1, 1))
                        need(act, v_mm, t.count(1, -1))
                        if scrambled:
                            for b in range(G):
                                act.activation(lnT[:, r, :].rearrange("p (j g b r) -> p b g j r", j=4, g=4, b=G)[:, b],
                                               bank[:, b * SEQ:(b + 1) * SEQ].rearrange("p (g j r) -> p g j r", g=4, j=4), ACT.Copy).then_inc(lnT_ready, 1)
                        else:
                            act.activation(lnT[:, r, :], bank[:, 0:qn], ACT.Copy).then_inc(lnT_ready, G)
                        for w, (mm, hi, parts, bias, n) in enumerate(((q_mm, qhi_ready, q_parts, bq, qn), (k_mm, khi_ready, k_parts, bk, kn))):
                            src = misc[(pos["q"] + w) % 2][:, 0:n]
                            act.wait_ge(mm, t.count(1, 1))
                            if linear:
                                need(act, feat_done, t.back(2).count(2, w + 1))
                                act.activation(feat[:, r, w, 0, :], src, ACT.Exp)
                                act.activation(feat[:, r, w, 1, :], src, ACT.Relu).then_inc(feat_act, 1)
                                act.wait_ge(feat_done, t.count(2, w + 1))
                                src = feat[:, r, w, 2, :]
                            need(act, stack_sp[r], t.half(16 * n_sp))
                            need(act, stack_pool[r], t.half(16 * n_pool))
                            if not linear:
                                need(act, max_in[r], t.half(16 * n_max))
                            if scrambled:
                                need(act, q_in[r], t.half(16 * 4))
                                need(act, k_in[r], t.half(16 * 4))
                                need(act, k_in_pool[r], t.half(16 * 8))
                            act.activation(parts[:, r, 0, :], src, ACT.Identity, bias=const["zero"][:] if linear else bias[:]).then_inc(hi, 1)
                        if scrambled:
                            act.wait_ge(vT_ready, t.count(1, 1))
                            need(act, v_grouped, t.count(1, -1))
                            for j in range(4):
                                act.dma_start(v_placed[8 * j:8 * j + 8, r, :], vT[:, r, 64 * j:64 * j + 64]).then_inc(v_in[r], 16)
                    if live(t.back(-1)):
                        rstd_of(t.back(-1))
                    if live(C):
                        for n in range(8):
                            if not linear:
                                act.wait_ge(scoresT_mm, C.count(8, n + 1))
                                need(act, values_mm, C.count(8, n - 3))
                                act.activation(probs[:keys, n % 4, :], scoreT_ps[n % 2][:keys, :], ACT.Exp, scale=scale).then_inc(probs_ready, 1)
                            if n == 5:
                                recip_of(C, 0)
                        recip_of(C, 1)

                run_steps(act, step)

            @block.vector
            def _(dve):
                dve.wait_ge(weights_in, 16 * n_weights)
                if scrambled:
                    ident = const["ident"][:]
                    dve.tensor_reduce(out=query_f[:], in_=ident.rearrange("p (f r) -> p f r", r=8), axis=AX.X, op=ALU.max).then_inc(queries_made, 1)
                    dve.tensor_reduce(out=query_r[:], in_=ident.rearrange("p (f r) -> p r f", r=8), axis=AX.X, op=ALU.max).then_inc(queries_made, 1)
                    dve.wait_ge(rope_in, 32)
                    turns = 0
                    for src, rows in ((raw, 128), (raw_b, 1)):
                        for w in range(2):
                            out = (wq, wk)[w][:] if rows == 128 else rot_b[:, w, :]
                            pair = src[:, w, :].rearrange("p (i e f) -> p e i f", e=2, f=16)
                            turned = out.rearrange("p (i e f) -> p e i f", e=2, f=16)
                            cos, sin = (rot[0:rows, n, :].unsqueeze(2).broadcast_to([rows, 4, 16]) for n in range(2))
                            for e, (p, q, op) in enumerate(((cos, sin, ALU.subtract), (sin, cos, ALU.add))):
                                need(dve, rope_add, turns)
                                dve.tensor_tensor(rope_tmp[0:rows, 0], pair[:, 0], p, ALU.mult).then_inc(rope_mul, 1)
                                dve.tensor_tensor(rope_tmp[0:rows, 1], pair[:, 1], q, ALU.mult).then_inc(rope_mul, 1)
                                turns += 1
                                dve.wait_ge(rope_mul, 2 * turns)
                                dve.tensor_tensor(turned[:, e], rope_tmp[0:rows, 0], rope_tmp[0:rows, 1], op).then_inc(rope_add, 1)
                    dve.wait_ge(rope_add, turns)
                    dve.sem_inc(rope_done, 1)
                    dve.wait_ge(rope_in, 64)

                def row_block(s, b):
                    return x_sb[:, s.ds1(G, b), :].rearrange("p a e -> p (a e)")

                def stats_of(s):
                    for b in range(G):
                        dve.bn_stats(stats[:, s.ring, b, :], row_block(s, b)).then_inc(stats_done, 1)
                    dve.wait_ge(stats_done, s.count(G, G))
                    pass_waits(dve)
                    for b in range(G):
                        last = dve.bn_aggr(mv[:, s.ring, b, :], stats[:, s.ring, b, :])
                    last.then_inc(mv_done, 1)

                def normalise(s):
                    dve.wait_ge(rstd_done, s.count(1, 1))
                    dve.wait_ge(mv_done, s.count(1, 1))
                    need(dve, xnT_mm, s.count(1, -1))
                    for b in range(G):
                        last = dve.tensor_scalar(xn[:, s.ring, b, :], row_block(s, b), mv[:, s.ring, b, 0:1], rstd[:, s.ring, b:b + 1],
                                                 ALU.subtract, ALU.mult)
                    last.then_inc(xn_done, 1)

                def add_y(s, b):
                    dve.wait_ge(y_mm, s.count(2, b + 1))
                    dve.wait_ge(x_biased, s.count(1, 1))
                    dve.tensor_tensor(row_block(s, b), misc[1 - b][:, 0:EMB], row_block(s, b), ALU.add).then_inc(y_added, 1)

                def attend(s, b):
                    dve.wait_ge(recip_ready, s.count(2, b + 1))
                    need(dve, y_mm, s.count(2, b - 1))
                    def view(tile, order):
                        return tile.rearrange(f"p (j {order}) -> p j f r", j=4, f=16) if scrambled else tile

                    dve.tensor_tensor(view(attended[:, b, :], "r f"), view(out_ps[:], "f r"), view(recip[:, b, :], "f r"), ALU.mult).then_inc(attended_ready, 1)

                stats_of(Step(0, 0))
                normalise(Step(0, 0))

                def step(t):
                    B, C, D = t.back(1), t.back(2), t.back(3)
                    r = t.ring
                    if scrambled and live(B):
                        dve.wait_ge(v_in[B.ring], B.half(16 * 4, 1))
                        need(dve, vback_mm, B.count(1, 0))
                        dve.tensor_copy(grouped(v_stack[:]), placed(v_placed[:, B.ring, :])).then_inc(v_grouped, 1)
                    if live(t.back(-1)):
                        stats_of(t.back(-1))
                    if live(t):
                        for w, (hi, lo, parts, bias, n) in enumerate(((qhi_ready, qlo_ready, q_parts, bq, qn), (khi_ready, klo_ready, k_parts, bk, kn))):
                            if linear:
                                dve.wait_ge(feat_act, t.count(2, w + 1))
                                dve.scalar_tensor_tensor(out=feat[:, r, w, 2, :], in0=feat[:, r, w, 0, :], scalar=1.0, in1=feat[:, r, w, 1, :],
                                                         op0=ALU.min, op1=ALU.add).then_inc(feat_done, 1)
                                dve.wait_ge(feat_done, t.count(2, w + 1))
                                dve.wait_ge(hi, t.count(1, 1))
                                dve.tensor_tensor(parts[:, r, 1, :], feat[:, r, w, 2, :], parts[:, r, 0, :], ALU.subtract).then_inc(lo, 1)
                            else:
                                dve.wait_ge(hi, t.count(1, 1))
                                dve.scalar_tensor_tensor(out=parts[:, r, 1, :], in0=misc[(pos["q"] + w) % 2][:, 0:n], scalar=bias[:],
                                                         in1=parts[:, r, 0, :], op0=ALU.add, op1=ALU.subtract).then_inc(lo, 1)
                        bank = misc[pos["v"] % 2]
                        dve.wait_ge(v_mm, t.count(1, 1))
                        if scrambled:
                            need(dve, v_in[r], t.half(16 * 4))
                            dve.tensor_scalar(vT[:, r, :], bank[:, 0:qn], bv[:, 0:1], None, ALU.add).then_inc(vT_ready, 1)
                        else:
                            src = bank[:keys, 0:G * EMB].rearrange("p (b e) -> p b e", b=G)
                            need(dve, v_ready, t.count(1, -1))
                            if linear:
                                dve.tensor_copy(v_raw[:keys, r], src).then_inc(vraw_ready, 1)
                            else:
                                dve.tensor_tensor(v_raw[:keys, r], src, bv[:keys].unsqueeze(1).broadcast_to([keys, G, EMB]), ALU.add).then_inc(vraw_ready, 1)
                    if scrambled and live(B):
                        dve.wait_ge(vback_mm, B.count(1, 1))
                        need(dve, values_mm, B.back(1).count(8, 0))
                        dve.tensor_copy(v_sb[:, B.ring].rearrange("p b e -> p (b e)"), misc[pos["vback"] % 2][:, 0:G * EMB]).then_inc(v_ready, 1)
                    if live(D):
                        add_y(D, 1)
                    for n in range(8):
                        b, g = divmod(n, 4)
                        if live(C) and n == 6:
                            attend(C, 0)
                        if not linear and live(B):
                            dve.wait_ge(scores_mm, B.count(8, n + 1))
                            if n == 0:
                                need(dve, maxT_mm, B.count(1, -1))
                            dve.tensor_reduce(out=negmax[:, B.ring, :].rearrange("p (j q) -> p j q", j=4)[:, :, g * G + b],
                                              in_=score_ps[n % 2][:, 0:4 * keys].rearrange("p (j k) -> p j k", j=4),
                                              axis=AX.X, op=ALU.max, negate=True).then_inc(max_done, 1)
                        if scrambled and live(B) and n == 7:
                            dve.wait_ge(max_done, B.count(8, 8))
                            dve.wait_ge(queries_made, 2)
                            need(dve, maxT_mm, B.count(1, 0))
                            dve.tensor_tensor(max_spread[:], negmax[:, B.ring, :].unsqueeze(2).broadcast_to([128, 16 * G, 8]),
                                              query_r[:].unsqueeze(1).broadcast_to([128, 16 * G, 8]), ALU.mult).then_inc(max_spread_done, 1)
                        if linear and live(C):
                            dve.wait_ge(scoresT_mm, C.count(8, n + 1))
                            need(dve, values_mm, C.count(8, n - 3))
                            dve.tensor_tensor(probs[:, n % 4, :].rearrange("p (j c) -> p j c", j=4),
                                              scoreT_ps[n % 2][:].rearrange("p (j c) -> p j c", j=4),
                                              const["causal"][:].unsqueeze(1).broadcast_to([128, 4, SEQ]), ALU.mult).then_inc(probs_ready, 1)
                    if live(t.back(-1)):
                        normalise(t.back(-1))
                    if scrambled and live(B):
                        dve.wait_ge(k_in[B.ring], B.half(16 * 4, 1))
                        dve.wait_ge(k_in_pool[B.ring], B.half(16 * 8, 1))
                        need(dve, scoresT_mm, B.back(1).count(8, 0))
                        dve.tensor_copy(grouped(k_stack[B.ring][0:96, :]), placed(k_placed[0:96, B.ring, :])).then_inc(k_grouped, 1)
                    if live(C):
                        add_y(C, 0)
                        attend(C, 1)

                run_steps(dve, step)

            @block.tensor
            def _(pe):
                pe.wait_ge(weights_in, 16 * n_weights)
                if scrambled:
                    pe.wait_ge(rope_done, 1)
                rows = 96 if linear else 97

                def used(name, s):
                    if name in ("q", "k") and linear:
                        return feat_act, s.count(2, 1 + (name == "k"))
                    return {
                        "maxT": lambda: (maxT_ready, s.count(1, 1)), "ctxT": lambda: (ctxT_ready, s.count(1, 1)),
                        "xnT": lambda: (lnT_ready, s.count(G, G)), "q": lambda: (qlo_ready, s.count(1, 1)),
                        "k": lambda: (klo_ready, s.count(1, 1)),
                        "v": lambda: (vT_ready if scrambled else vraw_ready, s.count(1, 1)),
                        "vback": lambda: (v_ready, s.count(1, 1)),
                        "y1": lambda: (y_added, s.count(2, 2)), "y0": lambda: (y_added, s.count(2, 1)),
                    }[name]()

                def take_bank(name, s):
                    at = pos[name]
                    while True:
                        at -= 2
                        if at < 0:
                            at += len(uses)
                            s = s.back(1)
                        if s.static and s.off < 0:
                            return
                        before, lag = uses[at]
                        if live(s.back(lag)):
                            pe.wait_ge(*used(before, s.back(lag)))
                            return

                def project_out(s, b, t):
                    pe.wait_ge(attended_ready, s.count(2, b + 1))
                    take_bank(f"y{b}", t)
                    for j in range(4):
                        last = pe.matmul(misc[1 - b][:, 0:EMB], attended[:, b, j * SEQ:(j + 1) * SEQ], wo[:, j, :], start=(j == 0), stop=(j == 3))
                    last.then_inc(y_mm, 1)

                def step(t):
                    B, C, D = t.back(1), t.back(2), t.back(3)
                    r = t.ring
                    if not linear and live(C):
                        take_bank("maxT", t)
                        if scrambled:
                            pe.wait_ge(queries_made, 2)
                            pe.wait_ge(max_spread_done, C.count(1, 1))
                            pe.matmul(misc[0][0:16, 0:16 * G * 8], query_f[:], max_spread[:].rearrange("p q r -> p (q r)"), start=True, stop=True).then_inc(maxT_mm, 1)
                        else:
                            pe.wait_ge(max_done, C.count(8, 8))
                            pe.transpose(misc[0][0:16 * G, 0:SEQ], negmax[:, C.ring, :], const["ident"][:]).then_inc(maxT_mm, 1)
                    if live(t):
                        if cross:
                            pe.wait_ge(ctx_loaded[r], t.half(16, 1))
                            take_bank("ctxT", t)
                            for b in range(G):
                                last = pe.transpose(misc[pos["ctxT"] % 2][:, b * CTX:(b + 1) * CTX], ctx_in[:CTX, r, b, :], const["ident"][:CTX, :CTX])
                            last.then_inc(ctxT_mm, 1)
                        pe.wait_ge(xn_done, t.count(1, 1))
                        take_bank("xnT", t)
                        for b in range(G):
                            last = pe.transpose(misc[pos["xnT"] % 2][:, b * SEQ:(b + 1) * SEQ], xn[:, r, b, :], const["ident"][:])
                        last.then_inc(xnT_mm, 1)
                        pe.wait_ge(lnT_ready, t.count(G, G))
                        take_bank("q", t)
                        pe.matmul(misc[pos["q"] % 2][:, 0:qn], wq[:], lnT[:, r, :], start=True, stop=True).then_inc(q_mm, 1)
                        source = ctxT if cross else lnT
                        if cross:
                            pe.wait_ge(ctxT_ready, t.count(1, 1))
                        take_bank("k", t)
                        pe.matmul(misc[pos["k"] % 2][:, 0:kn], wk[:], source[:, r, :], start=True, stop=True).then_inc(k_mm, 1)
                        take_bank("v", t)
                        bank = misc[pos["v"] % 2]
                        if scrambled:
                            pe.matmul(bank[:, 0:qn], wv[:], lnT[:, r, :], start=True, stop=True).then_inc(v_mm, 1)
                        else:
                            for b in range(G):
                                last = pe.matmul(bank[:keys, b * EMB:(b + 1) * EMB], source[:, r, b * keys:(b + 1) * keys], wv[:], start=True, stop=True)
                            last.then_inc(v_mm, 1)
                    if scrambled and live(B):
                        pe.wait_ge(v_grouped, B.count(1, 1))
                        take_bank("vback", t)
                        pass_waits(pe)
                        for b in range(G):
                            for g in range(4):
                                at = b * EMB + 32 * g
                                last = pe.transpose(misc[pos["vback"] % 2][:, at:at + 32], head(v_stack[:], g, b, SEQ), const["ident"][:32, :32])
                        last.then_inc(vback_mm, 1)
                    if live(D):
                        project_out(D, 1, t)
                    for n in range(10):
                        b, g = divmod(n, 4)
                        if n < 8 and not linear and live(B):
                            if n == 0:
                                pe.wait_ge(max_in[B.ring], B.half(16 * n_max, 1))
                                if scrambled:
                                    pe.wait_ge(q_grouped, B.count(1, 1))
                            need(pe, max_done, B.count(8, n - 1))
                            pe.matmul(score_ps[n % 2][:, 0:4 * keys], head(q_hi[B.ring][:], g, b, SEQ), heads4(k_blocks[B.ring][:], g, b, keys),
                                      start=True, stop=True).then_inc(scores_mm, 1)
                        if n < 8 and live(C):
                            if n == 0:
                                pe.wait_ge(stack_sp[C.ring], C.half(16 * n_sp, 1))
                                pe.wait_ge(stack_pool[C.ring], C.half(16 * n_pool, 1))
                                if not linear:
                                    pe.wait_ge(shift_in[C.ring], C.half(16 * n_shift, 1))
                                pe.wait_ge(v_ready, C.count(1, 1))
                                if scrambled:
                                    pe.wait_ge(k_grouped, C.count(1, 1))
                            need(pe, probs_ready, C.count(8, n - 1))
                            pe.matmul(scoreT_ps[n % 2][:keys, :], head(k_stack[C.ring][0:rows], g, b, keys), heads4(q_blocks[C.ring][0:rows], g, b, SEQ),
                                      start=True, stop=True).then_inc(scoresT_mm, 1)
                        if n >= 2 and live(C):
                            b, g = divmod(n - 2, 4)
                            pe.wait_ge(probs_ready, C.count(8, n - 1))
                            if g == 0:
                                need(pe, attended_ready, C.count(2, b))
                                need(pe, logden_ready, C.count(2, b))
                            rows_g = slice(32 * g, 32 * g + 32)
                            pe.matmul(out_ps[rows_g, :], v_sb[:keys, C.ring, b, rows_g], probs[:keys, g, :], start=True, stop=True, tile_position=(0, 32 * g))
                            ones = den_w[:keys, C.ring, b, :] if weighted else const["ones"][:keys, 0:32]
                            pe.matmul(den_ps[rows_g, :], ones, probs[:keys, g, :], start=True, stop=True, tile_position=(0, 32 * g)).then_inc(values_mm, 1)
                        if n == 8 and live(C):
                            project_out(C, 0, t)

                def before_loop():
                    take_bank(uses[0][0], Step(0, 5))
                    take_bank(uses[1][0], Step(0, 5))

                run_steps(pe, step, before_loop)


GF = 4
TOK = GF * SEQ


class ExpertPhase:

    def __init__(self, nc, ctx, tag):
        self.nc, self.ctx, self.tag, self.steps_n = nc, ctx, tag, BATCH // GF
        self.sem = Semaphores(nc, ctx, tag)

    def sb(self, name, shape, dt=F32):
        return self.ctx.enter_context(self.nc.sbuf_tensor(f"{self.tag}_{name}", shape, dt))

    def live(self, s):
        return not s.static or 0 <= s.off < self.steps_n

    def run_steps(self, eng, body):
        lead = 3
        for t in range(lead):
            body(Step(0, t))
        with eng.Fori(0, (self.steps_n - 1 - lead) // 2) as i:
            for u in range(2):
                body(Step(i, lead + u))
        for t in range(self.steps_n - 1, self.steps_n + 2):
            body(Step(0, t))


def experts_phase(nc, x_sb, const, ins):
    NH, NE, D, I = 8, 16, 16, 64
    with ExitStack() as ctx:
        ph = ExpertPhase(nc, ctx, "f0")
        sb, sem, live = ph.sb, ph.sem, ph.live
        wm, bm = sb("wm", [128, EMB]), sb("bm", [128, 1])
        emb = sb("emb", [128, NH * NE])
        w1_raw, w1_hi, w1 = sb("w1_raw", [96, NE * I]), sb("w1_hi", [96, NE * I], F32R), sb("w1", [96, NE * I], F32R)
        b1 = sb("b1", [128, NE // 2])
        w2, b2 = sb("w2", [128, NE // 2, 32]), sb("b2", [128, 2])
        wo, bo = sb("wo", [128, EMB]), sb("bo", [128, EMB])
        spread = sb("spread", [128, 16, 128], F32R)
        gather = sb("gather", [128, 2, 32])
        rank = sb("rank", [128, NE])
        stats, mv = sb("stats", [128, 2, GF, 6]), sb("mv", [128, 2, GF, 2])
        logvar, rstd = sb("logvar", [128, 2, GF]), sb("rstd", [128, 2, GF])
        xn, lnT = sb("xn", [128, GF, EMB]), sb("lnT", [128, TOK])
        hT, h_parts = sb("hT", [128, TOK]), sb("h_parts", [128, 2, TOK], F32R)
        h_stack = [sb(f"h_stack{r}", [96, NH, TOK], F32R) for r in range(2)]
        top = sb("top", [128, 6, GF * NH])
        shifted, expd = sb("shifted", [128, TOK]), sb("expd", [128, TOK])
        first, second, keyed = sb("first", [128, TOK]), sb("second", [128, TOK]), sb("keyed", [128, TOK])
        chosen = sb("chosen", [128, TOK])
        wT = sb("wT", [128, 2, 2, TOK], F32R)
        act_out = sb("act_out", [128, 4, TOK])
        spread_sb = sb("spread_sb", [128, 2, TOK])
        prod = sb("prod", [128, 2, TOK])
        combT = sb("combT", [128, TOK])
        banks = [ctx.enter_context(nc.psum_tensor(f"f0_bank{n}", [128, 512], F32)) for n in range(7)]
        hid_ps, exp_ps, spread_ps, comb_ps, misc = banks[0:2], banks[2:4], banks[4], banks[5], banks[6]

        stack_free = sem("stack_free")
        stats_seen, loaded, zeroed, w1_split, prepared = sem("stats_seen"), sem("loaded"), sem("zeroed"), sem("w1_split"), sem("prepared")
        stats_done, mv_done, logvar_done, rstd_done, xn_done, x_biased = (sem(n) for n in (
            "stats_done", "mv_done", "logvar_done", "rstd_done", "xn_done", "x_biased"))
        xnT_mm, lnT_ready, h_mm, hT_ready, hhi_ready, hlo_ready = (sem(n) for n in (
            "xnT_mm", "lnT_ready", "h_mm", "hT_ready", "hhi_ready", "hlo_ready"))
        stacked = [sem(f"stacked{r}") for r in range(2)]
        logits_mm, shifted_ready, expd_ready, route_seq, first_ready, sum_ready = (sem(n) for n in (
            "logits_mm", "shifted_ready", "expd_ready", "route_seq", "first_ready", "sum_ready"))
        second_ready, pool_seq, chosen_ready, wT_mm, whi_ready, wT_ready = (sem(n) for n in (
            "second_ready", "pool_seq", "chosen_ready", "wT_mm", "whi_ready", "wT_ready"))
        hid_mm, act_ready, exp_mm, spread_mm, spread_ready, prod_ready, comb_mm, comb_ready, y_mm, y_added = (sem(n) for n in (
            "hid_mm", "act_ready", "exp_mm", "spread_mm", "spread_ready", "prod_ready", "comb_mm", "comb_ready", "y_mm", "y_added"))
        sums_done = sem("sums_done")
        N_LOADS = 13

        def act_out_of(s, n):
            return act_out[:, n % 4, :]

        def grp(ap):
            return ap.rearrange("p (q e) -> p q e", e=NE)

        def per_head(n):
            return top[:, n, :].unsqueeze(2).broadcast_to([128, GF * NH, NE])

        def blk(s, k):
            return (s, k) if k >= 0 else (s.back(1), k + 16)

        with nc.Block() as block:
            @block.sync
            def _(sp):
                for dst, name in ((wm, "wm"), (bm, "bm"), (emb, "emb"), (b1, "b1"), (w2, "w2"), (b2, "b2"), (wo, "wo"), (gather, "gather")):
                    sp.dma_start(dst[:], ins[f"f0_{name}"]).then_inc(loaded, 16)
                sp.dma_start(bo[:], ins["f0_bo"].broadcast_to([128, EMB])).then_inc(loaded, 16)
                sp.dma_start(rank[:], ins["f0_rank"].broadcast_to([128, NE])).then_inc(loaded, 16)
                sp.wait_ge(zeroed, 1)
                for rep in range(3):
                    sp.dma_start(w1_raw[32 * rep:32 * rep + D, :], ins["f0_w1"]).then_inc(loaded, 16)

                def step(t):
                    if live(t):
                        need(sp, hid_mm, t.back(1).count(64, 0))
                        sp.sem_inc(stack_free, 1)
                        sp.wait_ge(hlo_ready, t.count(1, 1))
                        for rep, part in enumerate((0, 1, 0)):
                            sp.dma_start(raw_words(h_stack[t.ring][32 * rep:32 * rep + D, :, :]), raw_words(h_parts[:, part, :])) \
                                .then_inc(stacked[t.ring], 16)

                ph.run_steps(sp, step)

            @block.gpsimd
            def _(pool):
                pool.memset(w1_raw[:], 0.0).then_inc(zeroed, 1)
                for r in range(2):
                    pool.memset(h_stack[r][:].bitcast(F32), 0.0).then_inc(zeroed, 1)
                pool.wait_ge(zeroed, 3)
                pool.wait_ge(loaded, 16 * N_LOADS)
                pool.sem_inc(prepared, 1)

                def step(t):
                    if not live(t):
                        return
                    pool.wait_ge(xn_done, t.count(1, 1))
                    pool.tensor_tensor(x_sb[:, t.ds(GF), :], x_sb[:, t.ds(GF), :],
                                       bo[:].unsqueeze(1).broadcast_to([128, GF, EMB]), ALU.add).then_inc(x_biased, 1)
                    pool.wait_ge(second_ready, t.count(1, 1))
                    need(pool, wT_mm, t.count(1, 0))
                    pool.tensor_tensor(chosen[:], first[:], second[:], ALU.add).then_inc(pool_seq, 1)
                    pool.wait_ge(pool_seq, t.count(3, 1))
                    pool.wait_ge(expd_ready, t.count(1, 1))
                    pool.tensor_tensor(chosen[:], chosen[:], expd[:], ALU.mult).then_inc(pool_seq, 1)
                    pool.wait_ge(pool_seq, t.count(3, 2))
                    pool.wait_ge(sum_ready, t.count(1, 1))
                    pool.tensor_tensor(grp(chosen[:]), grp(chosen[:]), per_head(2), ALU.mult).then_inc(pool_seq, 1)

                ph.run_steps(pool, step)

            @block.scalar
            def _(act):
                act.wait_ge(prepared, 1)

                def rstd_of(s):
                    act.wait_ge(mv_done, s.count(1, 1))
                    act.activation(logvar[:, s.ring, :], mv[:, s.ring, :, 1], ACT.Ln, bias=const["eps_ln"][:]).then_inc(logvar_done, 1)
                    act.wait_ge(logvar_done, s.count(1, 1))
                    act.activation(rstd[:, s.ring, :], logvar[:, s.ring, :], ACT.Exp, scale=-0.5).then_inc(rstd_done, 1)

                act.preload_act_table_set("natural_log_exp_and_others")
                rstd_of(Step(0, 0))

                def step(t):
                    M = t.back(1)
                    for k in range(16):
                        if live(t) and k == 4:
                            act.wait_ge(xnT_mm, t.count(1, 1))
                            act.activation(lnT[:], misc[:], ACT.Copy).then_inc(lnT_ready, 1)
                        if live(t) and k == 6:
                            act.wait_ge(h_mm, t.count(1, 1))
                            need(act, stacked[t.back(1).ring], (t.back(1).half(48, 1)) if not t.static or t.off > 0 else 0)
                            act.activation(h_parts[:, 0, :], misc[:], ACT.Identity, bias=bm[:]).then_inc(hhi_ready, 1)
                            act.activation(hT[:], misc[:], ACT.Identity, bias=bm[:]).then_inc(hT_ready, 1)
                        if k == 9 and (live(t) or live(t.back(-1))):
                            act.preload_act_table_set("natural_log_exp_and_others")
                            if live(t):
                                act.wait_ge(shifted_ready, t.count(1, 1))
                                act.activation(expd[:], shifted[:], ACT.Exp).then_inc(expd_ready, 1)
                            if live(t.back(-1)):
                                rstd_of(t.back(-1))
                            act.preload_act_table(ACT.Gelu)
                        if live(t) and k == 15:
                            act.wait_ge(wT_mm, t.count(1, 1))
                            act.activation(wT[:, t.ring, 0, :], misc[:], ACT.Copy).then_inc(whi_ready, 1)
                        if live(M):
                            for p in range(4):
                                n = 4 * k + p
                                act.wait_ge(hid_mm, M.count(64, n + 1))
                                need(act, exp_mm, M.count(64, n - 3))
                                act.activation(act_out_of(M, n), hid_ps[n % 2][:], ACT.Gelu,
                                               bias=b1[:, n % 8:n % 8 + 1]).then_inc(act_ready, 1)

                ph.run_steps(act, step)

            @block.vector
            def _(dve):
                dve.wait_ge(prepared, 1)
                dve.tensor_copy(spread[:].rearrange("p a (e o) -> p (a e) o", o=16), const["ident"][:].unsqueeze(2).broadcast_to([128, 128, 16]))
                dve.tensor_copy(w1_hi[:], w1_raw[:]).then_inc(w1_split, 1)
                dve.wait_ge(w1_split, 1)
                dve.tensor_copy(w1[0:64, :], w1_hi[0:64, :])
                dve.tensor_tensor(w1[64:96, :], w1_raw[64:96, :], w1_hi[64:96, :], ALU.subtract).then_inc(prepared, 1)

                def row_block(s, b):
                    return x_sb[:, s.ds1(GF, b), :].rearrange("p a e -> p (a e)")

                def stats_of(s):
                    for b in range(GF):
                        dve.bn_stats(stats[:, s.ring, b, :], row_block(s, b)).then_inc(stats_done, 1)
                    dve.wait_ge(stats_done, s.count(GF, GF))
                    dve.sem_inc(stats_seen, 1)
                    for b in range(GF):
                        last = dve.bn_aggr(mv[:, s.ring, b, :], stats[:, s.ring, b, :])
                    last.then_inc(mv_done, 1)

                def normalise(s):
                    dve.wait_ge(rstd_done, s.count(1, 1))
                    dve.wait_ge(mv_done, s.count(1, 1))
                    need(dve, xnT_mm, s.count(1, 0))
                    for b in range(GF):
                        last = dve.tensor_scalar(xn[:, b, :], row_block(s, b), mv[:, s.ring, b, 0:1], rstd[:, s.ring, b:b + 1], ALU.subtract, ALU.mult)
                    last.then_inc(xn_done, 1)

                stats_of(Step(0, 0))
                normalise(Step(0, 0))

                SEQ_N = 9

                def link(ins_, s, n):
                    ins_.then_inc(route_seq, 1)
                    dve.wait_ge(route_seq, s.count(SEQ_N, n))

                def weigh(s, k):
                    dve.wait_ge(exp_mm, s.count(64, 4 * k + 4))
                    dve.wait_ge(spread_ready, s.count(16, k + 1))
                    need(dve, comb_mm, s.count(16, k - 1))
                    dve.scalar_tensor_tensor(out=prod[:, k % 2, :], in0=exp_ps[k % 2][:], scalar=b2[:, k % 2:k % 2 + 1], in1=spread_sb[:, k % 2, :],
                                             op0=ALU.add, op1=ALU.mult).then_inc(prod_ready, 1)

                def step(t):
                    M, O = t.back(1), t.back(2)
                    for k in range(16):
                        if live(M):
                            dve.wait_ge(spread_mm, M.count(16, k + 1))
                            need(dve, prod_ready, M.count(16, k - 1))
                            dve.tensor_copy(spread_sb[:, k % 2, :], spread_ps[:]).then_inc(spread_ready, 1)
                        s, kb = blk(M, k - 1)
                        if live(s):
                            weigh(s, kb)
                        if k == 2 and live(O):
                            dve.wait_ge(comb_mm, O.count(16, 16))
                            need(dve, y_mm, O.count(1, 0))
                            dve.tensor_copy(combT[:], comb_ps[:]).then_inc(comb_ready, 1)
                        if k == 6 and live(t):
                            dve.wait_ge(hhi_ready, t.count(1, 1))
                            dve.wait_ge(hT_ready, t.count(1, 1))
                            need(dve, stacked[t.back(1).ring], (t.back(1).half(48, 1)) if not t.static or t.off > 0 else 0)
                            dve.tensor_tensor(h_parts[:, 1, :], hT[:], h_parts[:, 0, :], ALU.subtract).then_inc(hlo_ready, 1)
                        if k == 7 and live(t.back(-1)):
                            stats_of(t.back(-1))
                        if k == 8 and live(t):
                            dve.wait_ge(logits_mm, t.count(1, 1))
                            need(dve, pool_seq, t.count(3, 0))
                            link(dve.tensor_reduce(out=top[:, 0, :], in_=grp(misc[:]), axis=AX.X, op=ALU.max), t, 1)
                            dve.tensor_tensor(grp(shifted[:]), grp(misc[:]), per_head(0), ALU.subtract).then_inc(shifted_ready, 1)
                            dve.wait_ge(shifted_ready, t.count(1, 1))
                            link(dve.scalar_tensor_tensor(out=grp(keyed[:]), in0=grp(shifted[:]), scalar=0.0,
                                                          in1=rank[:].unsqueeze(1).broadcast_to([128, GF * NH, NE]), op0=ALU.is_equal, op1=ALU.mult), t, 2)
                        if k == 9 and live(t):
                            link(dve.tensor_reduce(out=top[:, 3, :], in_=grp(keyed[:]), axis=AX.X, op=ALU.max), t, 3)
                            link(dve.tensor_tensor(grp(first[:]), grp(keyed[:]), per_head(3), ALU.is_equal), t, 4)
                        if k == 10 and live(t):
                            dve.wait_ge(expd_ready, t.count(1, 1))
                            link(dve.scalar_tensor_tensor(out=shifted[:], in0=first[:], scalar=-3.0e38, in1=shifted[:], op0=ALU.mult, op1=ALU.add), t, 5)
                            link(dve.tensor_reduce(out=top[:, 4, :], in_=grp(shifted[:]), axis=AX.X, op=ALU.max), t, 6)
                        if k == 11 and live(t):
                            link(dve.tensor_tensor(grp(second[:]), grp(shifted[:]), per_head(4), ALU.is_equal), t, 7)
                            link(dve.tensor_tensor(grp(keyed[:]), grp(second[:]), rank[:].unsqueeze(1).broadcast_to([128, GF * NH, NE]), ALU.mult), t, 8)
                        if k == 12 and live(t):
                            link(dve.tensor_reduce(out=top[:, 5, :], in_=grp(keyed[:]), axis=AX.X, op=ALU.max), t, 9)
                            dve.tensor_tensor(grp(second[:]), grp(keyed[:]), per_head(5), ALU.is_equal).then_inc(second_ready, 1)
                            dve.tensor_reduce(out=top[:, 1, :], in_=grp(expd[:]), axis=AX.X, op=ALU.add).then_inc(sums_done, 1)
                            dve.wait_ge(sums_done, t.count(1, 1))
                            dve.reciprocal(top[:, 2, :], top[:, 1, :]).then_inc(sum_ready, 1)
                        if k == 10 and live(t.back(-1)):
                            normalise(t.back(-1))
                        if k == 13 and live(O):
                            dve.wait_ge(y_mm, O.count(1, 1))
                            dve.wait_ge(x_biased, O.count(1, 1))
                            xs = x_sb[:, O.ds(GF), :].rearrange("p b e -> p (b e)")
                            dve.tensor_tensor(xs, misc[:], xs, ALU.add).then_inc(y_added, 1)
                        if k == 15 and live(t):
                            dve.wait_ge(whi_ready, t.count(1, 1))
                            dve.tensor_tensor(wT[:, t.ring, 1, :], misc[:], wT[:, t.ring, 0, :], ALU.subtract).then_inc(wT_ready, 1)

                ph.run_steps(dve, step)

            @block.tensor
            def _(pe):
                pe.wait_ge(prepared, 2)

                def second_layer(s, n):
                    k, q = n // 4, n % 4
                    pe.wait_ge(act_ready, s.count(64, n + 1))
                    if q == 0:
                        need(pe, prod_ready, s.count(16, k - 1))
                    pe.matmul(exp_ps[k % 2][32 * q:32 * q + 32, :], w2[:, n % 8, :], act_out_of(s, n), start=True, stop=True,
                              tile_position=(0, 32 * q)).then_inc(exp_mm, 1)

                def combine(s, k):
                    j = k // 2
                    pe.wait_ge(prod_ready, s.count(16, k + 1))
                    if k == 0:
                        need(pe, comb_ready, s.count(1, 0))
                    q = j // 2
                    pe.matmul(comb_ps[32 * q:32 * q + 32, :], gather[:, j % 2, :], prod[:, k % 2, :], start=(k % 4 == 0), stop=(k % 4 == 3),
                              tile_position=(0, 32 * q)).then_inc(comb_mm, 1)

                def step(t):
                    M, O = t.back(1), t.back(2)
                    for k in range(16):
                        if k == 3 and live(t):
                            pe.wait_ge(xn_done, t.count(1, 1))
                            need(pe, wT_ready, t.count(1, 0))
                            for b in range(GF):
                                last = pe.transpose(misc[:, b * SEQ:(b + 1) * SEQ], xn[:, b, :], const["ident"][:])
                            last.then_inc(xnT_mm, 1)
                        if k == 5 and live(t):
                            pe.wait_ge(lnT_ready, t.count(1, 1))
                            pe.matmul(misc[:], wm[:], lnT[:], start=True, stop=True).then_inc(h_mm, 1)
                        if k == 7 and live(t):
                            pe.wait_ge(hT_ready, t.count(1, 1))
                            for b in range(GF):
                                last = pe.matmul(misc[:, b * SEQ:(b + 1) * SEQ], hT[:, b * SEQ:(b + 1) * SEQ], emb[:], start=True, stop=True)
                            last.then_inc(logits_mm, 1)
                        if k == 11 and live(O):
                            pe.wait_ge(comb_ready, O.count(1, 1))
                            if live(t):
                                pe.wait_ge(shifted_ready, t.count(1, 1))
                            elif t.static:
                                need(pe, wT_ready, ph.steps_n)
                            need(pe, y_added, O.count(1, 0))
                            for b in range(GF):
                                last = pe.matmul(misc[:, b * EMB:(b + 1) * EMB], combT[:, b * SEQ:(b + 1) * SEQ], wo[:], start=True, stop=True)
                            last.then_inc(y_mm, 1)
                        if k == 14 and live(t):
                            pe.wait_ge(pool_seq, t.count(3, 3))
                            pe.wait_ge(shifted_ready, t.count(1, 1))
                            if live(O):
                                need(pe, y_added, O.count(1, 1))
                            for b in range(GF):
                                last = pe.transpose(misc[:, b * SEQ:(b + 1) * SEQ], chosen[:, b * SEQ:(b + 1) * SEQ], const["ident"][:])
                            last.then_inc(wT_mm, 1)
                        if live(M):
                            if k == 0:
                                pe.wait_ge(stacked[M.ring], M.half(48, 1))
                                pe.wait_ge(wT_ready, M.count(1, 1))
                            need(pe, spread_ready, M.count(16, k))
                            for part in range(2):
                                last = pe.matmul(spread_ps[:], spread[:, k, :], wT[:, M.ring, part, :], start=(part == 0), stop=(part == 1))
                            last.then_inc(spread_mm, 1)
                        for p in range(4):
                            n = 4 * k + p
                            if live(M):
                                need(pe, act_ready, M.count(64, n - 1))
                                pe.matmul(hid_ps[n % 2][:], w1[:, 128 * (n % 8):128 * (n % 8) + 128], h_stack[M.ring][:, n // 8, :],
                                          start=True, stop=True).then_inc(hid_mm, 1)
                            s, before = (M, n - 2) if n >= 2 else (M.back(1), n + 62)
                            if live(s):
                                second_layer(s, before)
                        s, kb = blk(M, k - 2)
                        if live(s):
                            combine(s, kb)

                ph.run_steps(pe, step)


def mixture_phase(nc, x_sb, const, ins):
    NE, HID = 8, 256
    with ExitStack() as ctx:
        ph = ExpertPhase(nc, ctx, "f1")
        sb, sem, live = ph.sb, ph.sem, ph.live
        w_raw, w_hi, w_lo = sb("w_raw", [128, NE * 2 * HID]), sb("w_hi", [128, NE * 2 * HID], F32R), sb("w_lo", [128, NE * 2 * HID], F32R)
        wd, wr, norm_scale = sb("wd", [128, NE, 2, EMB]), sb("wr", [128, NE]), sb("norm_scale", [128, 1])
        rank = sb("rank", [128, NE])
        eps_both = sb("eps_both", [128, 1])
        stats, mv = sb("stats", [128, 2, GF, 6]), sb("mv", [128, 2, GF, 2])
        logvar, rstd = sb("logvar", [128, 2, 2, GF]), sb("rstd", [128, 2, 2, GF])
        xn, xr = sb("xn", [128, GF, EMB]), sb("xr", [128, GF, EMB])
        xT, x_hi, x_lo = sb("xT", [128, TOK]), sb("x_hi", [128, 2, TOK], F32R), sb("x_lo", [128, 2, TOK], F32R)
        shifted, keyed = (sb(n, [128, GF * NE]) for n in ("shifted", "keyed"))
        first, second, chosen = (sb(n, [128, GF * NE]) for n in ("first", "second", "chosen"))
        weights = sb("weights", [128, 2, GF * NE])
        top = sb("top", [128, 7, GF])
        silu, h = sb("silu", [128, 2, TOK]), sb("h", [128, 4, TOK])
        banks = [ctx.enter_context(nc.psum_tensor(f"f1_bank{n}", [128, 512], F32)) for n in range(7)]
        gate_ps, u_ps, y_ps, misc = banks[0:2], banks[2:4], banks[4:6], banks[6]

        stats_seen, loaded, prepared, w_split, rest_seq = sem("stats_seen"), sem("loaded"), sem("prepared"), sem("w_split"), sem("rest_seq")
        stats_done, mv_done, logvar_done, rstd_done, xn_done, xr_done, skip_added = (sem(n) for n in (
            "stats_done", "mv_done", "logvar_done", "rstd_done", "xn_done", "xr_done", "skip_added"))
        xr_transposed, xT_ready, xhi_ready, xlo_ready, logits_mm, route_seq, second_exp, weights_ready = (sem(n) for n in (
            "xr_transposed", "xT_ready", "xhi_ready", "xlo_ready", "logits_mm", "route_seq", "second_exp", "weights_ready"))
        gate_mm, u_mm, silu_ready, h_ready, down_mm, y_added = (sem(n) for n in (
            "gate_mm", "u_mm", "silu_ready", "h_ready", "down_mm", "y_added"))

        def grp(ap):
            return ap.rearrange("p (b e) -> p b e", e=NE)

        def per_token(n):
            return top[:, n, :].unsqueeze(2).broadcast_to([128, GF, NE])

        with nc.Block() as block:
            @block.sync
            def _(sp):
                for dst, name in ((w_raw, "w_up"), (wd, "wd"), (wr, "wr"), (norm_scale, "norm_scale")):
                    sp.dma_start(dst[:], ins[f"f1_{name}"]).then_inc(loaded, 16)
                sp.dma_start(rank[:], ins["f1_rank"].broadcast_to([128, NE])).then_inc(loaded, 16)

            @block.gpsimd
            def _(pool):
                pool.memset(eps_both[:], 1e-5 * 1e-6).then_inc(prepared, 1)
                pool.wait_ge(loaded, 16 * 5)
                pool.sem_inc(prepared, 1)

                def step(t):
                    if live(t):
                        pool.wait_ge(xn_done, t.count(1, 1))
                        pool.wait_ge(xr_done, t.count(1, 1))
                        pool.tensor_tensor(x_sb[:, t.ds(GF), :], x_sb[:, t.ds(GF), :], xn[:], ALU.add).then_inc(skip_added, 1)

                ph.run_steps(pool, step)

            @block.scalar
            def _(act):
                act.wait_ge(prepared, 2)

                def rstd_of(s):
                    act.wait_ge(mv_done, s.count(1, 1))
                    act.activation(logvar[:, s.ring, 0, :], mv[:, s.ring, :, 1], ACT.Ln, bias=const["eps_ln"][:])
                    act.activation(logvar[:, s.ring, 1, :], mv[:, s.ring, :, 1], ACT.Ln, bias=eps_both[:], scale=1.0 + 1e-6).then_inc(logvar_done, 1)
                    act.wait_ge(logvar_done, s.count(1, 1))
                    act.activation(rstd[:, s.ring, :, :], logvar[:, s.ring, :, :], ACT.Exp, scale=-0.5).then_inc(rstd_done, 1)

                act.preload_act_table_set("natural_log_exp_and_others")
                rstd_of(Step(0, 0))

                def step(t):
                    M = t.back(1)
                    for k in range(NE):
                        if k == 1 and live(t):
                            act.wait_ge(xr_transposed, t.count(1, 1))
                            need(act, logits_mm, t.count(1, 0))
                            act.activation(x_hi[:, t.ring, :], misc[:], ACT.Identity, scale=norm_scale[:]).then_inc(xhi_ready, 1)
                            act.activation(xT[:], misc[:], ACT.Identity, scale=norm_scale[:]).then_inc(xT_ready, 1)
                        if k == 5 and (live(t) or live(t.back(-1))):
                            act.preload_act_table_set("natural_log_exp_and_others")
                            if live(t):
                                act.wait_ge(route_seq, t.count(8, 6))
                                act.activation(top[:, 4, :], top[:, 2, :], ACT.Exp).then_inc(second_exp, 1)
                            if live(t.back(-1)):
                                rstd_of(t.back(-1))
                            act.preload_act_table(ACT.Silu)
                        if live(M):
                            for n in (2 * k, 2 * k + 1):
                                act.wait_ge(gate_mm, M.count(16, n + 1))
                                need(act, h_ready, M.count(16, n - 1))
                                act.activation(silu[:, n % 2, :], gate_ps[n % 2][:], ACT.Silu).then_inc(silu_ready, 1)

                ph.run_steps(act, step)

            @block.vector
            def _(dve):
                dve.wait_ge(prepared, 2)
                dve.tensor_copy(w_hi[:], w_raw[:]).then_inc(w_split, 1)
                dve.wait_ge(w_split, 1)
                dve.tensor_tensor(w_lo[:], w_raw[:], w_hi[:], ALU.subtract).then_inc(prepared, 1)

                def row_block(s, b):
                    return x_sb[:, s.ds1(GF, b), :].rearrange("p a e -> p (a e)")

                def stats_of(s):
                    for b in range(GF):
                        dve.bn_stats(stats[:, s.ring, b, :], row_block(s, b)).then_inc(stats_done, 1)
                    dve.wait_ge(stats_done, s.count(GF, GF))
                    dve.sem_inc(stats_seen, 1)
                    for b in range(GF):
                        last = dve.bn_aggr(mv[:, s.ring, b, :], stats[:, s.ring, b, :])
                    last.then_inc(mv_done, 1)

                def normalise(s):
                    dve.wait_ge(rstd_done, s.count(1, 1))
                    dve.wait_ge(mv_done, s.count(1, 1))
                    need(dve, skip_added, s.count(1, 0))
                    need(dve, xr_transposed, s.count(1, 0))
                    for dst, which, done in ((xr, 1, xr_done), (xn, 0, xn_done)):
                        for b in range(GF):
                            last = dve.tensor_scalar(dst[:, b, :], row_block(s, b), mv[:, s.ring, b, 0:1], rstd[:, s.ring, which, b:b + 1],
                                                     ALU.subtract, ALU.mult)
                        last.then_inc(done, 1)

                def link(op, s, n):
                    op.then_inc(route_seq, 1)
                    dve.wait_ge(route_seq, s.count(8, n))

                def choose_first(t):
                    dve.wait_ge(logits_mm, t.count(1, 1))
                    link(dve.tensor_reduce(out=top[:, 0, :], in_=grp(misc[:, :GF * NE]), axis=AX.X, op=ALU.max), t, 1)
                    link(dve.tensor_tensor(grp(shifted[:]), grp(misc[:, :GF * NE]), per_token(0), ALU.subtract), t, 2)
                    link(dve.scalar_tensor_tensor(out=grp(keyed[:]), in0=grp(shifted[:]), scalar=0.0,
                                                  in1=rank[:].unsqueeze(1).broadcast_to([128, GF, NE]), op0=ALU.is_equal, op1=ALU.mult), t, 3)
                    link(dve.tensor_reduce(out=top[:, 1, :], in_=grp(keyed[:]), axis=AX.X, op=ALU.max), t, 4)
                    link(dve.tensor_tensor(grp(first[:]), grp(keyed[:]), per_token(1), ALU.is_equal), t, 5)

                def choose_second(t):
                    dve.scalar_tensor_tensor(out=shifted[:], in0=first[:], scalar=-3.0e38, in1=shifted[:], op0=ALU.mult, op1=ALU.add).then_inc(rest_seq, 1)
                    dve.wait_ge(rest_seq, t.count(3, 1))
                    link(dve.tensor_reduce(out=top[:, 2, :], in_=grp(shifted[:]), axis=AX.X, op=ALU.max), t, 6)
                    dve.tensor_tensor(grp(second[:]), grp(shifted[:]), per_token(2), ALU.is_equal).then_inc(rest_seq, 1)
                    dve.wait_ge(rest_seq, t.count(3, 2))
                    dve.tensor_tensor(grp(keyed[:]), grp(second[:]), rank[:].unsqueeze(1).broadcast_to([128, GF, NE]), ALU.mult).then_inc(rest_seq, 1)
                    dve.wait_ge(rest_seq, t.count(3, 3))
                    link(dve.tensor_reduce(out=top[:, 3, :], in_=grp(keyed[:]), axis=AX.X, op=ALU.max), t, 7)
                    link(dve.tensor_tensor(grp(second[:]), grp(keyed[:]), per_token(3), ALU.is_equal), t, 8)

                def weigh_chosen(t):
                    dve.wait_ge(second_exp, t.count(1, 1))
                    dve.tensor_scalar(top[:, 5, :], top[:, 4, :], 1.0, None, ALU.add)
                    dve.tensor_tensor(grp(chosen[:]), grp(second[:]), per_token(4), ALU.mult).then_inc(weights_ready, 1)
                    dve.wait_ge(weights_ready, t.count(3, 1))
                    dve.reciprocal(top[:, 6, :], top[:, 5, :])
                    dve.tensor_tensor(chosen[:], chosen[:], first[:], ALU.add).then_inc(weights_ready, 1)
                    dve.wait_ge(weights_ready, t.count(3, 2))
                    dve.tensor_tensor(grp(weights[:, t.ring, :]), grp(chosen[:]), per_token(6), ALU.mult).then_inc(weights_ready, 1)

                stats_of(Step(0, 0))
                normalise(Step(0, 0))

                def mix(s, e):
                    dve.wait_ge(down_mm, s.count(NE, e + 1))
                    if e == 0:
                        dve.wait_ge(weights_ready, s.count(3, 3))
                        dve.wait_ge(skip_added, s.count(1, 1))
                    else:
                        dve.wait_ge(y_added, s.count(NE, e))
                    for b in range(GF):
                        last = dve.scalar_tensor_tensor(out=row_block(s, b), in0=y_ps[e % 2][:, b * EMB:(b + 1) * EMB],
                                                        scalar=weights[:, s.ring, b * NE + e:b * NE + e + 1], in1=row_block(s, b),
                                                        op0=ALU.mult, op1=ALU.add)
                    last.then_inc(y_added, 1)

                def step(t):
                    M = t.back(1)
                    for k in range(NE):
                        for n in (2 * k, 2 * k + 1):
                            if live(M):
                                dve.wait_ge(silu_ready, M.count(16, n + 1))
                                dve.wait_ge(u_mm, M.count(16, n + 1))
                                need(dve, down_mm, M.count(NE, k - 1))
                                dve.tensor_tensor(h[:, n % 4, :], u_ps[n % 2][:], silu[:, n % 2, :], ALU.mult).then_inc(h_ready, 1)
                        if k == 1 and live(t):
                            dve.wait_ge(xT_ready, t.count(1, 1))
                            dve.wait_ge(xhi_ready, t.count(1, 1))
                            dve.tensor_tensor(x_lo[:, t.ring, :], xT[:], x_hi[:, t.ring, :], ALU.subtract).then_inc(xlo_ready, 1)
                        if k == 3 and live(t):
                            choose_first(t)
                        if k == 4 and live(t):
                            choose_second(t)
                        if k == 4 and live(t.back(-1)):
                            stats_of(t.back(-1))
                        if k == 6 and live(t):
                            weigh_chosen(t)
                        if k == 6 and live(t.back(-1)):
                            normalise(t.back(-1))
                        s, e = (M, k - 1) if k > 0 else (M.back(1), NE - 1)
                        if live(s):
                            mix(s, e)

                ph.run_steps(dve, step)

            @block.tensor
            def _(pe):
                pe.wait_ge(prepared, 3)

                def up(ps, s, col):
                    x_h, x_l = x_hi[:, s.ring, :], x_lo[:, s.ring, :]
                    pe.matmul(ps[:], w_hi[:, col:col + 128], x_h, start=True, stop=False)
                    pe.matmul(ps[:], w_hi[:, col:col + 128], x_l, start=False, stop=False)
                    return pe.matmul(ps[:], w_lo[:, col:col + 128], x_h, start=False, stop=True)

                def down(s, e):
                    pe.wait_ge(h_ready, s.count(16, 2 * e + 2))
                    need(pe, y_added, s.count(NE, e - 1))
                    for b in range(GF):
                        for c in range(2):
                            last = pe.matmul(y_ps[e % 2][:, b * EMB:(b + 1) * EMB], h[:, 2 * (e % 2) + c, b * SEQ:(b + 1) * SEQ], wd[:, e, c, :],
                                             start=(c == 0), stop=(c == 1))
                    last.then_inc(down_mm, 1)

                def step(t):
                    M = t.back(1)
                    for k in range(NE):
                        if k == 0 and live(t):
                            pe.wait_ge(xr_done, t.count(1, 1))
                            need(pe, route_seq, t.count(8, 0))
                            for b in range(GF):
                                last = pe.transpose(misc[:, b * SEQ:(b + 1) * SEQ], xr[:, b, :], const["ident"][:])
                            last.then_inc(xr_transposed, 1)
                        if k == 2 and live(t):
                            pe.wait_ge(xT_ready, t.count(1, 1))
                            pe.wait_ge(xhi_ready, t.count(1, 1))
                            for b in range(GF):
                                last = pe.matmul(misc[:, b * NE:(b + 1) * NE], xT[:, b * SEQ:(b + 1) * SEQ], wr[:], start=True, stop=True)
                            last.then_inc(logits_mm, 1)
                        if live(M):
                            if k == 0:
                                pe.wait_ge(xlo_ready, M.count(1, 1))
                            for c in range(2):
                                n = 2 * k + c
                                need(pe, silu_ready, M.count(16, n - 1))
                                up(gate_ps[n % 2], M, 2 * HID * k + HID + 128 * c).then_inc(gate_mm, 1)
                                need(pe, h_ready, M.count(16, n - 1))
                                up(u_ps[n % 2], M, 2 * HID * k + 128 * c).then_inc(u_mm, 1)
                        s, e = (M, k - 1) if k > 0 else (M.back(1), NE - 1)
                        if live(s):
                            down(s, e)

                ph.run_steps(pe, step)


def expert_layouts(a, np):
    d = {}
    heads_last = lambda w: np.ascontiguousarray(w.reshape(*w.shape[:-1], 8, 16).swapaxes(-1, -2).reshape(w.shape))
    d["f0_wm"], d["f0_bm"] = heads_last(a["L0_ffn_Wm"]), heads_last(a["L0_ffn_bm"]).reshape(128, 1)
    emb = np.zeros((16, 8, 8, 16), np.float32)
    for h in range(8):
        emb[:, h, h] = a["L0_ffn_expert_emb"]
    d["f0_emb"] = emb.reshape(128, 128)
    d["f0_w1"] = np.ascontiguousarray(a["L0_ffn_W1"].transpose(1, 0, 2).reshape(16, 1024))
    d["f0_b1"] = np.ascontiguousarray(a["L0_ffn_b1"].reshape(8, 128).T)
    w2 = np.zeros((8, 2, 64, 2, 16), np.float32)
    for e in range(2):
        w2[:, e, :, e] = a["L0_ffn_W2"].reshape(8, 2, 64, 16)[:, e]
    d["f0_w2"] = np.ascontiguousarray(w2.reshape(8, 128, 32).transpose(1, 0, 2))
    d["f0_b2"] = np.ascontiguousarray(a["L0_ffn_b2"].reshape(2, 128).T)
    d["f0_wo"], d["f0_bo"] = a["L0_ffn_Wo"], a["L0_ffn_bo"].reshape(1, 128)
    d["f0_rank"] = (16 - np.arange(16, dtype=np.float32)).reshape(1, 16)
    gather = np.zeros((8, 16, 2, 32), np.float32)
    for parity in range(2):
        for o in range(16):
            gather[:, o, parity, 16 * parity + o] = 1.0
    d["f0_gather"] = gather.reshape(128, 2, 32)
    d["f1_w_up"] = np.ascontiguousarray(a["L1_ffn_w_up"].transpose(2, 0, 1).reshape(128, 8 * 512))
    d["f1_wd"] = np.ascontiguousarray(a["L1_ffn_w_down"].transpose(0, 2, 1).reshape(8, 2, 128, 128).transpose(2, 0, 1, 3))
    d["f1_wr"], d["f1_norm_scale"] = np.ascontiguousarray(a["L1_ffn_w_router"].T), a["L1_ffn_norm_scale"].reshape(128, 1)
    d["f1_rank"] = (8 - np.arange(8, dtype=np.float32)).reshape(1, 8)
    return d


def setup_constants(nc, ctx, ins):
    def sb(name, shape, dt=F32):
        return ctx.enter_context(nc.sbuf_tensor(name, shape, dt))

    x_sb = sb("x_sb", [128, BATCH, EMB])
    const = {name: sb(f"const_{name}", shape) for name, shape in (
        ("ident", [128, 128]), ("ones", [128, 128]), ("causal", [128, 128]), ("eps_ln", [128, 1]), ("eps_den", [128, 1]),
        ("eps_rms", [128, 1]), ("zero", [128, 1]), ("abundance", [128, BATCH]))}
    made, loaded = ctx.enter_context(nc.semaphore("made")), ctx.enter_context(nc.semaphore("loaded"))
    with nc.Block() as block:
        @block.sync
        def _(sp):
            for part in range(4):
                n = BATCH // 4
                sp.dma_start(x_sb[:, part * n:(part + 1) * n, :], ins["x"][part * n:(part + 1) * n].rearrange("b s e -> s b e")).then_inc(loaded, 16)
            sp.dma_start(const["abundance"][:CTX, :], ins["abundance"]).then_inc(loaded, 16)
            sp.wait_ge(loaded, 16 * 5)

        @block.gpsimd
        def _(pool):
            pool.memset(const["ident"][:], 0.0).then_inc(made, 1)
            pool.memset(const["ones"][:], 1.0).then_inc(made, 1)
            pool.wait_ge(made, 2)
            pool.affine_select(out=const["ident"][:], in_=const["ident"][:], compare_op=ALU.not_equal, fill=1.0, base=0,
                               pattern=[[-1, 128]], channel_multiplier=1)
            pool.affine_select(out=const["causal"][:], in_=const["ones"][:], compare_op=ALU.is_ge, fill=0.0, base=0,
                               pattern=[[1, 128]], channel_multiplier=-1)

        @block.vector
        def _(dve):
            for name, value in (("eps_ln", 1e-5), ("eps_den", 1e-6), ("eps_rms", 1e-6), ("zero", 0.0)):
                dve.memset(const[name][:], value)
    return x_sb, const


def setup_stacks(nc, ctx, tag):
    def sb(name, shape):
        return ctx.enter_context(nc.sbuf_tensor(f"{tag}_{name}", shape, F32R))

    stacks = {
        "q_blocks": [sb(f"q_blocks{r}", [128, 4, 4 * G * SEQ]) for r in range(2)],
        "k_blocks": [sb(f"k_blocks{r}", [128, 4, 4 * G * SEQ]) for r in range(2)],
        "k_stack": [sb(f"k_stack{r}", [128, 4 * G * SEQ]) for r in range(2)],
        "q_hi": [sb(f"q_hi{r}", [128, 4 * G * SEQ]) for r in range(2)],
    }
    zeroed = Semaphores(nc, ctx, tag)("zeroed")
    with nc.Block() as block:
        @block.gpsimd
        def _(pool):
            for r in range(2):
                pool.memset(stacks["k_stack"][r][:].bitcast(F32), 0.0).then_inc(zeroed, 1)
                pool.memset(stacks["q_hi"][r][:].bitcast(F32), 0.0).then_inc(zeroed, 1)
                pool.memset(stacks["k_blocks"][r][:].bitcast(F32), 0.0).then_inc(zeroed, 1)
            pool.wait_ge(zeroed, 6)
            for r in range(2):
                pool.memset(stacks["k_stack"][r][96:97, :].bitcast(F32), 1.0)

        @block.vector
        def _(dve):
            for r in range(2):
                dve.memset(stacks["q_blocks"][r][:].bitcast(F32), 0.0)
    return stacks


def decoder(nc, ins, out, phases=ALL_PHASES):
    with ExitStack() as ctx:
        x_sb, const = setup_constants(nc, ctx, ins)

        def attention_pair(tag, pair):
            with ExitStack() as pair_ctx:
                pair = [(kind, p) for kind, p in pair if p in phases]
                stacks = setup_stacks(nc, pair_ctx, tag) if pair else None
                for kind, p in pair:
                    names = [k for k in ("wq", "wk", "wv", "wo", "bo", "bq", "bk", "bv", "cos", "sin") if f"{p}_{k}" in ins]
                    attention_phase(nc, kind, p, x_sb, const, stacks, {**{k: ins[f"{p}_{k}"] for k in names}, "ctx": ins["ctx"]})

        attention_pair("stacks0", (("linear", "a0"), ("cross", "c0")))
        if "f0" in phases:
            experts_phase(nc, x_sb, const, ins)
        attention_pair("stacks1", (("scrambled", "a1"), ("weighted", "c1")))
        if "f1" in phases:
            mixture_phase(nc, x_sb, const, ins)
        stored = ctx.enter_context(nc.semaphore("stored"))
        with nc.Block() as block:
            @block.sync
            def _(sp):
                for part in range(4):
                    n = BATCH // 4
                    sp.dma_start(out[part * n:(part + 1) * n].rearrange("b s e -> s b e"), x_sb[:, part * n:(part + 1) * n, :]).then_inc(stored, 16)
                sp.wait_ge(stored, 64)


def layouts(a):
    import numpy as np

    def headed(w):
        return np.ascontiguousarray(w.reshape(*w.shape[:-1], 4, 4, 8).transpose(*range(w.ndim - 1), w.ndim, w.ndim + 1, w.ndim - 1).reshape(w.shape))

    def dims_first(w):
        return np.ascontiguousarray(w.reshape(*w.shape[:-1], 16, 8).swapaxes(-1, -2).reshape(w.shape))

    def masked_out(wT):
        out = np.zeros((128, 4, 128), np.float32)
        for h in range(16):
            out[8 * h:8 * h + 8, h % 4] = wT[8 * h:8 * h + 8]
        return out

    row = lambda v: np.ascontiguousarray(v.reshape(1, -1))
    col = lambda v: np.ascontiguousarray(v.reshape(-1, 1))
    t = lambda w: np.ascontiguousarray(w.T)
    d = {"x": a["x"], "ctx": a["ctx_1024"], "abundance": t(a["fside_BxS2_0"])}
    d["a0_wq"], d["a0_wk"] = headed(t(a["L0_attn_Wq"])), headed(t(a["L0_attn_Wk"]))
    d["a0_wv"], d["a0_wo"], d["a0_bo"] = t(a["L0_attn_Wv"]), masked_out(t(a["L0_attn_Wp"])), row(a["L0_attn_bp"])
    w, b, wo, bo = a["L1_xattn_in_proj_weight"], a["L1_xattn_in_proj_bias"], a["L1_xattn_out_proj_weight"], a["L1_xattn_out_proj_bias"]
    for tag, (wq, wk, wv, wo, bq, bk, bv, bo) in {
        "c0": [a[f"L0_xattn_{n}"] for n in ("Wq", "Wk", "Wv", "Wo", "bq", "bk", "bv", "bo")],
        "c1": [w[:128], w[128:256], w[256:], wo, b[:128], b[128:256], b[256:], bo],
    }.items():
        d[f"{tag}_wq"], d[f"{tag}_wk"], d[f"{tag}_wv"] = headed(t(wq)), headed(t(wk)), t(wv)
        d[f"{tag}_wo"], d[f"{tag}_bo"], d[f"{tag}_bv"] = masked_out(t(wo)), row(bo), row(bv)
        d[f"{tag}_bq"], d[f"{tag}_bk"] = col(headed(bq)), col(headed(bk))
    for n in ("wq", "wk", "wv"):
        d[f"a1_{n}"] = dims_first(t(a[f"L1_attn_{n}"]))
    d["a1_wo"], d["a1_bo"] = masked_out(t(a["L1_attn_wo"])), row(a["L1_attn_bo"])
    d["a1_bq"], d["a1_bk"], d["a1_bv"] = row(dims_first(a["L1_attn_bq"])), row(dims_first(a["L1_attn_bk"])), col(dims_first(a["L1_attn_bv"]))
    d["a1_cos"], d["a1_sin"] = row(a["L1_attn_rot_cos"][SEQ]), row(a["L1_attn_rot_sin"][SEQ])
    d.update(expert_layouts(a, np))
    return d


def kernel(**inputs):
    import concourse.bacc as _bacc
    import numpy as _np
    from concourse.bass_utils import run_bass_kernel_spmd as _run

    nc = _bacc.Bacc("TRN2", target_bir_lowering=False, num_devices=1)
    arrays = layouts({name: _np.asarray(value) for name, value in inputs.items()})
    arrays = {f"in_{name}": _np.ascontiguousarray(a) for name, a in arrays.items()}
    args = {name[3:]: nc.dram_tensor(name, a.shape, mybir.dt.from_np(a.dtype), kind="ExternalInput").ap() for name, a in arrays.items()}
    out = nc.dram_tensor("out", (BATCH, SEQ, EMB), F32, kind="ExternalOutput").ap()
    decoder(nc, args, out)
    return _run(nc, [arrays], core_ids=[0]).results[0]["out"]
```

```python
import math
from contextlib import ExitStack

import concourse.bass as bass
from concourse import mybir

F32, F32R = mybir.dt.float32, mybir.dt.float32r
ACT = mybir.ActivationFunctionType
ALU = mybir.AluOpType
AX = mybir.AxisListType

BATCH, SEQ, EMB, CTX = 64, 128, 128, 120
HEADS, HD = 16, 8
G = 2


class Step:

    def __init__(self, i, off):
        self.i, self.off, self.static, self.ring = i, off, isinstance(i, int), off % 2

    def back(self, n):
        return Step(self.i, self.off - n)

    def count(self, per_step, plus):
        return self.i * (2 * per_step) + (self.off * per_step + plus)

    def half(self, per_use, uses=0):
        return self.i * per_use + (self.off // 2 + uses) * per_use

    def ds(self, n):
        return bass.ds(self.i * (2 * n) + self.off * n, n)

    def ds1(self, n, b):
        return bass.ds(self.i * (2 * n) + (self.off * n + b), 1)


def need(eng, sem, value):
    if not isinstance(value, int) or value > 0:
        eng.wait_ge(sem, value)


class Semaphores:

    def __init__(self, nc, ctx, tag):
        self.nc, self.tag, self.made = nc, tag, []
        ctx.callback(self.zero)

    def __call__(self, name):
        self.made.append(self.nc.alloc_semaphore(f"{self.tag}_{name}"))
        return self.made[-1]

    def zero(self):
        self.nc.all_engine_barrier()
        self.nc.clear_and_free_semaphores(self.made)
        self.nc.all_engine_barrier()


def raw_words(ap):
    return ap.bitcast(F32)


ALL_PHASES = ("a0", "c0", "f0", "a1", "c1", "f1")


def attention_phase(nc, kind, tag, x_sb, const, stacks, dram):
    cross = kind in ("cross", "weighted")
    linear, scrambled, weighted = kind == "linear", kind == "scrambled", kind == "weighted"
    keys = CTX if cross else SEQ
    kn, qn = G * keys, G * SEQ
    scale = 1.0 if linear else 1.0 / math.sqrt(EMB if kind == "cross" else HD)
    q_blocks, k_stack, q_hi, k_blocks = stacks["q_blocks"], stacks["k_stack"], stacks["q_hi"], stacks["k_blocks"]
    steps_n = BATCH // G
    uses = [("xnT", 0), ("y0", 3), ("q", 0), ("k", 0), ("v", 0)]
    if cross:
        uses = [("ctxT", 0)] + uses
    if scrambled:
        uses += [("vback", 1)]
    uses += [("y1", 3)]
    if not linear:
        uses += [("maxT", 1)]
    pos = {name: n for n, (name, _) in enumerate(uses)}
    n_max, n_sp, n_pool, n_shift = (4, 8, 4, 4) if scrambled else (5, 8, 7, 1)

    ctx = ExitStack()
    with ctx:
        def sb(name, shape, dt=F32):
            return ctx.enter_context(nc.sbuf_tensor(f"{tag}_{name}", shape, dt))

        sem = Semaphores(nc, ctx, tag)

        def sem2(name):
            return [sem(f"{name}{r}") for r in range(2)]

        wq, wk, wv = sb("wq", [128, EMB]), sb("wk", [128, EMB]), sb("wv", [128, EMB])
        wo, bo = sb("wo", [128, 4, EMB]), sb("bo", [128, EMB])
        bq, bk, bv = sb("bq", [128, 1]), sb("bk", [128, 1]), sb("bv", [128, EMB])
        stats, mv = sb("stats", [128, 2, G, 6]), sb("mv", [128, 2, G, 2])
        logvar, rstd = sb("logvar", [128, 2, G]), sb("rstd", [128, 2, G])
        xn, lnT = sb("xn", [128, 2, G, EMB]), sb("lnT", [128, 2, qn])
        q_parts, k_parts = sb("q_parts", [128, 2, 2, qn], F32R), sb("k_parts", [128, 2, 2, kn], F32R)
        v_raw, v_sb = sb("v_raw", [128, 2, G, EMB]), sb("v", [128, 2, G, EMB])
        if cross:
            ctx_in, ctxT = sb("ctx_in", [128, 2, G, EMB]), sb("ctxT", [128, 2, kn])
        if linear:
            feat = sb("feat", [128, 2, 2, 3, qn])
        else:
            negmax, negmaxT = sb("negmax", [128, 2, 16 * G]), sb("negmaxT", [16 if scrambled else 16 * G, 2, 16 * G * HD if scrambled else SEQ], F32R)
        if scrambled:
            vT, v_stack = sb("vT", [128, 2, qn]), sb("v_stack", [32, 4 * qn])
            k_placed, q_placed, v_placed = sb("k_placed", [128, 2, 4 * qn], F32R), sb("q_placed", [32, 2, 4 * qn], F32R), sb("v_placed", [32, 2, 4 * qn])
            rot, raw, raw_b = sb("rot", [128, 2, 4]), sb("raw", [128, 2, EMB]), sb("raw_b", [1, 2, EMB])
            rope_tmp, rot_b = sb("rope_tmp", [128, 2, 4, 16]), sb("rot_b", [1, 2, EMB])
            query_f, query_r, max_spread = sb("query_f", [128, 16], F32R), sb("query_r", [128, 8]), sb("max_spread", [128, 16 * G, 8], F32R)
        if weighted:
            den_w = sb("den_w", [128, 2, G, 32])
        probs = sb("probs", [128, 8, 512])
        logden, recip, attended = sb("logden", [128, 2, 512]), sb("recip", [128, 2, 512]), sb("attended", [128, 2, 512])
        banks = [ctx.enter_context(nc.psum_tensor(f"{tag}_bank{n}", [128, 512], F32)) for n in range(8)]
        misc, score_ps, scoreT_ps, out_ps, den_ps = banks[0:2], banks[2:4], banks[4:6], banks[6], banks[7]
        passed = {eng.engine: sem(f"passed_{name}") for name, eng in (("dve", nc.vector), ("pool", nc.gpsimd), ("pe", nc.tensor), ("sp", nc.sync))}
        weights_in, stats_done, mv_done = sem("weights_in"), sem("stats_done"), sem("mv_done")
        logvar_done, rstd_done, xn_done, x_biased = sem("logvar_done"), sem("rstd_done"), sem("xn_done"), sem("x_biased")
        xnT_mm, q_mm, k_mm, v_mm = sem("xnT_mm"), sem("q_mm"), sem("k_mm"), sem("v_mm")
        lnT_ready, vraw_ready, v_ready = sem("lnT_ready"), sem("vraw_ready"), sem("v_ready")
        qhi_ready, qlo_ready, khi_ready, klo_ready = sem("qhi_ready"), sem("qlo_ready"), sem("khi_ready"), sem("klo_ready")
        stack_high, stack_low = sem2("stack_high"), sem2("stack_low")
        scoresT_mm, probs_ready, values_mm = sem("scoresT_mm"), sem("probs_ready"), sem("values_mm")
        logden_ready, recip_ready, attended_ready = sem("logden_ready"), sem("recip_ready"), sem("attended_ready")
        y_mm, y_added = sem("y_mm"), sem("y_added")
        if cross:
            ctx_loaded, ctxT_mm, ctxT_ready = sem2("ctx_loaded"), sem("ctxT_mm"), sem("ctxT_ready")
        if linear:
            feat_act, feat_done = sem("feat_act"), sem("feat_done")
        else:
            max_in, shift_in = sem2("max_in"), sem2("shift_in")
            scores_mm, max_done, maxT_mm, maxT_ready = sem("scores_mm"), sem("max_done"), sem("maxT_mm"), sem("maxT_ready")
        if scrambled:
            max_spread_done, queries_made = sem("max_spread_done"), sem("queries_made")
            vT_ready, vback_mm, v_in = sem("vT_ready"), sem("vback_mm"), sem2("v_in")
            k_in, k_in_pool, q_in = sem2("k_in"), sem2("k_in_pool"), sem2("q_in")
            q_grouped, k_grouped, v_grouped = sem("q_grouped"), sem("k_grouped"), sem("v_grouped")
            rope_in, rope_mul, rope_add, rope_done = sem("rope_in"), sem("rope_mul"), sem("rope_add"), sem("rope_done")

        def head(tile, g, b, n):
            return tile[:, (g * G + b) * n:(g * G + b + 1) * n]

        def heads4(tile, g, b, n):
            if scrambled:
                at = 16 * g + 8 * b
                return tile.rearrange("p j (f q) -> p j f q", f=16)[:, :, :, at:at + 8]
            return tile[:, :, (g * G + b) * n:(g * G + b + 1) * n]

        def rows_of(parts, r, part, j):
            return raw_words(parts[:, r, part, 64 * j:64 * j + 64] if scrambled else parts[32 * j:32 * j + 32, r, part, :])

        def grouped(tile):
            return tile.rearrange("p (q f r) -> p q f r", f=16, r=8)

        def placed(tile):
            return tile.rearrange("p (f q r) -> p q f r", f=16, r=8)

        SLOTS = 10
        AT = {"pe_y0": 1, "pe_values1": 1, "pe_qk": 3, "pe_v": 5, "pe_values0": 7, "pe_y1": 8,
              "act_high": 3, "act_recip1": 3, "act_rstd": 6, "act_recip0": 8,
              "dve_y0": 1, "dve_low": 3, "dve_attend1": 5, "dve_stats": 5, "dve_v": 6, "dve_norm": 7, "dve_y1": 9, "dve_attend0": 9}
        if linear:
            AT.update({"pe_values1": 2, "act_high": 4, "dve_low": 5})

        def live(s):
            return not s.static or 0 <= s.off < steps_n

        def run_steps(eng, body):
            lead = 5
            loops = (steps_n - lead) // 2
            for t in range(lead):
                body(Step(0, t))
            with eng.Fori(0, loops) as i:
                for u in range(2):
                    body(Step(i, lead + u))
            for t in range(lead + 2 * loops, steps_n + 3):
                body(Step(0, t))

        n_weights = 8 if not linear else 5

        def pass_waits(eng):
            eng.sem_inc(passed[eng.engine], 1)

        with nc.Block() as block:
            @block.sync
            def _(sp):
                sp.dma_start(raw[:, 0, :] if scrambled else wq[:], dram["wq"]).then_inc(weights_in, 16)
                sp.dma_start(raw[:, 1, :] if scrambled else wk[:], dram["wk"]).then_inc(weights_in, 16)
                sp.dma_start(wv[:], dram["wv"]).then_inc(weights_in, 16)
                sp.dma_start(wo[:], dram["wo"]).then_inc(weights_in, 16)
                sp.dma_start(bo[:], dram["bo"].broadcast_to([128, EMB])).then_inc(weights_in, 16)
                if scrambled:
                    sp.dma_start(raw_b[:, 0, :], dram["bq"]).then_inc(weights_in, 16)
                    sp.dma_start(raw_b[:, 1, :], dram["bk"]).then_inc(weights_in, 16)
                    sp.dma_start(bv[:, 0:1], dram["bv"]).then_inc(weights_in, 16)
                    sp.dma_start(rot[:, 0, :], dram["cos"].broadcast_to([128, 4])).then_inc(rope_in, 16)
                    sp.dma_start(rot[:, 1, :], dram["sin"].broadcast_to([128, 4])).then_inc(rope_in, 16)
                    sp.wait_ge(rope_done, 1)
                    sp.dma_start(bq[:], rot_b[0:1, 0, :]).then_inc(rope_in, 16)
                    sp.dma_start(bk[:], rot_b[0:1, 1, :]).then_inc(rope_in, 16)
                elif not linear:
                    sp.dma_start(bq[:], dram["bq"]).then_inc(weights_in, 16)
                    sp.dma_start(bk[:], dram["bk"]).then_inc(weights_in, 16)
                    sp.dma_start(bv[:], dram["bv"].broadcast_to([128, EMB])).then_inc(weights_in, 16)

                def load_ctx(s):
                    need(sp, ctxT_mm, s.count(1, -1))
                    pass_waits(sp)
                    sp.dma_start(ctx_in[:CTX, s.ring, :, :], dram["ctx"][s.ds(G), :, :].rearrange("b s e -> s b e")) \
                        .then_inc(ctx_loaded[s.ring], 16)

                if cross:
                    load_ctx(Step(0, 0))

                def place_maxima(C):
                    sp.wait_ge(maxT_ready, C.count(1, 1))
                    pass_waits(sp)
                    need(sp, scoresT_mm, C.back(1).count(8, 0))
                    pass_waits(sp)
                    if scrambled:
                        for j in range(4):
                            sp.dma_start(raw_words(q_blocks[C.ring][96:97, j, :]), raw_words(negmaxT[:, C.ring, 32 * G * j:32 * G * (j + 1)])) \
                                .then_inc(shift_in[C.ring], 16)
                    else:
                        sp.dma_start(raw_words(q_blocks[C.ring][96:97, :, :]), raw_words(negmaxT[:, C.ring, :])).then_inc(shift_in[C.ring], 16)

                def place_q(B):
                    r = B.ring
                    need(sp, scoresT_mm, B.back(1).count(8, 0))
                    pass_waits(sp)
                    sp.wait_ge(qhi_ready, B.count(1, 1))
                    for rep in range(2):
                        for j in range(4):
                            at = 32 * rep + 8 * j
                            sp.dma_start(raw_words(q_blocks[r][at:at + 8, j, :]), rows_of(q_parts, r, 0, j)).then_inc(stack_high[r], 16)
                    if scrambled:
                        sp.wait_ge(khi_ready, B.count(1, 1))
                        for j in range(4):
                            sp.dma_start(raw_words(k_placed[8 * j:8 * j + 8, r, :]), rows_of(k_parts, r, 0, j)).then_inc(k_in[r], 16)

                def place_for_maxima(t):
                    r = t.ring
                    need(sp, scores_mm, t.back(1).count(8, 0))
                    pass_waits(sp)
                    sp.wait_ge(qhi_ready, t.count(1, 1))
                    if scrambled:
                        for j in range(4):
                            sp.dma_start(raw_words(q_placed[8 * j:8 * j + 8, r, :]), rows_of(q_parts, r, 0, j)).then_inc(q_in[r], 16)
                    else:
                        sp.dma_start(raw_words(q_hi[r][0:32, :]), raw_words(q_parts[:, r, 0, :])).then_inc(max_in[r], 16)
                    sp.wait_ge(khi_ready, t.count(1, 1))
                    for j in range(4):
                        sp.dma_start(raw_words(k_blocks[r][8 * j:8 * j + 8, j, :4 * kn]), rows_of(k_parts, r, 0, j)).then_inc(max_in[r], 16)

                def step(t):
                    if not linear and live(t.back(2)):
                        place_maxima(t.back(2))
                    if live(t.back(1)):
                        place_q(t.back(1))
                    if cross and live(t.back(-1)):
                        load_ctx(t.back(-1))
                    if not linear and live(t):
                        place_for_maxima(t)

                run_steps(sp, step)

            @block.gpsimd
            def _(pool):
                pool.wait_ge(weights_in, 16 * n_weights)

                def step(t):
                    if not live(t):
                        return
                    r = t.ring
                    pool.wait_ge(xn_done, t.count(1, 1))
                    pool.tensor_tensor(x_sb[:, t.ds(G), :], x_sb[:, t.ds(G), :],
                                       bo[:].unsqueeze(1).broadcast_to([128, G, EMB]), ALU.add).then_inc(x_biased, 1)
                    if scrambled:
                        need(pool, k_grouped, t.count(1, -1))
                    else:
                        need(pool, scoresT_mm, t.back(1).count(8, 0))
                    pool.wait_ge(khi_ready, t.count(1, 1))
                    pool.wait_ge(klo_ready, t.count(1, 1))
                    pass_waits(pool)
                    for rep, part in ((0, 0), (1, 1), (2, 0)):
                        if not scrambled:
                            pool.dma_start(raw_words(k_stack[r][32 * rep:32 * rep + 32, :4 * kn]), raw_words(k_parts[:, r, part, :])).then_inc(stack_low[r], 16)
                        elif rep:
                            for j in range(4):
                                at = 32 * rep + 8 * j
                                pool.dma_start(raw_words(k_placed[at:at + 8, r, :]), rows_of(k_parts, r, part, j)).then_inc(k_in_pool[r], 16)
                    if scrambled:
                        pool.wait_ge(vT_ready, t.count(1, 1))
                        need(pool, v_grouped, t.count(1, -1))
                        pass_waits(pool)
                        for j in range(4):
                            pool.dma_start(v_placed[8 * j:8 * j + 8, r, :], vT[:, r, 64 * j:64 * j + 64]).then_inc(v_in[r], 16)
                        need(pool, scoresT_mm, t.back(1).count(8, 0))
                    pool.wait_ge(qlo_ready, t.count(1, 1))
                    pass_waits(pool)
                    for j in range(4):
                        pool.dma_start(raw_words(q_blocks[r][64 + 8 * j:72 + 8 * j, j, :]), rows_of(q_parts, r, 1, j)).then_inc(stack_low[r], 16)
                    if not scrambled:
                        pool.wait_ge(vraw_ready, t.count(1, 1))
                        need(pool, values_mm, t.back(1).count(8, 0))
                        pass_waits(pool)
                        if weighted:
                            a = const["abundance"][:keys, t.ds(G)].unsqueeze(2)
                            pool.tensor_tensor(v_sb[:keys, r], v_raw[:keys, r], a.broadcast_to([keys, G, EMB]), ALU.mult)
                            pool.tensor_tensor(den_w[:keys, r], const["ones"][:keys, 0:32].unsqueeze(1).broadcast_to([keys, G, 32]),
                                               a.broadcast_to([keys, G, 32]), ALU.mult).then_inc(v_ready, 1)
                        else:
                            pool.tensor_copy(v_sb[:keys, r], v_raw[:keys, r]).then_inc(v_ready, 1)

                run_steps(pool, step)

            @block.scalar
            def _(act):
                act.preload_act_table_set("natural_log_exp_and_others")
                def rstd_of(s):
                    act.wait_ge(mv_done, s.count(1, 1))
                    act.activation(logvar[:, s.ring, :], mv[:, s.ring, :, 1], ACT.Ln, bias=const["eps_ln"][:]).then_inc(logvar_done, 1)
                    act.wait_ge(logvar_done, s.count(1, 1))
                    need(act, xn_done, s.count(1, -1))
                    act.activation(rstd[:, s.ring, :], logvar[:, s.ring, :], ACT.Exp, scale=-0.5).then_inc(rstd_done, 1)

                def recip_of(s, b):
                    act.wait_ge(values_mm, s.count(8, 4 * b + 4))
                    need(act, recip_ready, s.count(2, b - 1))
                    act.activation(logden[:, b, :], den_ps[:], ACT.Ln, bias=const["eps_den" if linear else "zero"][:]).then_inc(logden_ready, 1)
                    act.wait_ge(logden_ready, s.count(2, b + 1))
                    need(act, attended_ready, s.count(2, b - 1))
                    act.activation(recip[:, b, :], logden[:, b, :], ACT.Exp, scale=-1.0).then_inc(recip_ready, 1)

                def features(t):
                    for w, mm in enumerate((q_mm, k_mm)):
                        src = misc[(pos["q"] + w) % 2][:, 0:qn]
                        act.wait_ge(mm, t.count(1, 1))
                        need(act, feat_done, t.back(2).count(2, w + 1))
                        act.activation(feat[:, t.ring, w, 0, :], src, ACT.Exp)
                        act.activation(feat[:, t.ring, w, 1, :], src, ACT.Relu).then_inc(feat_act, 1)

                def high_parts(t):
                    r = t.ring
                    for w, (mm, hi, parts, bias, n) in enumerate(((q_mm, qhi_ready, q_parts, bq, qn), (k_mm, khi_ready, k_parts, bk, kn))):
                        src = misc[(pos["q"] + w) % 2][:, 0:n]
                        if linear:
                            act.wait_ge(feat_done, t.count(2, w + 1))
                            src = feat[:, r, w, 2, :]
                        else:
                            act.wait_ge(mm, t.count(1, 1))
                        need(act, stack_high[r], t.half(16 * n_sp))
                        need(act, stack_low[r], t.half(16 * n_pool))
                        if not linear:
                            need(act, max_in[r], t.half(16 * n_max))
                        if scrambled:
                            need(act, q_in[r], t.half(16 * 4))
                            need(act, k_in[r], t.half(16 * 4))
                            need(act, k_in_pool[r], t.half(16 * 8))
                        act.activation(parts[:, r, 0, :], src, ACT.Identity, bias=const["zero"][:] if linear else bias[:]).then_inc(hi, 1)

                def take_maxima(B):
                    act.wait_ge(maxT_mm, B.count(1, 1))
                    need(act, shift_in[B.ring], B.half(16 * n_shift))
                    act.activation(negmaxT[:, B.ring, :], misc[pos["maxT"] % 2][0:negmaxT.shape[0], 0:negmaxT.shape[2]], ACT.Copy).then_inc(maxT_ready, 1)

                def group_q(t):
                    act.wait_ge(q_in[t.ring], t.half(16 * 4, 1))
                    need(act, scores_mm, t.back(1).count(8, 0))
                    act.activation(grouped(q_hi[t.ring][0:32, :]), placed(q_placed[:, t.ring, :]), ACT.Copy).then_inc(q_grouped, 1)

                rstd_of(Step(0, 0))
                act.wait_ge(weights_in, 16 * n_weights)
                if scrambled:
                    act.wait_ge(rope_in, 64)

                def step(t):
                    C = t.back(2)
                    r = t.ring
                    if live(t):
                        if cross:
                            act.wait_ge(ctxT_mm, t.count(1, 1))
                            need(act, v_mm, t.count(1, -1))
                            act.activation(ctxT[:, r, :], misc[pos["ctxT"] % 2][:, 0:kn], ACT.Copy).then_inc(ctxT_ready, 1)
                        bank = misc[pos["xnT"] % 2]
                        act.wait_ge(xnT_mm, t.count(1, 1))
                        need(act, v_mm, t.count(1, -1))
                        if scrambled:
                            for b in range(G):
                                act.activation(lnT[:, r, :].rearrange("p (j g b r) -> p b g j r", j=4, g=4, b=G)[:, b],
                                               bank[:, b * SEQ:(b + 1) * SEQ].rearrange("p (g j r) -> p g j r", g=4, j=4), ACT.Copy).then_inc(lnT_ready, 1)
                        else:
                            act.activation(lnT[:, r, :], bank[:, 0:qn], ACT.Copy).then_inc(lnT_ready, G)
                    for slot in range(SLOTS):
                        n = slot - 2
                        if not linear and live(C) and n >= 0:
                            act.wait_ge(scoresT_mm, C.count(8, n + 1))
                            need(act, values_mm, C.count(8, n - 7))
                            act.activation(probs[:keys, n, :], scoreT_ps[n % 2][:keys, :], ACT.Exp, scale=scale).then_inc(probs_ready, 1)
                        if slot == 3 and linear and live(t):
                            features(t)
                        if slot == AT["act_high"] and live(t):
                            high_parts(t)
                        if slot == AT["act_recip1"] and live(t.back(3)):
                            recip_of(t.back(3), 1)
                        if slot == AT["act_rstd"] and live(t.back(-1)):
                            rstd_of(t.back(-1))
                        if slot == AT["act_recip0"] and live(C):
                            recip_of(C, 0)
                        if slot == 8 and not linear and live(t.back(1)):
                            take_maxima(t.back(1))
                        if slot == 9 and scrambled and live(t):
                            group_q(t)

                run_steps(act, step)

            @block.vector
            def _(dve):
                def row_block(s, b):
                    return x_sb[:, s.ds1(G, b), :].rearrange("p a e -> p (a e)")

                def stats_of(s):
                    for b in range(G):
                        dve.bn_stats(stats[:, s.ring, b, :], row_block(s, b)).then_inc(stats_done, 1)
                    dve.wait_ge(stats_done, s.count(G, G))
                    pass_waits(dve)
                    for b in range(G):
                        last = dve.bn_aggr(mv[:, s.ring, b, :], stats[:, s.ring, b, :])
                    last.then_inc(mv_done, 1)

                def normalise(s):
                    dve.wait_ge(rstd_done, s.count(1, 1))
                    dve.wait_ge(mv_done, s.count(1, 1))
                    need(dve, xnT_mm, s.count(1, -1))
                    for b in range(G):
                        last = dve.tensor_scalar(xn[:, s.ring, b, :], row_block(s, b), mv[:, s.ring, b, 0:1], rstd[:, s.ring, b:b + 1],
                                                 ALU.subtract, ALU.mult)
                    last.then_inc(xn_done, 1)

                def add_y(s, b):
                    dve.wait_ge(y_mm, s.count(2, b + 1))
                    dve.wait_ge(x_biased, s.count(1, 1))
                    dve.tensor_tensor(row_block(s, b), misc[pos[f"y{b}"] % 2][:, 0:EMB], row_block(s, b), ALU.add).then_inc(y_added, 1)

                def attend(s, b):
                    dve.wait_ge(recip_ready, s.count(2, b + 1))
                    need(dve, y_mm, s.count(2, b - 1))
                    def view(tile, order):
                        return tile.rearrange(f"p (j {order}) -> p j f r", j=4, f=16) if scrambled else tile

                    dve.tensor_tensor(view(attended[:, b, :], "r f"), view(out_ps[:], "f r"), view(recip[:, b, :], "f r"), ALU.mult).then_inc(attended_ready, 1)

                stats_of(Step(0, 0))
                normalise(Step(0, 0))
                dve.wait_ge(weights_in, 16 * n_weights)
                if scrambled:
                    ident = const["ident"][:]
                    dve.tensor_reduce(out=query_f[:], in_=ident.rearrange("p (f r) -> p f r", r=8), axis=AX.X, op=ALU.max).then_inc(queries_made, 1)
                    dve.tensor_reduce(out=query_r[:], in_=ident.rearrange("p (f r) -> p r f", r=8), axis=AX.X, op=ALU.max).then_inc(queries_made, 1)
                    dve.wait_ge(rope_in, 32)
                    turns = 0
                    for src, rows in ((raw, 128), (raw_b, 1)):
                        for w in range(2):
                            out = (wq, wk)[w][:] if rows == 128 else rot_b[:, w, :]
                            pair = src[:, w, :].rearrange("p (i e f) -> p e i f", e=2, f=16)
                            turned = out.rearrange("p (i e f) -> p e i f", e=2, f=16)
                            cos, sin = (rot[0:rows, n, :].unsqueeze(2).broadcast_to([rows, 4, 16]) for n in range(2))
                            for e, (p, q, op) in enumerate(((cos, sin, ALU.subtract), (sin, cos, ALU.add))):
                                need(dve, rope_add, turns)
                                dve.tensor_tensor(rope_tmp[0:rows, 0], pair[:, 0], p, ALU.mult).then_inc(rope_mul, 1)
                                dve.tensor_tensor(rope_tmp[0:rows, 1], pair[:, 1], q, ALU.mult).then_inc(rope_mul, 1)
                                turns += 1
                                dve.wait_ge(rope_mul, 2 * turns)
                                dve.tensor_tensor(turned[:, e], rope_tmp[0:rows, 0], rope_tmp[0:rows, 1], op).then_inc(rope_add, 1)
                    dve.wait_ge(rope_add, turns)
                    dve.sem_inc(rope_done, 1)
                    dve.wait_ge(rope_in, 64)

                def finish_features(t):
                    for w in range(2):
                        dve.wait_ge(feat_act, t.count(2, w + 1))
                        need(dve, qlo_ready if w == 0 else klo_ready, t.count(1, -1))
                        dve.scalar_tensor_tensor(out=feat[:, t.ring, w, 2, :], in0=feat[:, t.ring, w, 0, :], scalar=1.0, in1=feat[:, t.ring, w, 1, :],
                                                 op0=ALU.min, op1=ALU.add).then_inc(feat_done, 1)

                def low_parts(t):
                    r = t.ring
                    for w, (hi, lo, parts, bias, n) in enumerate(((qhi_ready, qlo_ready, q_parts, bq, qn), (khi_ready, klo_ready, k_parts, bk, kn))):
                        dve.wait_ge(hi, t.count(1, 1))
                        if linear:
                            dve.tensor_tensor(parts[:, r, 1, :], feat[:, r, w, 2, :], parts[:, r, 0, :], ALU.subtract).then_inc(lo, 1)
                        else:
                            dve.scalar_tensor_tensor(out=parts[:, r, 1, :], in0=misc[(pos["q"] + w) % 2][:, 0:n], scalar=bias[:],
                                                     in1=parts[:, r, 0, :], op0=ALU.add, op1=ALU.subtract).then_inc(lo, 1)

                def take_values(t):
                    r = t.ring
                    bank = misc[pos["v"] % 2]
                    dve.wait_ge(v_mm, t.count(1, 1))
                    if scrambled:
                        need(dve, v_in[r], t.half(16 * 4))
                        dve.tensor_scalar(vT[:, r, :], bank[:, 0:qn], bv[:, 0:1], None, ALU.add).then_inc(vT_ready, 1)
                    else:
                        src = bank[:keys, 0:G * EMB].rearrange("p (b e) -> p b e", b=G)
                        need(dve, v_ready, t.count(1, -1))
                        if linear:
                            dve.tensor_copy(v_raw[:keys, r], src).then_inc(vraw_ready, 1)
                        else:
                            dve.tensor_tensor(v_raw[:keys, r], src, bv[:keys].unsqueeze(1).broadcast_to([keys, G, EMB]), ALU.add).then_inc(vraw_ready, 1)

                def group_values(B):
                    dve.wait_ge(v_in[B.ring], B.half(16 * 4, 1))
                    need(dve, vback_mm, B.count(1, 0))
                    dve.tensor_copy(grouped(v_stack[:]), placed(v_placed[:, B.ring, :])).then_inc(v_grouped, 1)

                def group_keys(B):
                    dve.wait_ge(k_in[B.ring], B.half(16 * 4, 1))
                    dve.wait_ge(k_in_pool[B.ring], B.half(16 * 8, 1))
                    need(dve, scoresT_mm, B.back(1).count(8, 0))
                    dve.tensor_copy(grouped(k_stack[B.ring][0:96, :]), placed(k_placed[0:96, B.ring, :])).then_inc(k_grouped, 1)

                def take_values_back(B):
                    dve.wait_ge(vback_mm, B.count(1, 1))
                    need(dve, values_mm, B.back(1).count(8, 0))
                    dve.tensor_copy(v_sb[:, B.ring].rearrange("p b e -> p (b e)"), misc[pos["vback"] % 2][:, 0:G * EMB]).then_inc(v_ready, 1)

                def maximum(B, n):
                    b, g = divmod(n, 4)
                    dve.wait_ge(scores_mm, B.count(8, n + 1))
                    if n == 0:
                        need(dve, maxT_mm, B.count(1, -1))
                    dve.tensor_reduce(out=negmax[:, B.ring, :].rearrange("p (j q) -> p j q", j=4)[:, :, g * G + b],
                                      in_=score_ps[n % 2][:, 0:4 * keys].rearrange("p (j k) -> p j k", j=4),
                                      axis=AX.X, op=ALU.max, negate=True).then_inc(max_done, 1)

                def spread_maxima(B):
                    dve.wait_ge(max_done, B.count(8, 8))
                    dve.wait_ge(queries_made, 2)
                    need(dve, maxT_mm, B.count(1, 0))
                    dve.tensor_tensor(max_spread[:], negmax[:, B.ring, :].unsqueeze(2).broadcast_to([128, 16 * G, 8]),
                                      query_r[:].unsqueeze(1).broadcast_to([128, 16 * G, 8]), ALU.mult).then_inc(max_spread_done, 1)

                def mask(C, n):
                    dve.wait_ge(scoresT_mm, C.count(8, n + 1))
                    need(dve, values_mm, C.count(8, n - 7))
                    dve.tensor_tensor(probs[:, n, :].rearrange("p (j c) -> p j c", j=4), scoreT_ps[n % 2][:].rearrange("p (j c) -> p j c", j=4),
                                      const["causal"][:].unsqueeze(1).broadcast_to([128, 4, SEQ]), ALU.mult).then_inc(probs_ready, 1)

                def step(t):
                    B, C, D = t.back(1), t.back(2), t.back(3)
                    for slot in range(SLOTS):
                        if not linear and live(B) and slot < 8:
                            maximum(B, slot)
                        if linear and live(C) and slot >= 2:
                            mask(C, slot - 2)
                        if slot == AT["dve_y0"] and live(D):
                            add_y(D, 0)
                        if slot == 3 and linear and live(t):
                            finish_features(t)
                        if not linear and slot == AT["dve_low"] and live(t):
                            low_parts(t)
                        if slot == AT["dve_attend1"] and live(D):
                            attend(D, 1)
                        if linear and slot == AT["dve_low"] and live(t):
                            low_parts(t)
                        if slot == AT["dve_stats"] and live(t.back(-1)):
                            stats_of(t.back(-1))
                        if slot == AT["dve_v"] and live(t):
                            take_values(t)
                        if slot == 6 and scrambled and live(B):
                            group_values(B)
                        if slot == AT["dve_norm"] and live(t.back(-1)):
                            normalise(t.back(-1))
                        if slot == 7 and scrambled and live(B):
                            spread_maxima(B)
                            group_keys(B)
                        if slot == 9 and scrambled and live(B):
                            take_values_back(B)
                        if slot == AT["dve_y1"] and live(D):
                            add_y(D, 1)
                        if slot == AT["dve_attend0"] and live(C):
                            attend(C, 0)

                run_steps(dve, step)

            @block.tensor
            def _(pe):
                pe.wait_ge(weights_in, 16 * n_weights)
                if scrambled:
                    pe.wait_ge(rope_done, 1)
                rows = 96 if linear else 97

                def used(name, s):
                    if name in ("q", "k") and linear:
                        return feat_act, s.count(2, 1 + (name == "k"))
                    return {
                        "maxT": lambda: (maxT_ready, s.count(1, 1)), "ctxT": lambda: (ctxT_ready, s.count(1, 1)),
                        "xnT": lambda: (lnT_ready, s.count(G, G)), "q": lambda: (qlo_ready, s.count(1, 1)),
                        "k": lambda: (klo_ready, s.count(1, 1)),
                        "v": lambda: (vT_ready if scrambled else vraw_ready, s.count(1, 1)),
                        "vback": lambda: (v_ready, s.count(1, 1)),
                        "y1": lambda: (y_added, s.count(2, 2)), "y0": lambda: (y_added, s.count(2, 1)),
                    }[name]()

                def take_bank(name, s):
                    at = pos[name]
                    while True:
                        at -= 2
                        if at < 0:
                            at += len(uses)
                            s = s.back(1)
                        if s.static and s.off < 0:
                            return
                        before, lag = uses[at]
                        if live(s.back(lag)):
                            pe.wait_ge(*used(before, s.back(lag)))
                            return

                def project_out(s, b, t):
                    pe.wait_ge(attended_ready, s.count(2, b + 1))
                    take_bank(f"y{b}", t)
                    for j in range(4):
                        last = pe.matmul(misc[pos[f"y{b}"] % 2][:, 0:EMB], attended[:, b, j * SEQ:(j + 1) * SEQ], wo[:, j, :], start=(j == 0), stop=(j == 3))
                    last.then_inc(y_mm, 1)

                def transpose_maxima(B, t):
                    take_bank("maxT", t)
                    if scrambled:
                        pe.wait_ge(queries_made, 2)
                        pe.wait_ge(max_spread_done, B.count(1, 1))
                        pe.matmul(misc[pos["maxT"] % 2][0:16, 0:16 * G * 8], query_f[:], max_spread[:].rearrange("p q r -> p (q r)"), start=True, stop=True).then_inc(maxT_mm, 1)
                    else:
                        pe.wait_ge(max_done, B.count(8, 8))
                        pe.transpose(misc[pos["maxT"] % 2][0:16 * G, 0:SEQ], negmax[:, B.ring, :], const["ident"][:]).then_inc(maxT_mm, 1)

                def transpose_inputs(t):
                    r = t.ring
                    if cross:
                        pe.wait_ge(ctx_loaded[r], t.half(16, 1))
                        take_bank("ctxT", t)
                        for b in range(G):
                            last = pe.transpose(misc[pos["ctxT"] % 2][:, b * CTX:(b + 1) * CTX], ctx_in[:CTX, r, b, :], const["ident"][:CTX, :CTX])
                        last.then_inc(ctxT_mm, 1)
                    pe.wait_ge(xn_done, t.count(1, 1))
                    take_bank("xnT", t)
                    for b in range(G):
                        last = pe.transpose(misc[pos["xnT"] % 2][:, b * SEQ:(b + 1) * SEQ], xn[:, r, b, :], const["ident"][:])
                    last.then_inc(xnT_mm, 1)

                def project_qk(t):
                    r = t.ring
                    pe.wait_ge(lnT_ready, t.count(G, G))
                    take_bank("q", t)
                    pe.matmul(misc[pos["q"] % 2][:, 0:qn], wq[:], lnT[:, r, :], start=True, stop=True).then_inc(q_mm, 1)
                    if cross:
                        pe.wait_ge(ctxT_ready, t.count(1, 1))
                    take_bank("k", t)
                    pe.matmul(misc[pos["k"] % 2][:, 0:kn], wk[:], (ctxT if cross else lnT)[:, r, :], start=True, stop=True).then_inc(k_mm, 1)

                def project_v(t):
                    r = t.ring
                    source = ctxT if cross else lnT
                    take_bank("v", t)
                    bank = misc[pos["v"] % 2]
                    if scrambled:
                        pe.matmul(bank[:, 0:qn], wv[:], lnT[:, r, :], start=True, stop=True).then_inc(v_mm, 1)
                    else:
                        for b in range(G):
                            last = pe.matmul(bank[:keys, b * EMB:(b + 1) * EMB], source[:, r, b * keys:(b + 1) * keys], wv[:], start=True, stop=True)
                        last.then_inc(v_mm, 1)

                def transpose_values(B, t):
                    pe.wait_ge(v_grouped, B.count(1, 1))
                    take_bank("vback", t)
                    pass_waits(pe)
                    for b in range(G):
                        for g in range(4):
                            at = b * EMB + 32 * g
                            last = pe.transpose(misc[pos["vback"] % 2][:, at:at + 32], head(v_stack[:], g, b, SEQ), const["ident"][:32, :32])
                    last.then_inc(vback_mm, 1)

                def scores(B, n):
                    b, g = divmod(n, 4)
                    if n == 0:
                        pe.wait_ge(max_in[B.ring], B.half(16 * n_max, 1))
                        if scrambled:
                            pe.wait_ge(q_grouped, B.count(1, 1))
                    need(pe, max_done, B.count(8, n - 1))
                    pe.matmul(score_ps[n % 2][:, 0:4 * keys], head(q_hi[B.ring][:], g, b, SEQ), heads4(k_blocks[B.ring][:], g, b, keys),
                              start=True, stop=True).then_inc(scores_mm, 1)

                def scores_transposed(C, n):
                    b, g = divmod(n, 4)
                    if n == 0:
                        pe.wait_ge(stack_high[C.ring], C.half(16 * n_sp, 1))
                        pe.wait_ge(stack_low[C.ring], C.half(16 * n_pool, 1))
                        if not linear:
                            pe.wait_ge(shift_in[C.ring], C.half(16 * n_shift, 1))
                        if scrambled:
                            pe.wait_ge(k_grouped, C.count(1, 1))
                    need(pe, probs_ready, C.count(8, n - 1))
                    pe.matmul(scoreT_ps[n % 2][:keys, :], head(k_stack[C.ring][0:rows], g, b, keys), heads4(q_blocks[C.ring][0:rows], g, b, SEQ),
                              start=True, stop=True).then_inc(scoresT_mm, 1)

                def values(s, b):
                    if b == 0:
                        pe.wait_ge(v_ready, s.count(1, 1))
                    need(pe, attended_ready, s.count(2, b))
                    need(pe, logden_ready, s.count(2, b))
                    pe.wait_ge(probs_ready, s.count(8, 4 * b + 4))
                    for g in range(4):
                        rows_g = slice(32 * g, 32 * g + 32)
                        pe.matmul(out_ps[rows_g, :], v_sb[:keys, s.ring, b, rows_g], probs[:keys, 4 * b + g, :], start=True, stop=True, tile_position=(0, 32 * g))
                    for g in range(4):
                        rows_g = slice(32 * g, 32 * g + 32)
                        ones = den_w[:keys, s.ring, b, :] if weighted else const["ones"][:keys, 0:32]
                        pe.matmul(den_ps[rows_g, :], ones, probs[:keys, 4 * b + g, :], start=True, stop=True, tile_position=(0, 32 * g)).then_inc(values_mm, 1)

                def step(t):
                    B, C, D = t.back(1), t.back(2), t.back(3)
                    for slot in range(SLOTS):
                        if not linear and live(B) and slot < 8:
                            scores(B, slot)
                        if live(C) and slot >= 2:
                            scores_transposed(C, slot - 2)
                        if slot == 0 and live(t):
                            transpose_inputs(t)
                        if slot == AT["pe_y0"] and live(D):
                            project_out(D, 0, t)
                        if slot == AT["pe_values1"] and live(D):
                            values(D, 1)
                        if slot == AT["pe_qk"] and live(t):
                            project_qk(t)
                        if slot == AT["pe_v"] and live(t):
                            project_v(t)
                        if slot == AT["pe_values0"] and live(C):
                            values(C, 0)
                        if slot == 8 and scrambled and live(B):
                            transpose_values(B, t)
                        if slot == AT["pe_y1"] and live(D):
                            project_out(D, 1, t)
                        if slot == 8 and not linear and live(B):
                            transpose_maxima(B, t)

                run_steps(pe, step)


GF = 4
TOK = GF * SEQ


class ExpertPhase:

    def __init__(self, nc, ctx, tag):
        self.nc, self.ctx, self.tag, self.steps_n = nc, ctx, tag, BATCH // GF
        self.sem = Semaphores(nc, ctx, tag)

    def sb(self, name, shape, dt=F32):
        return self.ctx.enter_context(self.nc.sbuf_tensor(f"{self.tag}_{name}", shape, dt))

    def live(self, s):
        return not s.static or 0 <= s.off < self.steps_n

    def run_steps(self, eng, body):
        lead = 3
        for t in range(lead):
            body(Step(0, t))
        with eng.Fori(0, (self.steps_n - 1 - lead) // 2) as i:
            for u in range(2):
                body(Step(i, lead + u))
        for t in range(self.steps_n - 1, self.steps_n + 2):
            body(Step(0, t))


def experts_phase(nc, x_sb, const, ins):
    NH, NE, D, I = 8, 16, 16, 64
    with ExitStack() as ctx:
        ph = ExpertPhase(nc, ctx, "f0")
        sb, sem, live = ph.sb, ph.sem, ph.live
        wm, bm = sb("wm", [128, EMB]), sb("bm", [128, 1])
        emb = sb("emb", [128, NH * NE])
        w1_raw, w1_hi, w1 = sb("w1_raw", [96, NE * I]), sb("w1_hi", [96, NE * I], F32R), sb("w1", [96, NE * I], F32R)
        w2, b2 = sb("w2", [128, NE // 2, 32]), sb("b2", [128, 2])
        wo, bo = sb("wo", [128, EMB]), sb("bo", [128, EMB])
        spread = sb("spread", [128, 16, 128], F32R)
        gather = sb("gather", [128, 2, 32])
        rank = sb("rank", [128, NE])
        stats, mv = sb("stats", [128, 2, GF, 6]), sb("mv", [128, 2, GF, 2])
        logvar, rstd = sb("logvar", [128, 2, GF]), sb("rstd", [128, 2, GF])
        xn, lnT = sb("xn", [128, GF, EMB]), sb("lnT", [128, TOK])
        hT, h_parts = sb("hT", [128, TOK]), sb("h_parts", [128, 2, TOK], F32R)
        h_stack = [sb(f"h_stack{r}", [96, NH, TOK], F32R) for r in range(2)]
        top = sb("top", [128, 6, GF * NH])
        shifted, expd = sb("shifted", [128, TOK]), sb("expd", [128, TOK])
        first, second, keyed = sb("first", [128, TOK]), sb("second", [128, TOK]), sb("keyed", [128, TOK])
        chosen = sb("chosen", [128, TOK])
        wT = sb("wT", [128, 2, 2, TOK], F32R)
        act_out = sb("act_out", [128, 8, TOK])
        spread_sb = sb("spread_sb", [128, 2, TOK])
        prod = sb("prod", [128, 2, TOK])
        combT = sb("combT", [128, TOK])
        banks = [ctx.enter_context(nc.psum_tensor(f"f0_bank{n}", [128, 512], F32)) for n in range(8)]
        hid_ps, exp_ps, spread_ps, comb_ps, misc = banks[0:3], banks[3:5], banks[5], banks[6], banks[7]

        stack_free = sem("stack_free")
        stats_seen, loaded, zeroed, w1_split, prepared = sem("stats_seen"), sem("loaded"), sem("zeroed"), sem("w1_split"), sem("prepared")
        stats_done, mv_done, logvar_done, rstd_done, xn_done, x_biased = (sem(n) for n in (
            "stats_done", "mv_done", "logvar_done", "rstd_done", "xn_done", "x_biased"))
        xnT_mm, lnT_ready, h_mm, hT_ready, hhi_ready, hlo_ready = (sem(n) for n in (
            "xnT_mm", "lnT_ready", "h_mm", "hT_ready", "hhi_ready", "hlo_ready"))
        stacked = [sem(f"stacked{r}") for r in range(2)]
        logits_mm, shifted_ready, expd_ready, route_seq, first_ready, sum_ready = (sem(n) for n in (
            "logits_mm", "shifted_ready", "expd_ready", "route_seq", "first_ready", "sum_ready"))
        second_ready, pool_seq, wT_mm, whi_ready, wT_ready = (sem(n) for n in (
            "second_ready", "pool_seq", "wT_mm", "whi_ready", "wT_ready"))
        hid_mm, act_ready, exp_mm, spread_mm, spread_ready, prod_ready, comb_mm, comb_ready, y_mm, y_added = (sem(n) for n in (
            "hid_mm", "act_ready", "exp_mm", "spread_mm", "spread_ready", "prod_ready", "comb_mm", "comb_ready", "y_mm", "y_added"))
        sums_done = sem("sums_done")
        N_LOADS = 18

        def hid_bank(s, n):
            return hid_ps[(n + s.ring) % 3]

        def act_out_of(s, n):
            return act_out[:, n % 8, :]

        def grp(ap):
            return ap.rearrange("p (q e) -> p q e", e=NE)

        def per_head(n):
            return top[:, n, :].unsqueeze(2).broadcast_to([128, GF * NH, NE])

        def blk(s, k):
            return (s, k) if k >= 0 else (s.back(1), k + 16)

        with nc.Block() as block:
            @block.sync
            def _(sp):
                for dst, name in ((wm, "wm"), (bm, "bm"), (emb, "emb"), (w2, "w2"), (b2, "b2"), (wo, "wo"), (gather, "gather")):
                    sp.dma_start(dst[:], ins[f"f0_{name}"]).then_inc(loaded, 16)
                sp.dma_start(bo[:], ins["f0_bo"].broadcast_to([128, EMB])).then_inc(loaded, 16)
                sp.dma_start(rank[:], ins["f0_rank"].broadcast_to([128, NE])).then_inc(loaded, 16)
                sp.wait_ge(zeroed, 3)
                for rep in range(3):
                    sp.dma_start(w1_raw[32 * rep:32 * rep + D, :], ins["f0_w1"]).then_inc(loaded, 16)
                for row in (D, 64 + D):
                    sp.dma_start(w1_raw[row:row + 1, :], ins["f0_b1"]).then_inc(loaded, 16)
                    for r in range(2):
                        sp.dma_start(raw_words(h_stack[r][row:row + 1, :, :]), const["ones"][0:NH * TOK // 128, :]).then_inc(loaded, 16)

                def step(t):
                    if live(t):
                        need(sp, hid_mm, t.back(1).count(64, 0))
                        sp.sem_inc(stack_free, 1)
                        sp.wait_ge(hlo_ready, t.count(1, 1))
                        for rep, part in enumerate((0, 1, 0)):
                            sp.dma_start(raw_words(h_stack[t.ring][32 * rep:32 * rep + D, :, :]), raw_words(h_parts[:, part, :])) \
                                .then_inc(stacked[t.ring], 16)

                ph.run_steps(sp, step)

            @block.gpsimd
            def _(pool):
                pool.memset(w1_raw[:], 0.0).then_inc(zeroed, 1)
                for r in range(2):
                    pool.memset(h_stack[r][:].bitcast(F32), 0.0).then_inc(zeroed, 1)
                pool.wait_ge(loaded, 16 * N_LOADS)
                pool.sem_inc(prepared, 1)

                def step(t):
                    if not live(t):
                        return
                    pool.wait_ge(hhi_ready, t.count(1, 1))
                    pool.wait_ge(hT_ready, t.count(1, 1))
                    need(pool, stacked[t.back(1).ring], (t.back(1).half(48, 1)) if not t.static or t.off > 0 else 0)
                    pool.tensor_tensor(h_parts[:, 1, :], hT[:], h_parts[:, 0, :], ALU.subtract).then_inc(hlo_ready, 1)
                    pool.wait_ge(route_seq, t.count(8, 7))
                    pool.tensor_tensor(grp(keyed[:]), grp(second[:]), rank[:].unsqueeze(1).broadcast_to([128, GF * NH, NE]), ALU.mult).then_inc(pool_seq, 1)
                    pool.wait_ge(second_ready, t.count(1, 1))
                    need(pool, wT_mm, t.count(1, 0))
                    pool.tensor_tensor(chosen[:], first[:], second[:], ALU.add).then_inc(pool_seq, 1)
                    pool.wait_ge(pool_seq, t.count(4, 2))
                    pool.wait_ge(expd_ready, t.count(1, 1))
                    pool.tensor_tensor(chosen[:], chosen[:], expd[:], ALU.mult).then_inc(pool_seq, 1)
                    pool.wait_ge(pool_seq, t.count(4, 3))
                    pool.wait_ge(sum_ready, t.count(1, 1))
                    pool.tensor_tensor(grp(chosen[:]), grp(chosen[:]), per_head(2), ALU.mult).then_inc(pool_seq, 1)
                    pool.wait_ge(xn_done, t.count(1, 1))
                    pool.tensor_tensor(x_sb[:, t.ds(GF), :], x_sb[:, t.ds(GF), :],
                                       bo[:].unsqueeze(1).broadcast_to([128, GF, EMB]), ALU.add).then_inc(x_biased, 1)

                ph.run_steps(pool, step)

            @block.scalar
            def _(act):
                def rstd_of(s):
                    act.wait_ge(mv_done, s.count(1, 1))
                    act.activation(logvar[:, s.ring, :], mv[:, s.ring, :, 1], ACT.Ln, bias=const["eps_ln"][:]).then_inc(logvar_done, 1)
                    act.wait_ge(logvar_done, s.count(1, 1))
                    act.activation(rstd[:, s.ring, :], logvar[:, s.ring, :], ACT.Exp, scale=-0.5).then_inc(rstd_done, 1)

                act.preload_act_table_set("natural_log_exp_and_others")
                rstd_of(Step(0, 0))
                act.wait_ge(prepared, 1)

                def step(t):
                    M = t.back(1)
                    for k in range(16):
                        if live(t) and k == 2:
                            act.wait_ge(xnT_mm, t.count(1, 1))
                            act.activation(lnT[:], misc[:], ACT.Copy).then_inc(lnT_ready, 1)
                        if live(t) and k == 4:
                            act.wait_ge(h_mm, t.count(1, 1))
                            need(act, stacked[t.back(1).ring], (t.back(1).half(48, 1)) if not t.static or t.off > 0 else 0)
                            act.activation(h_parts[:, 0, :], misc[:], ACT.Identity, bias=bm[:]).then_inc(hhi_ready, 1)
                            act.activation(hT[:], misc[:], ACT.Identity, bias=bm[:]).then_inc(hT_ready, 1)
                        if k == 7 and (live(t) or live(t.back(-1))):
                            act.preload_act_table_set("natural_log_exp_and_others")
                            if live(t):
                                act.wait_ge(shifted_ready, t.count(1, 1))
                                act.activation(expd[:], shifted[:], ACT.Exp).then_inc(expd_ready, 1)
                            if live(t.back(-1)):
                                rstd_of(t.back(-1))
                            act.preload_act_table(ACT.Gelu)
                        if live(M):
                            for p in range(4):
                                n = 4 * k + p
                                act.wait_ge(hid_mm, M.count(64, n + 1))
                                if p == 0:
                                    need(act, exp_mm, M.count(64, n - 4))
                                act.activation(act_out_of(M, n), hid_bank(M, n)[:], ACT.Gelu).then_inc(act_ready, 1)
                        if live(t) and k == 15:
                            act.wait_ge(wT_mm, t.count(1, 1))
                            act.activation(wT[:, t.ring, 0, :], misc[:], ACT.Copy).then_inc(whi_ready, 1)

                ph.run_steps(act, step)

            @block.vector
            def _(dve):
                def row_block(s, b):
                    return x_sb[:, s.ds1(GF, b), :].rearrange("p a e -> p (a e)")

                def stats_of(s):
                    for b in range(GF):
                        dve.bn_stats(stats[:, s.ring, b, :], row_block(s, b)).then_inc(stats_done, 1)
                    dve.wait_ge(stats_done, s.count(GF, GF))
                    dve.sem_inc(stats_seen, 1)
                    for b in range(GF):
                        last = dve.bn_aggr(mv[:, s.ring, b, :], stats[:, s.ring, b, :])
                    last.then_inc(mv_done, 1)

                def normalise(s):
                    dve.wait_ge(rstd_done, s.count(1, 1))
                    dve.wait_ge(mv_done, s.count(1, 1))
                    need(dve, xnT_mm, s.count(1, 0))
                    for b in range(GF):
                        last = dve.tensor_scalar(xn[:, b, :], row_block(s, b), mv[:, s.ring, b, 0:1], rstd[:, s.ring, b:b + 1], ALU.subtract, ALU.mult)
                    last.then_inc(xn_done, 1)

                stats_of(Step(0, 0))
                normalise(Step(0, 0))
                dve.wait_ge(prepared, 1)
                dve.tensor_copy(spread[:].rearrange("p a (e o) -> p (a e) o", o=16), const["ident"][:].unsqueeze(2).broadcast_to([128, 128, 16]))
                dve.tensor_copy(w1_hi[:], w1_raw[:]).then_inc(w1_split, 1)
                dve.wait_ge(w1_split, 1)
                dve.tensor_copy(w1[0:64, :], w1_hi[0:64, :])
                dve.tensor_tensor(w1[64:96, :], w1_raw[64:96, :], w1_hi[64:96, :], ALU.subtract).then_inc(prepared, 1)

                SEQ_N = 8

                def link(ins_, s, n):
                    ins_.then_inc(route_seq, 1)
                    dve.wait_ge(route_seq, s.count(SEQ_N, n))

                def weigh(s, k):
                    dve.wait_ge(exp_mm, s.count(64, 4 * k + 4))
                    dve.wait_ge(spread_ready, s.count(16, k + 1))
                    need(dve, comb_mm, s.count(16, k - 1))
                    dve.scalar_tensor_tensor(out=prod[:, k % 2, :], in0=exp_ps[k % 2][:], scalar=b2[:, k % 2:k % 2 + 1], in1=spread_sb[:, k % 2, :],
                                             op0=ALU.add, op1=ALU.mult).then_inc(prod_ready, 1)

                def route(t, k):
                    ranks = rank[:].unsqueeze(1).broadcast_to([128, GF * NH, NE])
                    if k == 6:
                        dve.wait_ge(logits_mm, t.count(1, 1))
                        need(dve, pool_seq, t.count(4, 0))
                        link(dve.tensor_reduce(out=top[:, 0, :], in_=grp(misc[:]), axis=AX.X, op=ALU.max), t, 1)
                        dve.tensor_tensor(grp(shifted[:]), grp(misc[:]), per_head(0), ALU.subtract).then_inc(shifted_ready, 1)
                    if k == 7:
                        dve.wait_ge(shifted_ready, t.count(1, 1))
                        link(dve.scalar_tensor_tensor(out=grp(keyed[:]), in0=grp(shifted[:]), scalar=0.0, in1=ranks, op0=ALU.is_equal, op1=ALU.mult), t, 2)
                        link(dve.tensor_reduce(out=top[:, 3, :], in_=grp(keyed[:]), axis=AX.X, op=ALU.max), t, 3)
                    if k == 8:
                        link(dve.tensor_tensor(grp(first[:]), grp(keyed[:]), per_head(3), ALU.is_equal), t, 4)
                    if k == 9:
                        dve.wait_ge(expd_ready, t.count(1, 1))
                        link(dve.scalar_tensor_tensor(out=shifted[:], in0=first[:], scalar=-3.0e38, in1=shifted[:], op0=ALU.mult, op1=ALU.add), t, 5)
                        link(dve.tensor_reduce(out=top[:, 4, :], in_=grp(shifted[:]), axis=AX.X, op=ALU.max), t, 6)
                    if k == 12:
                        dve.wait_ge(pool_seq, t.count(4, 1))
                        link(dve.tensor_reduce(out=top[:, 5, :], in_=grp(keyed[:]), axis=AX.X, op=ALU.max), t, 8)
                        dve.tensor_tensor(grp(second[:]), grp(keyed[:]), per_head(5), ALU.is_equal).then_inc(second_ready, 1)
                    if k == 10:
                        link(dve.tensor_tensor(grp(second[:]), grp(shifted[:]), per_head(4), ALU.is_equal), t, 7)
                    if k == 11:
                        dve.tensor_reduce(out=top[:, 1, :], in_=grp(expd[:]), axis=AX.X, op=ALU.add).then_inc(sums_done, 1)
                        dve.wait_ge(sums_done, t.count(1, 1))
                        dve.reciprocal(top[:, 2, :], top[:, 1, :]).then_inc(sum_ready, 1)

                def step(t):
                    M, O = t.back(1), t.back(2)
                    for k in range(16):
                        if live(M):
                            dve.wait_ge(spread_mm, M.count(16, k + 1))
                            need(dve, prod_ready, M.count(16, k - 1))
                            dve.tensor_copy(spread_sb[:, k % 2, :], spread_ps[:]).then_inc(spread_ready, 1)
                        s, kb = blk(M, k - 1)
                        if live(s):
                            weigh(s, kb)
                        if k == 1 and live(O):
                            dve.wait_ge(comb_mm, O.count(16, 16))
                            need(dve, y_mm, O.count(1, 0))
                            dve.tensor_copy(combT[:], comb_ps[:]).then_inc(comb_ready, 1)
                        if k == 0 and live(t.back(-1)):
                            stats_of(t.back(-1))
                        if live(t) and 6 <= k <= 12:
                            route(t, k)
                        if k == 8 and live(O):
                            dve.wait_ge(y_mm, O.count(1, 1))
                            dve.wait_ge(x_biased, O.count(1, 1))
                            xs = x_sb[:, O.ds(GF), :].rearrange("p b e -> p (b e)")
                            dve.tensor_tensor(xs, misc[:], xs, ALU.add).then_inc(y_added, 1)
                        if k == 13 and live(t.back(-1)):
                            normalise(t.back(-1))
                        if k == 15 and live(t):
                            dve.wait_ge(whi_ready, t.count(1, 1))
                            dve.tensor_tensor(wT[:, t.ring, 1, :], misc[:], wT[:, t.ring, 0, :], ALU.subtract).then_inc(wT_ready, 1)

                ph.run_steps(dve, step)

            @block.tensor
            def _(pe):
                pe.wait_ge(prepared, 2)

                def first_layer(s, n):
                    need(pe, act_ready, s.count(64, (-1, 0, 0)[n] if n < 3 and s.ring == 0 else n - 2))
                    pe.matmul(hid_bank(s, n)[:], w1[:, 128 * (n % 8):128 * (n % 8) + 128], h_stack[s.ring][:, n // 8, :],
                              start=True, stop=True).then_inc(hid_mm, 1)

                def second_layer(s, k):
                    pe.wait_ge(act_ready, s.count(64, 4 * k + 4))
                    need(pe, prod_ready, s.count(16, k - 1))
                    busy = max(k - 1, 0) // 4
                    for q in ((busy + 1 + i) % 4 for i in range(4)):
                        n = 4 * k + q
                        pe.matmul(exp_ps[k % 2][32 * q:32 * q + 32, :], w2[:, n % 8, :], act_out_of(s, n), start=True, stop=True,
                                  tile_position=(0, 32 * q)).then_inc(exp_mm, 1)

                def combine(s, k):
                    j = k // 2
                    pe.wait_ge(prod_ready, s.count(16, k + 1))
                    if k == 0:
                        need(pe, comb_ready, s.count(1, 0))
                    q = j // 2
                    pe.matmul(comb_ps[32 * q:32 * q + 32, :], gather[:, j % 2, :], prod[:, k % 2, :], start=(k % 4 == 0), stop=(k % 4 == 3),
                              tile_position=(0, 32 * q)).then_inc(comb_mm, 1)

                def step(t):
                    M, O = t.back(1), t.back(2)
                    for k in range(16):
                        if k == 1 and live(t):
                            pe.wait_ge(xn_done, t.count(1, 1))
                            need(pe, wT_ready, t.count(1, 0))
                            for b in range(GF):
                                last = pe.transpose(misc[:, b * SEQ:(b + 1) * SEQ], xn[:, b, :], const["ident"][:])
                            last.then_inc(xnT_mm, 1)
                        if k == 3 and live(t):
                            pe.wait_ge(lnT_ready, t.count(1, 1))
                            pe.matmul(misc[:], wm[:], lnT[:], start=True, stop=True).then_inc(h_mm, 1)
                        if k == 5 and live(t):
                            pe.wait_ge(hT_ready, t.count(1, 1))
                            for b in range(GF):
                                last = pe.matmul(misc[:, b * SEQ:(b + 1) * SEQ], hT[:, b * SEQ:(b + 1) * SEQ], emb[:], start=True, stop=True)
                            last.then_inc(logits_mm, 1)
                        if k == 7 and live(O):
                            pe.wait_ge(comb_ready, O.count(1, 1))
                            if live(t):
                                pe.wait_ge(shifted_ready, t.count(1, 1))
                            elif t.static:
                                need(pe, wT_ready, ph.steps_n)
                            need(pe, y_added, O.count(1, 0))
                            for b in range(GF):
                                last = pe.matmul(misc[:, b * EMB:(b + 1) * EMB], combT[:, b * SEQ:(b + 1) * SEQ], wo[:], start=True, stop=True)
                            last.then_inc(y_mm, 1)
                        if live(M):
                            if k == 0:
                                pe.wait_ge(stacked[M.ring], M.half(48, 1))
                            first_layer(M, 4 * k)
                            first_layer(M, 4 * k + 1)
                            need(pe, spread_ready, M.count(16, k))
                            if k == 0:
                                pe.wait_ge(wT_ready, M.count(1, 1))
                            for part in range(2):
                                last = pe.matmul(spread_ps[:], spread[:, k, :], wT[:, M.ring, part, :], start=(part == 0), stop=(part == 1))
                            last.then_inc(spread_mm, 1)
                            first_layer(M, 4 * k + 2)
                        s, kb = blk(M, k - 2)
                        if live(s):
                            combine(s, kb)
                        s, kb = blk(M, k - 1)
                        if live(s):
                            second_layer(s, kb)
                        if live(M):
                            first_layer(M, 4 * k + 3)
                        if k == 14 and live(t):
                            pe.wait_ge(pool_seq, t.count(4, 4))
                            pe.wait_ge(shifted_ready, t.count(1, 1))
                            if live(O):
                                need(pe, y_added, O.count(1, 1))
                            for b in range(GF):
                                last = pe.transpose(misc[:, b * SEQ:(b + 1) * SEQ], chosen[:, b * SEQ:(b + 1) * SEQ], const["ident"][:])
                            last.then_inc(wT_mm, 1)


                ph.run_steps(pe, step)


def mixture_phase(nc, x_sb, const, ins):
    NE, HID = 8, 256
    with ExitStack() as ctx:
        ph = ExpertPhase(nc, ctx, "f1")
        sb, sem, live = ph.sb, ph.sem, ph.live
        w_raw, w_hi, w_lo = sb("w_raw", [128, NE * 2 * HID]), sb("w_hi", [128, NE * 2 * HID], F32R), sb("w_lo", [128, NE * 2 * HID], F32R)
        wd, wr, norm_scale = sb("wd", [128, NE, 2, EMB]), sb("wr", [128, NE]), sb("norm_scale", [128, 1])
        rank = sb("rank", [128, NE])
        eps_both = sb("eps_both", [128, 1])
        stats, mv = sb("stats", [128, 2, GF, 6]), sb("mv", [128, 2, GF, 2])
        logvar, rstd = sb("logvar", [128, 2, 2, GF]), sb("rstd", [128, 2, 2, GF])
        xn, xr = sb("xn", [128, GF, EMB]), sb("xr", [128, GF, EMB])
        xT, x_hi, x_lo = sb("xT", [128, TOK]), sb("x_hi", [128, 2, TOK], F32R), sb("x_lo", [128, 2, TOK], F32R)
        shifted, keyed = (sb(n, [128, GF * NE]) for n in ("shifted", "keyed"))
        first, second, chosen = (sb(n, [128, GF * NE]) for n in ("first", "second", "chosen"))
        weights = sb("weights", [128, 2, GF * NE])
        top = sb("top", [128, 7, GF])
        silu, h = sb("silu", [128, 2, TOK]), sb("h", [128, 4, TOK])
        banks = [ctx.enter_context(nc.psum_tensor(f"f1_bank{n}", [128, 512], F32)) for n in range(7)]
        gate_ps, u_ps, y_ps, misc = banks[0:2], banks[2:4], banks[4:6], banks[6]

        eps_made = sem("eps_made")
        stats_seen, loaded, prepared, w_split, rest_seq = sem("stats_seen"), sem("loaded"), sem("prepared"), sem("w_split"), sem("rest_seq")
        stats_done, mv_done, logvar_done, rstd_done, xn_done, xr_done, skip_added = (sem(n) for n in (
            "stats_done", "mv_done", "logvar_done", "rstd_done", "xn_done", "xr_done", "skip_added"))
        xr_transposed, xT_ready, xhi_ready, xlo_ready, logits_mm, route_seq, second_exp, weights_ready = (sem(n) for n in (
            "xr_transposed", "xT_ready", "xhi_ready", "xlo_ready", "logits_mm", "route_seq", "second_exp", "weights_ready"))
        gate_mm, u_mm, silu_ready, h_ready, down_mm, y_added = (sem(n) for n in (
            "gate_mm", "u_mm", "silu_ready", "h_ready", "down_mm", "y_added"))

        def grp(ap):
            return ap.rearrange("p (b e) -> p b e", e=NE)

        def per_token(n):
            return top[:, n, :].unsqueeze(2).broadcast_to([128, GF, NE])

        with nc.Block() as block:
            @block.sync
            def _(sp):
                for dst, name in ((w_raw, "w_up"), (wd, "wd"), (wr, "wr"), (norm_scale, "norm_scale")):
                    sp.dma_start(dst[:], ins[f"f1_{name}"]).then_inc(loaded, 16)
                sp.dma_start(rank[:], ins["f1_rank"].broadcast_to([128, NE])).then_inc(loaded, 16)

            @block.gpsimd
            def _(pool):
                pool.memset(eps_both[:], 1e-5 * 1e-6).then_inc(eps_made, 1)
                pool.wait_ge(loaded, 16 * 5)
                pool.sem_inc(prepared, 1)

                def step(t):
                    if live(t):
                        pool.wait_ge(xn_done, t.count(1, 1))
                        pool.wait_ge(xr_done, t.count(1, 1))
                        pool.tensor_tensor(x_sb[:, t.ds(GF), :], x_sb[:, t.ds(GF), :], xn[:], ALU.add).then_inc(skip_added, 1)

                ph.run_steps(pool, step)

            @block.scalar
            def _(act):
                act.wait_ge(eps_made, 1)

                def rstd_of(s):
                    act.wait_ge(mv_done, s.count(1, 1))
                    act.activation(logvar[:, s.ring, 0, :], mv[:, s.ring, :, 1], ACT.Ln, bias=const["eps_ln"][:])
                    act.activation(logvar[:, s.ring, 1, :], mv[:, s.ring, :, 1], ACT.Ln, bias=eps_both[:], scale=1.0 + 1e-6).then_inc(logvar_done, 1)
                    act.wait_ge(logvar_done, s.count(1, 1))
                    act.activation(rstd[:, s.ring, :, :], logvar[:, s.ring, :, :], ACT.Exp, scale=-0.5).then_inc(rstd_done, 1)

                act.preload_act_table_set("natural_log_exp_and_others")
                rstd_of(Step(0, 0))
                act.wait_ge(prepared, 1)

                def step(t):
                    M = t.back(1)
                    for k in range(NE):
                        if k == 1 and live(t):
                            act.wait_ge(xr_transposed, t.count(1, 1))
                            need(act, logits_mm, t.count(1, 0))
                            act.activation(x_hi[:, t.ring, :], misc[:], ACT.Identity, scale=norm_scale[:]).then_inc(xhi_ready, 1)
                            act.activation(xT[:], misc[:], ACT.Identity, scale=norm_scale[:]).then_inc(xT_ready, 1)
                        if k == 5 and (live(t) or live(t.back(-1))):
                            act.preload_act_table_set("natural_log_exp_and_others")
                            if live(t):
                                act.wait_ge(route_seq, t.count(8, 6))
                                act.activation(top[:, 4, :], top[:, 2, :], ACT.Exp).then_inc(second_exp, 1)
                            if live(t.back(-1)):
                                rstd_of(t.back(-1))
                            act.preload_act_table(ACT.Silu)
                        if live(M):
                            for n in (2 * k, 2 * k + 1):
                                act.wait_ge(gate_mm, M.count(16, n + 1))
                                need(act, h_ready, M.count(16, n - 1))
                                act.activation(silu[:, n % 2, :], gate_ps[n % 2][:], ACT.Silu).then_inc(silu_ready, 1)

                ph.run_steps(act, step)

            @block.vector
            def _(dve):
                def row_block(s, b):
                    return x_sb[:, s.ds1(GF, b), :].rearrange("p a e -> p (a e)")

                def stats_of(s):
                    for b in range(GF):
                        dve.bn_stats(stats[:, s.ring, b, :], row_block(s, b)).then_inc(stats_done, 1)
                    dve.wait_ge(stats_done, s.count(GF, GF))
                    dve.sem_inc(stats_seen, 1)
                    for b in range(GF):
                        last = dve.bn_aggr(mv[:, s.ring, b, :], stats[:, s.ring, b, :])
                    last.then_inc(mv_done, 1)

                def normalise(s):
                    dve.wait_ge(rstd_done, s.count(1, 1))
                    dve.wait_ge(mv_done, s.count(1, 1))
                    need(dve, skip_added, s.count(1, 0))
                    need(dve, xr_transposed, s.count(1, 0))
                    for dst, which, done in ((xr, 1, xr_done), (xn, 0, xn_done)):
                        for b in range(GF):
                            last = dve.tensor_scalar(dst[:, b, :], row_block(s, b), mv[:, s.ring, b, 0:1], rstd[:, s.ring, which, b:b + 1],
                                                     ALU.subtract, ALU.mult)
                        last.then_inc(done, 1)

                def link(op, s, n):
                    op.then_inc(route_seq, 1)
                    dve.wait_ge(route_seq, s.count(8, n))

                def choose_first(t):
                    dve.wait_ge(logits_mm, t.count(1, 1))
                    link(dve.tensor_reduce(out=top[:, 0, :], in_=grp(misc[:, :GF * NE]), axis=AX.X, op=ALU.max), t, 1)
                    link(dve.tensor_tensor(grp(shifted[:]), grp(misc[:, :GF * NE]), per_token(0), ALU.subtract), t, 2)
                    link(dve.scalar_tensor_tensor(out=grp(keyed[:]), in0=grp(shifted[:]), scalar=0.0,
                                                  in1=rank[:].unsqueeze(1).broadcast_to([128, GF, NE]), op0=ALU.is_equal, op1=ALU.mult), t, 3)
                    link(dve.tensor_reduce(out=top[:, 1, :], in_=grp(keyed[:]), axis=AX.X, op=ALU.max), t, 4)
                    link(dve.tensor_tensor(grp(first[:]), grp(keyed[:]), per_token(1), ALU.is_equal), t, 5)

                def choose_second(t):
                    dve.scalar_tensor_tensor(out=shifted[:], in0=first[:], scalar=-3.0e38, in1=shifted[:], op0=ALU.mult, op1=ALU.add).then_inc(rest_seq, 1)
                    dve.wait_ge(rest_seq, t.count(3, 1))
                    link(dve.tensor_reduce(out=top[:, 2, :], in_=grp(shifted[:]), axis=AX.X, op=ALU.max), t, 6)
                    dve.tensor_tensor(grp(second[:]), grp(shifted[:]), per_token(2), ALU.is_equal).then_inc(rest_seq, 1)
                    dve.wait_ge(rest_seq, t.count(3, 2))
                    dve.tensor_tensor(grp(keyed[:]), grp(second[:]), rank[:].unsqueeze(1).broadcast_to([128, GF, NE]), ALU.mult).then_inc(rest_seq, 1)
                    dve.wait_ge(rest_seq, t.count(3, 3))
                    link(dve.tensor_reduce(out=top[:, 3, :], in_=grp(keyed[:]), axis=AX.X, op=ALU.max), t, 7)
                    link(dve.tensor_tensor(grp(second[:]), grp(keyed[:]), per_token(3), ALU.is_equal), t, 8)

                def weigh_chosen(t):
                    dve.wait_ge(second_exp, t.count(1, 1))
                    dve.tensor_scalar(top[:, 5, :], top[:, 4, :], 1.0, None, ALU.add)
                    dve.tensor_tensor(grp(chosen[:]), grp(second[:]), per_token(4), ALU.mult).then_inc(weights_ready, 1)
                    dve.wait_ge(weights_ready, t.count(3, 1))
                    dve.reciprocal(top[:, 6, :], top[:, 5, :])
                    dve.tensor_tensor(chosen[:], chosen[:], first[:], ALU.add).then_inc(weights_ready, 1)
                    dve.wait_ge(weights_ready, t.count(3, 2))
                    dve.tensor_tensor(grp(weights[:, t.ring, :]), grp(chosen[:]), per_token(6), ALU.mult).then_inc(weights_ready, 1)

                stats_of(Step(0, 0))
                normalise(Step(0, 0))
                dve.wait_ge(prepared, 1)
                dve.tensor_copy(w_hi[:], w_raw[:]).then_inc(w_split, 1)
                dve.wait_ge(w_split, 1)
                dve.tensor_tensor(w_lo[:], w_raw[:], w_hi[:], ALU.subtract).then_inc(prepared, 1)

                def mix(s, e):
                    dve.wait_ge(down_mm, s.count(NE, e + 1))
                    if e == 0:
                        dve.wait_ge(weights_ready, s.count(3, 3))
                        dve.wait_ge(skip_added, s.count(1, 1))
                    else:
                        dve.wait_ge(y_added, s.count(NE, e))
                    for b in range(GF):
                        last = dve.scalar_tensor_tensor(out=row_block(s, b), in0=y_ps[e % 2][:, b * EMB:(b + 1) * EMB],
                                                        scalar=weights[:, s.ring, b * NE + e:b * NE + e + 1], in1=row_block(s, b),
                                                        op0=ALU.mult, op1=ALU.add)
                    last.then_inc(y_added, 1)

                def step(t):
                    M = t.back(1)
                    for k in range(NE):
                        for n in (2 * k, 2 * k + 1):
                            if live(M):
                                dve.wait_ge(silu_ready, M.count(16, n + 1))
                                dve.wait_ge(u_mm, M.count(16, n + 1))
                                need(dve, down_mm, M.count(NE, k - 1))
                                dve.tensor_tensor(h[:, n % 4, :], u_ps[n % 2][:], silu[:, n % 2, :], ALU.mult).then_inc(h_ready, 1)
                        if k == 1 and live(t):
                            dve.wait_ge(xT_ready, t.count(1, 1))
                            dve.wait_ge(xhi_ready, t.count(1, 1))
                            dve.tensor_tensor(x_lo[:, t.ring, :], xT[:], x_hi[:, t.ring, :], ALU.subtract).then_inc(xlo_ready, 1)
                        if k == 3 and live(t):
                            choose_first(t)
                        if k == 4 and live(t):
                            choose_second(t)
                        if k == 4 and live(t.back(-1)):
                            stats_of(t.back(-1))
                        if k == 6 and live(t):
                            weigh_chosen(t)
                        if k == 6 and live(t.back(-1)):
                            normalise(t.back(-1))
                        s, e = (M, k - 1) if k > 0 else (M.back(1), NE - 1)
                        if live(s):
                            mix(s, e)

                ph.run_steps(dve, step)

            @block.tensor
            def _(pe):
                pe.wait_ge(prepared, 2)

                def up(ps, s, col):
                    x_h, x_l = x_hi[:, s.ring, :], x_lo[:, s.ring, :]
                    pe.matmul(ps[:], w_hi[:, col:col + 128], x_h, start=True, stop=False)
                    pe.matmul(ps[:], w_hi[:, col:col + 128], x_l, start=False, stop=False)
                    return pe.matmul(ps[:], w_lo[:, col:col + 128], x_h, start=False, stop=True)

                def down(s, e):
                    pe.wait_ge(h_ready, s.count(16, 2 * e + 2))
                    need(pe, y_added, s.count(NE, e - 1))
                    for b in range(GF):
                        for c in range(2):
                            last = pe.matmul(y_ps[e % 2][:, b * EMB:(b + 1) * EMB], h[:, 2 * (e % 2) + c, b * SEQ:(b + 1) * SEQ], wd[:, e, c, :],
                                             start=(c == 0), stop=(c == 1))
                    last.then_inc(down_mm, 1)

                def step(t):
                    M = t.back(1)
                    for k in range(NE):
                        if k == 0 and live(t):
                            pe.wait_ge(xr_done, t.count(1, 1))
                            need(pe, route_seq, t.count(8, 0))
                            for b in range(GF):
                                last = pe.transpose(misc[:, b * SEQ:(b + 1) * SEQ], xr[:, b, :], const["ident"][:])
                            last.then_inc(xr_transposed, 1)
                        if k == 2 and live(t):
                            pe.wait_ge(xT_ready, t.count(1, 1))
                            pe.wait_ge(xhi_ready, t.count(1, 1))
                            for b in range(GF):
                                last = pe.matmul(misc[:, b * NE:(b + 1) * NE], xT[:, b * SEQ:(b + 1) * SEQ], wr[:], start=True, stop=True)
                            last.then_inc(logits_mm, 1)
                        if live(M):
                            if k == 0:
                                pe.wait_ge(xlo_ready, M.count(1, 1))
                            for c in range(2):
                                n = 2 * k + c
                                need(pe, silu_ready, M.count(16, n - 1))
                                up(gate_ps[n % 2], M, 2 * HID * k + HID + 128 * c).then_inc(gate_mm, 1)
                                need(pe, h_ready, M.count(16, n - 1))
                                up(u_ps[n % 2], M, 2 * HID * k + 128 * c).then_inc(u_mm, 1)
                        s, e = (M, k - 1) if k > 0 else (M.back(1), NE - 1)
                        if live(s):
                            down(s, e)

                ph.run_steps(pe, step)


def expert_layouts(a, np):
    d = {}
    heads_last = lambda w: np.ascontiguousarray(w.reshape(*w.shape[:-1], 8, 16).swapaxes(-1, -2).reshape(w.shape))
    d["f0_wm"], d["f0_bm"] = heads_last(a["L0_ffn_Wm"]), heads_last(a["L0_ffn_bm"]).reshape(128, 1)
    emb = np.zeros((16, 8, 8, 16), np.float32)
    for h in range(8):
        emb[:, h, h] = a["L0_ffn_expert_emb"]
    d["f0_emb"] = emb.reshape(128, 128)
    d["f0_w1"] = np.ascontiguousarray(a["L0_ffn_W1"].transpose(1, 0, 2).reshape(16, 1024))
    d["f0_b1"] = a["L0_ffn_b1"].reshape(1, 1024)
    w2 = np.zeros((8, 2, 64, 2, 16), np.float32)
    for e in range(2):
        w2[:, e, :, e] = a["L0_ffn_W2"].reshape(8, 2, 64, 16)[:, e]
    d["f0_w2"] = np.ascontiguousarray(w2.reshape(8, 128, 32).transpose(1, 0, 2))
    d["f0_b2"] = np.ascontiguousarray(a["L0_ffn_b2"].reshape(2, 128).T)
    d["f0_wo"], d["f0_bo"] = a["L0_ffn_Wo"], a["L0_ffn_bo"].reshape(1, 128)
    d["f0_rank"] = (16 - np.arange(16, dtype=np.float32)).reshape(1, 16)
    gather = np.zeros((8, 16, 2, 32), np.float32)
    for parity in range(2):
        for o in range(16):
            gather[:, o, parity, 16 * parity + o] = 1.0
    d["f0_gather"] = gather.reshape(128, 2, 32)
    d["f1_w_up"] = np.ascontiguousarray(a["L1_ffn_w_up"].transpose(2, 0, 1).reshape(128, 8 * 512))
    d["f1_wd"] = np.ascontiguousarray(a["L1_ffn_w_down"].transpose(0, 2, 1).reshape(8, 2, 128, 128).transpose(2, 0, 1, 3))
    d["f1_wr"], d["f1_norm_scale"] = np.ascontiguousarray(a["L1_ffn_w_router"].T), a["L1_ffn_norm_scale"].reshape(128, 1)
    d["f1_rank"] = (8 - np.arange(8, dtype=np.float32)).reshape(1, 8)
    return d


def setup_constants(nc, ctx, ins):
    def sb(name, shape, dt=F32):
        return ctx.enter_context(nc.sbuf_tensor(name, shape, dt))

    x_sb = sb("x_sb", [128, BATCH, EMB])
    const = {name: sb(f"const_{name}", shape) for name, shape in (
        ("ident", [128, 128]), ("ones", [128, 128]), ("causal", [128, 128]), ("eps_ln", [128, 1]), ("eps_den", [128, 1]),
        ("zero", [128, 1]), ("abundance", [128, BATCH]))}
    made, loaded = ctx.enter_context(nc.semaphore("made")), ctx.enter_context(nc.semaphore("loaded"))
    with nc.Block() as block:
        @block.sync
        def _(sp):
            for part in range(4):
                n = BATCH // 4
                sp.dma_start(x_sb[:, part * n:(part + 1) * n, :], ins["x"][part * n:(part + 1) * n].rearrange("b s e -> s b e")).then_inc(loaded, 16)
            sp.dma_start(const["abundance"][:CTX, :], ins["abundance"]).then_inc(loaded, 16)

        @block.gpsimd
        def _(pool):
            pool.memset(const["ident"][:], 0.0).then_inc(made, 1)
            pool.memset(const["ones"][:], 1.0).then_inc(made, 1)
            pool.wait_ge(made, 2)
            pool.affine_select(out=const["ident"][:], in_=const["ident"][:], compare_op=ALU.not_equal, fill=1.0, base=0,
                               pattern=[[-1, 128]], channel_multiplier=1)
            pool.affine_select(out=const["causal"][:], in_=const["ones"][:], compare_op=ALU.is_ge, fill=0.0, base=0,
                               pattern=[[1, 128]], channel_multiplier=-1)

        @block.vector
        def _(dve):
            for name, value in (("eps_ln", 1e-5), ("eps_den", 1e-6), ("zero", 0.0)):
                dve.memset(const[name][:], value)
    return x_sb, const, loaded


def setup_stacks(nc, ctx, tag, loaded):
    def sb(name, shape):
        return ctx.enter_context(nc.sbuf_tensor(f"{tag}_{name}", shape, F32R))

    stacks = {
        "q_blocks": [sb(f"q_blocks{r}", [128, 4, 4 * G * SEQ]) for r in range(2)],
        "k_blocks": [sb(f"k_blocks{r}", [128, 4, 4 * G * SEQ]) for r in range(2)],
        "k_stack": [sb(f"k_stack{r}", [128, 4 * G * SEQ]) for r in range(2)],
        "q_hi": [sb(f"q_hi{r}", [128, 4 * G * SEQ]) for r in range(2)],
    }
    zeroed = Semaphores(nc, ctx, tag)("zeroed")
    with nc.Block() as block:
        @block.sync
        def _(sp):
            sp.wait_ge(loaded, 16 * 5)

        @block.gpsimd
        def _(pool):
            for r in range(2):
                pool.memset(stacks["k_stack"][r][:].bitcast(F32), 0.0).then_inc(zeroed, 1)
                pool.memset(stacks["q_hi"][r][:].bitcast(F32), 0.0).then_inc(zeroed, 1)
                pool.memset(stacks["k_blocks"][r][:].bitcast(F32), 0.0).then_inc(zeroed, 1)
            pool.wait_ge(zeroed, 6)
            for r in range(2):
                pool.memset(stacks["k_stack"][r][96:97, :].bitcast(F32), 1.0)

        @block.vector
        def _(dve):
            for r in range(2):
                dve.memset(stacks["q_blocks"][r][:].bitcast(F32), 0.0)
    return stacks


def decoder(nc, ins, out, phases=ALL_PHASES):
    with ExitStack() as ctx:
        x_sb, const, loaded = setup_constants(nc, ctx, ins)

        def attention_pair(tag, pair):
            with ExitStack() as pair_ctx:
                pair = [(kind, p) for kind, p in pair if p in phases]
                stacks = setup_stacks(nc, pair_ctx, tag, loaded) if pair or tag == "stacks0" else None
                for kind, p in pair:
                    names = [k for k in ("wq", "wk", "wv", "wo", "bo", "bq", "bk", "bv", "cos", "sin") if f"{p}_{k}" in ins]
                    attention_phase(nc, kind, p, x_sb, const, stacks, {**{k: ins[f"{p}_{k}"] for k in names}, "ctx": ins["ctx"]})

        attention_pair("stacks0", (("linear", "a0"), ("cross", "c0")))
        if "f0" in phases:
            experts_phase(nc, x_sb, const, ins)
        attention_pair("stacks1", (("scrambled", "a1"), ("weighted", "c1")))
        if "f1" in phases:
            mixture_phase(nc, x_sb, const, ins)
        stored = ctx.enter_context(nc.semaphore("stored"))
        with nc.Block() as block:
            @block.sync
            def _(sp):
                for part in range(4):
                    n = BATCH // 4
                    sp.dma_start(out[part * n:(part + 1) * n].rearrange("b s e -> s b e"), x_sb[:, part * n:(part + 1) * n, :]).then_inc(stored, 16)
                sp.wait_ge(stored, 64)


def layouts(a):
    import numpy as np

    def headed(w):
        return np.ascontiguousarray(w.reshape(*w.shape[:-1], 4, 4, 8).transpose(*range(w.ndim - 1), w.ndim, w.ndim + 1, w.ndim - 1).reshape(w.shape))

    def dims_first(w):
        return np.ascontiguousarray(w.reshape(*w.shape[:-1], 16, 8).swapaxes(-1, -2).reshape(w.shape))

    def masked_out(wT):
        out = np.zeros((128, 4, 128), np.float32)
        for h in range(16):
            out[8 * h:8 * h + 8, h % 4] = wT[8 * h:8 * h + 8]
        return out

    row = lambda v: np.ascontiguousarray(v.reshape(1, -1))
    col = lambda v: np.ascontiguousarray(v.reshape(-1, 1))
    t = lambda w: np.ascontiguousarray(w.T)
    d = {"x": a["x"], "ctx": a["ctx_1024"], "abundance": t(a["fside_BxS2_0"])}
    d["a0_wq"], d["a0_wk"] = headed(t(a["L0_attn_Wq"])), headed(t(a["L0_attn_Wk"]))
    d["a0_wv"], d["a0_wo"], d["a0_bo"] = t(a["L0_attn_Wv"]), masked_out(t(a["L0_attn_Wp"])), row(a["L0_attn_bp"])
    w, b, wo, bo = a["L1_xattn_in_proj_weight"], a["L1_xattn_in_proj_bias"], a["L1_xattn_out_proj_weight"], a["L1_xattn_out_proj_bias"]
    for tag, (wq, wk, wv, wo, bq, bk, bv, bo) in {
        "c0": [a[f"L0_xattn_{n}"] for n in ("Wq", "Wk", "Wv", "Wo", "bq", "bk", "bv", "bo")],
        "c1": [w[:128], w[128:256], w[256:], wo, b[:128], b[128:256], b[256:], bo],
    }.items():
        d[f"{tag}_wq"], d[f"{tag}_wk"], d[f"{tag}_wv"] = headed(t(wq)), headed(t(wk)), t(wv)
        d[f"{tag}_wo"], d[f"{tag}_bo"], d[f"{tag}_bv"] = masked_out(t(wo)), row(bo), row(bv)
        d[f"{tag}_bq"], d[f"{tag}_bk"] = col(headed(bq)), col(headed(bk))
    for n in ("wq", "wk", "wv"):
        d[f"a1_{n}"] = dims_first(t(a[f"L1_attn_{n}"]))
    d["a1_wo"], d["a1_bo"] = masked_out(t(a["L1_attn_wo"])), row(a["L1_attn_bo"])
    d["a1_bq"], d["a1_bk"], d["a1_bv"] = row(dims_first(a["L1_attn_bq"])), row(dims_first(a["L1_attn_bk"])), col(dims_first(a["L1_attn_bv"]))
    d["a1_cos"], d["a1_sin"] = row(a["L1_attn_rot_cos"][SEQ]), row(a["L1_attn_rot_sin"][SEQ])
    d.update(expert_layouts(a, np))
    return d


def kernel(**inputs):
    import concourse.bacc as _bacc
    import numpy as _np
    from concourse.bass_utils import run_bass_kernel_spmd as _run

    nc = _bacc.Bacc("TRN2", target_bir_lowering=False, num_devices=1)
    arrays = layouts({name: _np.asarray(value) for name, value in inputs.items()})
    arrays = {f"in_{name}": _np.ascontiguousarray(a) for name, a in arrays.items()}
    args = {name[3:]: nc.dram_tensor(name, a.shape, mybir.dt.from_np(a.dtype), kind="ExternalInput").ap() for name, a in arrays.items()}
    out = nc.dram_tensor("out", (BATCH, SEQ, EMB), F32, kind="ExternalOutput").ap()
    decoder(nc, args, out)
    return _run(nc, [arrays], core_ids=[0]).results[0]["out"]
```
